# Optimizing a Trainium2 kernel written in Bass

```python
import numpy as np
import jax
import jax.numpy as jnp

def _softmax(x, axis=-1):
    return jax.nn.softmax(x, axis=axis)

def _gelu(x):
    return jax.nn.gelu(x, approximate=True)

def _silu(x):
    return jax.nn.silu(x)

def _sigmoid(x):
    return jax.nn.sigmoid(x)

def _layernorm(x, axis=-1, eps=1e-05):
    m = jnp.mean(x, axis=axis, keepdims=True)
    v = jnp.var(x, axis=axis, keepdims=True)
    return (x - m) / jnp.sqrt(v + eps)

def _scatter_add(tgt, idx, src, axis=0):
    return tgt.at[idx].add(src)

def _segment_sum(src, seg, n):
    return jax.ops.segment_sum(src, seg, n)
kernel_name = 'mk_flamingo_gated_d1_seqx_r8_41ea64'

def setup_inputs(seed: int=0):
    np.random.seed(seed)
    _w = jnp.asarray

    def _rec_inputs():
        import jax
        import jax.numpy as jnp
        _rk = jax.random.key(seed)
        x = -0.0002928 + 1 * jax.random.normal(jax.random.fold_in(_rk, 1), (64, 64, 256), jnp.float32)
        _lenS = 64 - jax.random.randint(jax.random.fold_in(_rk, 7), (64,), 0, max(1, 64 // 4) + 1, jnp.int32)
        _lenS2 = 64 - jax.random.randint(jax.random.fold_in(_rk, 8), (64,), 0, max(1, 64 // 4) + 1, jnp.int32)
        _ctx_2048P = jax.random.normal(jax.random.fold_in(_rk, 11), (64, 16, 256), jnp.float32)
        _ctx_2048c = jax.random.dirichlet(jax.random.fold_in(_rk, 511), 0.3 * jnp.ones((16,), jnp.float32), (64, 64))
        _ctx_2048t = jnp.einsum('bsk,bkd->bsd', _ctx_2048c, _ctx_2048P)
        _ctx_2048t = _ctx_2048t * jax.lax.rsqrt(jnp.mean(jnp.square(_ctx_2048t)) + 1e-12) * 0.953939
        ctx_2048 = 4.13588e-05 + 0.999923 * (_ctx_2048t + 0.3 * jax.random.normal(jax.random.fold_in(_rk, 611), (64, 64, 256), jnp.float32))
        _validS = jnp.arange(64)[None, :] < _lenS[:, None]
        _validS2 = jnp.arange(64)[None, :] < _lenS2[:, None]
        _causal = jnp.tril(jnp.ones((64, 64), dtype=bool))
        mask_1xSxS2_ff0 = jnp.where(jnp.ones((1, 64, 64), dtype=bool), 0.0, -1000000000.0).astype(jnp.float32)
        _g = jax.random.normal(jax.random.fold_in(_rk, 9001), (2, 1), jnp.float32)
        _g = jnp.sign(_g) * jnp.maximum(jnp.abs(_g), 1.0) + (_g == 0) * 1.0
        g_xattn = _g[0]
        g_ffn = _g[1]
        return (x, ctx_2048, mask_1xSxS2_ff0, g_xattn, g_ffn)
    x, ctx_2048, mask_1xSxS2_ff0, g_xattn, g_ffn = _rec_inputs()

    def _L0_xattn_setup():
        import jax, jax.numpy as jnp
        import numpy as np
        H = 256
        NH = 16
        NKV = 4
        HD = 128
        GROUPS = NH // NKV
        EPS = 1e-06
        B, S, SE = (1, 256, 512)

        def _rmsnorm(x, w, eps=EPS):
            xf = x.astype(jnp.float32)
            var = jnp.mean(xf * xf, axis=-1, keepdims=True)
            return (xf * jax.lax.rsqrt(var + eps)).astype(x.dtype) * w
        key = jax.random.key(seed)
        ks = jax.random.split(key, 12)
        sc = 0.02
        return {'hidden_states': jax.random.normal(ks[0], (B, S, H), jnp.float32), 'encoder_hidden_states': jax.random.normal(ks[1], (B, SE, H), jnp.float32), 'attention_mask': jnp.zeros((B, S, SE), jnp.float32), 'Wq': jax.random.normal(ks[2], (H, NH * HD), jnp.float32) * sc, 'bq': jax.random.normal(ks[3], (NH * HD,), jnp.float32) * sc, 'Wk': jax.random.normal(ks[4], (H, NKV * HD), jnp.float32) * sc, 'bk': jax.random.normal(ks[5], (NKV * HD,), jnp.float32) * sc, 'Wv': jax.random.normal(ks[6], (H, NKV * HD), jnp.float32) * sc, 'bv': jax.random.normal(ks[7], (NKV * HD,), jnp.float32) * sc, 'Wo': jax.random.normal(ks[8], (NH * HD, H), jnp.float32) * sc, 'qn_w': jnp.ones((HD,), jnp.float32), 'kn_w': jnp.ones((HD,), jnp.float32)}
    _L0_xattn_all = _L0_xattn_setup()
    _L0_xattn_in = {k: v for k, v in _L0_xattn_all.items() if k in ('Wq', 'bq', 'Wk', 'bk', 'Wv', 'bv', 'Wo', 'qn_w', 'kn_w')}
    del _L0_xattn_all

    def _L0_ffn_setup():
        import jax, jax.numpy as jnp
        import numpy as np
        B, T, C = (2, 128, 256)
        E, TOPK = (8, 2)
        F_MOE = 176
        F_SHARED = 704
        key = jax.random.key(seed)
        ks = jax.random.split(key, 9)
        s = 0.02
        return {'x': jax.random.normal(ks[0], (B, T, C), dtype=jnp.float32), 'gate_w': jax.random.normal(ks[1], (E, C), dtype=jnp.float32) * s, 'expert_fc1': jax.random.normal(ks[2], (E, F_MOE, C), dtype=jnp.float32) * s, 'expert_fc2': jax.random.normal(ks[3], (E, F_MOE, C), dtype=jnp.float32) * s, 'expert_proj': jax.random.normal(ks[4], (E, C, F_MOE), dtype=jnp.float32) * s, 'shared_fc1': jax.random.normal(ks[5], (F_SHARED, C), dtype=jnp.float32) * s, 'shared_fc2': jax.random.normal(ks[6], (F_SHARED, C), dtype=jnp.float32) * s, 'shared_proj': jax.random.normal(ks[7], (C, F_SHARED), dtype=jnp.float32) * s, 'shared_gate_w': jax.random.normal(ks[8], (1, C), dtype=jnp.float32) * s}
    _L0_ffn_all = _L0_ffn_setup()
    _L0_ffn_in = {k: v for k, v in _L0_ffn_all.items() if k in ('gate_w', 'expert_fc1', 'expert_fc2', 'expert_proj', 'shared_fc1', 'shared_fc2', 'shared_proj', 'shared_gate_w')}
    del _L0_ffn_all
    return {'x': x, 'ctx_2048': ctx_2048, 'mask_1xSxS2_ff0': mask_1xSxS2_ff0, 'g_xattn': g_xattn, 'g_ffn': g_ffn, 'L0_xattn_Wq': _L0_xattn_in['Wq'], 'L0_xattn_bq': _L0_xattn_in['bq'], 'L0_xattn_Wk': _L0_xattn_in['Wk'], 'L0_xattn_bk': _L0_xattn_in['bk'], 'L0_xattn_Wv': _L0_xattn_in['Wv'], 'L0_xattn_bv': _L0_xattn_in['bv'], 'L0_xattn_Wo': _L0_xattn_in['Wo'], 'L0_xattn_qn_w': _L0_xattn_in['qn_w'], 'L0_xattn_kn_w': _L0_xattn_in['kn_w'], 'L0_ffn_gate_w': _L0_ffn_in['gate_w'], 'L0_ffn_expert_fc1': _L0_ffn_in['expert_fc1'], 'L0_ffn_expert_fc2': _L0_ffn_in['expert_fc2'], 'L0_ffn_expert_proj': _L0_ffn_in['expert_proj'], 'L0_ffn_shared_fc1': _L0_ffn_in['shared_fc1'], 'L0_ffn_shared_fc2': _L0_ffn_in['shared_fc2'], 'L0_ffn_shared_proj': _L0_ffn_in['shared_proj'], 'L0_ffn_shared_gate_w': _L0_ffn_in['shared_gate_w']}

def reference(x, ctx_2048, mask_1xSxS2_ff0, g_xattn, g_ffn, L0_xattn_Wq, L0_xattn_bq, L0_xattn_Wk, L0_xattn_bk, L0_xattn_Wv, L0_xattn_bv, L0_xattn_Wo, L0_xattn_qn_w, L0_xattn_kn_w, L0_ffn_gate_w, L0_ffn_expert_fc1, L0_ffn_expert_fc2, L0_ffn_expert_proj, L0_ffn_shared_fc1, L0_ffn_shared_fc2, L0_ffn_shared_proj, L0_ffn_shared_gate_w):
    import jax
    import jax.numpy as jnp

    def _L0_xattn_ref(hidden_states, encoder_hidden_states, attention_mask, Wq, bq, Wk, bk, Wv, bv, Wo, qn_w, kn_w):
        import jax, jax.numpy as jnp
        import numpy as np
        H = 256
        NH = 16
        NKV = 4
        HD = 128
        GROUPS = NH // NKV
        EPS = 1e-06
        B, S, SE = (1, 256, 512)

        def _rmsnorm(x, w, eps=EPS):
            xf = x.astype(jnp.float32)
            var = jnp.mean(xf * xf, axis=-1, keepdims=True)
            return (xf * jax.lax.rsqrt(var + eps)).astype(x.dtype) * w
        b, s, _ = hidden_states.shape
        se = encoder_hidden_states.shape[1]
        q = (hidden_states @ Wq + bq).reshape(b, s, NH, HD).transpose(0, 2, 1, 3)
        k = (encoder_hidden_states @ Wk + bk).reshape(b, se, NKV, HD).transpose(0, 2, 1, 3)
        v = (encoder_hidden_states @ Wv + bv).reshape(b, se, NKV, HD).transpose(0, 2, 1, 3)
        k = jnp.repeat(k, GROUPS, axis=1)
        v = jnp.repeat(v, GROUPS, axis=1)
        q = _rmsnorm(q, qn_w)
        k = _rmsnorm(k, kn_w)
        scale = 1.0 / np.sqrt(HD).astype(np.float32)
        scores = jnp.einsum('bhsd,bhed->bhse', q, k) * scale
        scores = scores + attention_mask[:, None, :, :]
        probs = jax.nn.softmax(scores.astype(jnp.float32), axis=-1).astype(q.dtype)
        out = jnp.einsum('bhse,bhed->bhsd', probs, v)
        out = out.transpose(0, 2, 1, 3).reshape(b, s, NH * HD)
        return out @ Wo

    def _L0_ffn_ref(x, gate_w, expert_fc1, expert_fc2, expert_proj, shared_fc1, shared_fc2, shared_proj, shared_gate_w):
        import jax, jax.numpy as jnp
        import numpy as np
        B, T, C = (2, 128, 256)
        E, TOPK = (8, 2)
        F_MOE = 176
        F_SHARED = 704
        b, t, c = x.shape
        xf = x.reshape(-1, c)
        n = xf.shape[0]
        router = xf @ gate_w.T
        probs = jax.nn.softmax(router.astype(jnp.float32), axis=1).astype(x.dtype)
        top_p, top_i = jax.lax.top_k(probs, TOPK)
        combine = jnp.zeros((n, E), dtype=x.dtype).at[jnp.arange(n)[:, None], top_i].set(top_p)
        h1 = jnp.einsum('nc,efc->enf', xf, expert_fc1)
        h2 = jnp.einsum('nc,efc->enf', xf, expert_fc2)
        h = jax.nn.silu(h1) * h2
        out_e = jnp.einsum('enf,ecf->enc', h, expert_proj)
        y = jnp.einsum('ne,enc->nc', combine, out_e)
        s1 = xf @ shared_fc1.T
        s2 = xf @ shared_fc2.T
        shared = jax.nn.silu(s1) * s2 @ shared_proj.T
        y = y + jax.nn.sigmoid(xf @ shared_gate_w.T) * shared
        return y.reshape(b, t, c)
    x = x + jnp.tanh(g_xattn[0]) * _L0_xattn_ref(_layernorm(x, axis=-1), ctx_2048, mask_1xSxS2_ff0, L0_xattn_Wq, L0_xattn_bq, L0_xattn_Wk, L0_xattn_bk, L0_xattn_Wv, L0_xattn_bv, L0_xattn_Wo, L0_xattn_qn_w, L0_xattn_kn_w)
    x = x + jnp.tanh(g_ffn[0]) * _L0_ffn_ref(_layernorm(x, axis=-1), L0_ffn_gate_w, L0_ffn_expert_fc1, L0_ffn_expert_fc2, L0_ffn_expert_proj, L0_ffn_shared_fc1, L0_ffn_shared_fc2, L0_ffn_shared_proj, L0_ffn_shared_gate_w)
    return x

_drawn_inputs = setup_inputs


def setup_inputs(seed=0):
    import zlib

    import numpy as np

    out = dict(_drawn_inputs(seed))
    spreads = {'L0_xattn_qn_w': (1.0, 0.6), 'L0_xattn_kn_w': (1.0, 0.6)}
    factors = {'L0_xattn_bq': 8.0,
     'L0_xattn_bk': 8.0,
     'L0_xattn_bv': 4.304,
     'L0_ffn_gate_w': 8.0,
     'L0_ffn_expert_fc1': 8.0,
     'L0_ffn_expert_fc2': 8.0,
     'L0_ffn_expert_proj': 8.0,
     'L0_ffn_shared_fc1': 4.293,
     'L0_ffn_shared_fc2': 4.264,
     'L0_ffn_shared_proj': 4.256,
     'L0_ffn_shared_gate_w': 8.0}
    for name, (base, spread) in spreads.items():
        noise = np.random.default_rng([zlib.crc32(name.encode()), seed]).standard_normal(out[name].shape)
        drawn = base * np.exp(spread * noise) if base else spread * noise
        out[name] = jnp.asarray(drawn.astype(out[name].dtype))
    for name, factor in factors.items():
        out[name] = (out[name] * factor).astype(out[name].dtype)
    return out
```

```python
from contextlib import ExitStack

import numpy as np
import concourse.bass as bass
from concourse import mybir

F32 = mybir.dt.float32
F32R = mybir.dt.float32r
F16 = mybir.dt.float16
BF16 = mybir.dt.bfloat16
ACT = mybir.ActivationFunctionType
ALU = mybir.AluOpType
AX = mybir.AxisListType

P = 128
C = 256
KC = C // P
HD = 128
NH = 16
NKV = 4
GQ = NH // NKV
SEQ = 64
BANK = 512
Q8 = 8
QF = NH * HD
KVF = NKV * HD
LN_EPS = 1e-5
RMS_EPS = 1e-6
QK_GAIN = 8192.0
NE = 8
F_SHARED = 704
F_MOE = 176
SH_CHUNKS = -(-F_SHARED // P)
EX_CHUNKS = NE * F_MOE // P
CHUNKS = SH_CHUNKS + EX_CHUNKS
SH_TAIL = F_SHARED - (SH_CHUNKS - 1) * P
GROUP = 512
GT = GROUP // P


def wait_for(eng, sem, value):
    if not isinstance(value, int) or value > 0:
        eng.wait_ge(sem, value)


def three_products(eng, out, stat_hi, stat_lo, mov_hi, mov_lo, first, last):
    eng.matmul(out, stat_hi, mov_hi, start=first, stop=False)
    eng.matmul(out, stat_hi, mov_lo, start=False, stop=False)
    return eng.matmul(out, stat_lo, mov_hi, start=False, stop=last)


def expert_spans(chunk):
    spans, at = [], chunk * P
    while at < (chunk + 1) * P:
        end = min((at // F_MOE + 1) * F_MOE, (chunk + 1) * P)
        spans.append((at // F_MOE, at - chunk * P, end - chunk * P))
        at = end
    return spans


def attention_pass(nc, ins, kept, scratch):
    x_tok = ins["x"].rearrange("b s c -> (b s) c")
    ctx_tok = ins["ctx"].rearrange("b s c -> (b s) c")
    T = x_tok.shape[0] // P
    x1_dram, x2h_dram, x2l_dram = scratch["x1"], scratch["x2h"], scratch["x2l"]
    ident, logits = kept["ident"], kept["logits"]

    with ExitStack() as es:
        def sb(name, shape, dt=F32):
            return es.enter_context(nc.sbuf_tensor(name, shape, dt))

        def sem(name):
            return es.enter_context(nc.semaphore(name))

        wq_h, wq_l = sb("wq_h", [P, KC, QF], F32R), sb("wq_l", [P, KC, QF], F32R)
        wkv_h, wkv_l = sb("wkv_h", [P, KC, 2 * KVF], F32R), sb("wkv_l", [P, KC, 2 * KVF], F32R)
        wo_h, wo_l = sb("wo_h", [P, NH, C], F32R), sb("wo_l", [P, NH, C], F32R)
        bias = sb("bias", [P, QF + 2 * KVF])
        mask = sb("mask", [P, SEQ])
        gate_rows = sb("gate_rows", [NE + 1, C])
        gate_t = sb("gate_t", [P, KC, NE + 1])
        norm_rows = sb("norm_rows", [P, 2, HD])
        norm_cols = sb("norm_cols", [P, 2])
        w_prod = sb("w_prod", [P, HD])
        w_small = sb("w_small", [P, 8])
        neg_half = sb("neg_half", [P, NH + NKV])
        eps = sb("eps", [P, 5])
        xt = sb("xt", [P, 2, C])
        ct = sb("ct", [P, 2, C])
        xr = sb("xr", [P, 2, C])
        xn = sb("xn", [P, C])
        xc_h, xc_l = sb("xc_h", [P, 2, KC, P], F32R), sb("xc_l", [P, 2, KC, P], F32R)
        stats = sb("stats", [P, 6])
        moments = sb("moments", [P, 2])
        rstd = sb("rstd", [P, 2])
        qk = sb("qk", [P, QF + KVF])
        sq_junk = sb("sq_junk", [P, QF + KVF], BF16)
        sumsq = sb("sumsq", [P, NH + NKV])
        meansq = sb("meansq", [P, NH + NKV])
        rnorm = sb("rnorm", [P, NH + NKV])
        v32 = sb("v32", [P, KVF])
        v_own = sb("v_own", [P, 2, 2, KVF], F32R)
        v_other = sb("v_other", [P, 2, 2, KVF], F32R)
        qt_h, qt_l = sb("qt_h", [P, NH, P], F16), sb("qt_l", [P, NH, P], F16)
        kt_h, kt_l = sb("kt_h", [P, NKV, P], F16), sb("kt_l", [P, NKV, P], F16)
        probs = sb("probs", [P, NH, SEQ])
        row_max = sb("row_max", [P, NH])
        row_sum = sb("row_sum", [P, NH])
        row_inv = sb("row_inv", [P, NH])
        pt_h, pt_l = sb("pt_h", [P, 2, GQ, P], F32R), sb("pt_l", [P, 2, GQ, P], F32R)
        ot_h, ot_l = sb("ot_h", [P, NH, P], F32R), sb("ot_l", [P, NH, P], F32R)
        x1 = sb("x1", [P, 2, C])
        stats2 = sb("stats2", [P, 6])
        moments2 = sb("moments2", [P, 2])
        rstd2 = sb("rstd2", [P, 2])
        spacer = sb("spacer", [P, 2])
        xn2 = sb("xn2", [P, C])
        x2t = sb("x2t", [P, KC, P])
        x2_h, x2_l = sb("x2_h", [P, 2, KC, P], F32R), sb("x2_l", [P, 2, KC, P], F32R)
        tanh_g = kept["tanh_g"]

        work = es.enter_context(nc.psum_tensor("work", [P, 5, BANK], F32))
        turn = es.enter_context(nc.psum_tensor("turn", [P, 2, BANK], F32))
        yb = es.enter_context(nc.psum_tensor("yb", [P, BANK], F32))

        consts_in = sem("consts_in")
        bias_in = sem("bias_in")
        raw_in = [sem(f"raw_in{i}") for i in range(2)]
        raw_h = sem("raw_h")
        raw_l = sem("raw_l")
        ident_zero, ident_done = sem("ident_zero"), sem("ident_done")
        pool_consts = sem("pool_consts")
        w_step = sem("w_step")
        gates_done = sem("gates_done")
        gate_turned, gate_split = sem("gate_turned"), sem("gate_split")
        x_in = [sem(f"x_in{i}") for i in range(2)]
        xr_in = [sem(f"xr_in{i}") for i in range(2)]
        x_stats, x_moments, x_vareps, x_rstd = sem("x_stats"), sem("x_moments"), sem("x_vareps"), sem("x_rstd")
        xn_ready, x_turned, x_high, x_split = sem("xn_ready"), sem("x_turned"), sem("x_high"), sem("x_split")
        proj_done = sem("proj_done")
        proj_taken = sem("proj_taken")
        squared = sem("squared")
        ms_ready, rn_ready = sem("ms_ready"), sem("rn_ready")
        normed = sem("normed")
        v_high, v_split = sem("v_high"), sem("v_split")
        v_swapped = [sem(f"v_swapped{i}") for i in range(2)]
        qk_turned, qk_high, qk_split = sem("qk_turned"), sem("qk_high"), sem("qk_split")
        s_done, s_taken, max_done = sem("s_done"), sem("s_taken"), sem("max_done")
        shifted, expd, summed, inverted, probs_ready = (
            sem("shifted"), sem("expd"), sem("summed"), sem("inverted"), sem("probs_ready"))
        p_turned, p_high, p_split = sem("p_turned"), sem("p_high"), sem("p_split")
        pv_done, o_high, o_split = sem("pv_done"), sem("o_high"), sem("o_split")
        y_done, x1_ready = sem("y_done"), sem("x1_ready")
        x2_stats, x2_moments, x2_vareps, x2_rstd = (
            sem("x2_stats"), sem("x2_moments"), sem("x2_vareps"), sem("x2_rstd"))
        xn2_ready, x2_turned, x2_copied, x2_high, x2_split = (
            sem("xn2_ready"), sem("x2_turned"), sem("x2_copied"), sem("x2_high"), sem("x2_split"))
        lg_done, lg_taken = sem("lg_done"), sem("lg_taken")
        x1_out = [sem(f"x1_out{i}") for i in range(2)]
        x2_out = [sem(f"x2_out{i}") for i in range(2)]

        stage = [qk[:, 0:QF], es.enter_context(nc.sbuf_tensor("stage", [P, QF], F32))[:, :]]
        wq_rows = ins["Wq"].rearrange("(k p) n -> p k n", p=P)
        wo_rows = ins["Wo"].rearrange("(h p) n -> p h n", p=P)
        kv_stage = lambda s: s.rearrange("p (k n) -> p k n", k=KC)
        wo_stage = lambda s: s.rearrange("p (h n) -> p h n", n=C)
        H2 = NH // 2
        bank_of = (4, 0, 1, 2, 3, 4)
        pieces = [
            (lambda s: kv_stage(s), wkv_h[:, :, :], wkv_l[:, :, :],
             [(lambda s: kv_stage(s)[:, :, 0:KVF], ins["Wk"].rearrange("(k p) n -> p k n", p=P)),
              (lambda s: kv_stage(s)[:, :, KVF:2 * KVF], ins["Wv"].rearrange("(k p) n -> p k n", p=P))]),
            (lambda s: s, wq_h[:, 0, :], wq_l[:, 0, :], [(lambda s: s, wq_rows[:, 0, :])]),
            (lambda s: s, wq_h[:, 1, :], wq_l[:, 1, :], [(lambda s: s, wq_rows[:, 1, :])]),
            (lambda s: wo_stage(s), wo_h[:, 0:H2, :], wo_l[:, 0:H2, :],
             [(lambda s: wo_stage(s), wo_rows[:, 0:H2, :])]),
            (lambda s: wo_stage(s), wo_h[:, H2:NH, :], wo_l[:, H2:NH, :],
             [(lambda s: wo_stage(s), wo_rows[:, H2:NH, :])]),
        ]
        stage_of = [1, 0, 1, 0, 1]
        raw_count = [[], []]
        for n, piece in enumerate(pieces):
            s = stage_of[n]
            before = raw_count[s][-1][1] if raw_count[s] else 0
            raw_count[s].append((n, before + 16 * len(piece[3])))
        raw_ready = {n: (s, c) for s in range(2) for n, c in raw_count[s]}
        WO_FIRST = 3

        def at(k, p, ahead):
            q = p + ahead
            return k + q // 2, q % 2

        def turns(step):
            def run(eng):
                for t in range(4):
                    step(t // 2, t % 2, t)
                with eng.Fori(2, T // 2 - 1) as k:
                    step(k, 0, k * 2)
                    step(k, 1, k * 2 + 1)
                for t in range(T - 2, T + 2):
                    step(t // 2, t % 2, t)
            return run

        def has(t, ahead):
            return not isinstance(t, int) or 0 <= t + ahead < T

        block = es.enter_context(nc.Block())

        @block.sync
        def _(sp):
            def load_tile(k, p, t):
                rows = bass.ds(t * P, P)
                sp.dma_start(xt[:, p, :], x_tok[rows, :]).then_inc(x_in[p], 16)
                sp.dma_start(ct[:, p, :], ctx_tok[rows, :]).then_inc(x_in[p], 16)

            def load_piece(n):
                s = stage_of[n]
                earlier = [m for m in range(n) if stage_of[m] == s]
                if earlier:
                    sp.wait_ge(raw_l, earlier[-1] + 1)
                for part, src in pieces[n][3]:
                    sp.dma_start(part(stage[s]), src).then_inc(raw_in[s], 16)

            load_tile(0, 0, 0)
            load_piece(0)
            load_tile(0, 1, 1)
            load_piece(1)
            sp.dma_start(mask[0:SEQ, :], ins["mask"][0, :, :]).then_inc(consts_in, 16)
            sp.dma_start(mask[SEQ:P, :], ins["mask"][0, :, :]).then_inc(consts_in, 16)
            for n, w in enumerate((ins["qn"], ins["kn"])):
                sp.dma_start(norm_rows[:, n, :], w.partition_broadcast(P)).then_inc(consts_in, 16)
                sp.dma_start(norm_cols[:, n:n + 1], w.rearrange("(p a) -> p a", a=1)).then_inc(consts_in, 16)
            sp.dma_start(gate_rows[0:NE, :], ins["gate_w"]).then_inc(consts_in, 16)
            sp.dma_start(gate_rows[NE:NE + 1, :], ins["shared_gate_w"]).then_inc(consts_in, 16)
            for n, g in enumerate((ins["g_xattn"], ins["g_ffn"])):
                sp.dma_start(kept["gates"][:, n:n + 1], g.partition_broadcast(P)).then_inc(consts_in, 16)
            at_col = 0
            for b in (ins["bq"], ins["bk"], ins["bv"]):
                n = b.shape[0]
                sp.dma_start(bias[:, at_col:at_col + n], b.partition_broadcast(P)).then_inc(bias_in, 16)
                at_col += n
            for n in range(2, len(pieces)):
                load_piece(n)

            def step(k, p, t):
                if has(t, 2):
                    wait_for(sp, xn_ready, t + 1)
                    wait_for(sp, x_turned, t + 1)
                    load_tile(*at(k, p, 2), t + 2)
                if has(t, 0):
                    wait_for(sp, x1_ready, t - 1)
                    sp.dma_start(xr[:, p, :], x_tok[bass.ds(t * P, P), :]).then_inc(xr_in[p], 16)
                    wait_for(sp, v_split, t + 1)
                    wait_for(sp, pv_done, t * 4 - 4)
                    half = P // 2
                    sp.dma_start(v_other[0:half, p, :, :].bitcast(F32), v_own[half:P, p, :, :].bitcast(F32)).then_inc(v_swapped[p], 16)
                    sp.dma_start(v_other[half:P, p, :, :].bitcast(F32), v_own[0:half, p, :, :].bitcast(F32)).then_inc(v_swapped[p], 16)
                if has(t, -2):
                    cols = bass.ds(t * P - 2 * P, P)
                    sp.wait_ge(x1_ready, t - 1)
                    sp.wait_ge(x2_split, t - 1)
                    sp.dma_start(x1_dram[cols, :], x1[:, p, :]).then_inc(x1_out[p], 16)
                    sp.dma_start(x2h_dram[:, :, cols].rearrange("k p n -> p k n"),
                                 x2_h[:, p, :, :].bitcast(F32)).then_inc(x2_out[p], 16)
                    sp.dma_start(x2l_dram[:, :, cols].rearrange("k p n -> p k n"),
                                 x2_l[:, p, :, :].bitcast(F32)).then_inc(x2_out[p], 16)

            turns(step)(sp)
            for p in range(2):
                sp.wait_ge(x1_out[p], 16 * T // 2)
                sp.wait_ge(x2_out[p], 32 * T // 2)

        @block.gpsimd
        def _(pool):
            pool.memset(ident[:, :], 0.0).then_inc(ident_zero, 1)
            pool.memset(neg_half[:, :], -0.5).then_inc(pool_consts, 1)
            pool.memset(eps[:, 0:1], LN_EPS).then_inc(pool_consts, 1)
            pool.memset(eps[:, 1:5], RMS_EPS * HD / QK_GAIN ** 2).then_inc(pool_consts, 1)
            pool.wait_ge(ident_zero, 1)
            pool.affine_select(out=ident[:, :], in_=ident[:, :], compare_op=ALU.not_equal, fill=1.0,
                               base=0, pattern=[[-1, P]], channel_multiplier=1).then_inc(ident_done, 1)
            pool.wait_ge(pool_consts, 3)

            def reciprocal_std(t):
                pool.wait_ge(x_moments, t + 1)
                wait_for(pool, xn_ready, t)
                pool.tensor_tensor(rstd[:, 0:1], moments[:, 1:2], eps[:, 0:1], ALU.add).then_inc(x_vareps, 1)
                pool.wait_ge(x_vareps, t + 1)
                pool.tensor_tensor(rstd[:, 1:2], rstd[:, 0:1], neg_half[:, 0:1], ALU.pow).then_inc(x_rstd, 1)

            def shift(t, u):
                heads = slice(u * Q8, u * Q8 + Q8)
                pool.wait_ge(max_done, t * 2 + (u + 1))
                pool.tensor_tensor(probs[:, heads, :], probs[:, heads, :],
                                   row_max[:, heads].unsqueeze(2).broadcast_to([P, Q8, SEQ]),
                                   ALU.subtract).then_inc(shifted, 1)

            def normalise_probs(t, u):
                heads = slice(u * Q8, u * Q8 + Q8)
                pool.wait_ge(inverted, t * 2 + (u + 1))
                pool.tensor_tensor(probs[:, heads, :], probs[:, heads, :],
                                   row_inv[:, heads].unsqueeze(2).broadcast_to([P, Q8, SEQ]),
                                   ALU.mult).then_inc(probs_ready, 1)

            def rms_norm(t, j):
                s = slice(4 * j, 4 * j + 4)
                col = QF if j == 0 else (j - 1) * BANK
                pool.wait_ge(squared, t * 5 + (j + 1))
                pool.tensor_tensor(meansq[:, s], sumsq[:, s], eps[:, 1:5], ALU.add).then_inc(ms_ready, 1)
                pool.wait_ge(ms_ready, t * 5 + (j + 1))
                pool.tensor_tensor(rnorm[:, s], meansq[:, s], neg_half[:, s], ALU.pow).then_inc(rn_ready, 1)
                pool.wait_ge(rn_ready, t * 5 + (j + 1))
                part = qk[:, col:col + BANK].rearrange("p (h d) -> p h d", d=HD)
                pool.tensor_tensor(part, part, rnorm[:, s].unsqueeze(2).broadcast_to([P, 4, HD]),
                                   ALU.mult).then_inc(normed, 1)

            reciprocal_std(0)
            reciprocal_std(1)

            def step(k, p, t):
                if has(t, -1):
                    shift(t - 1, 0)
                    shift(t - 1, 1)
                    normalise_probs(t - 1, 0)
                    normalise_probs(t - 1, 1)
                if has(t, 0):
                    rms_norm(t, 0)
                    for j in range(1, 5):
                        rms_norm(t, j)
                    pool.wait_ge(v_high, t + 1)
                    pool.tensor_tensor(v_own[:, p, 1, :], v32[:, :], v_own[:, p, 0, :],
                                       ALU.subtract).then_inc(v_split, 1)
                if has(t, 2):
                    reciprocal_std(t + 2)
                if has(t, -1):
                    pool.wait_ge(x2_moments, t)
                    wait_for(pool, xn2_ready, t - 1)
                    pool.tensor_tensor(rstd2[:, 0:1], moments2[:, 1:2], eps[:, 0:1], ALU.add).then_inc(x2_vareps, 1)
                    pool.wait_ge(x2_vareps, t)
                    pool.tensor_tensor(rstd2[:, 1:2], rstd2[:, 0:1], neg_half[:, 0:1], ALU.pow
                                       ).then_inc(x2_rstd, 1)

            turns(step)(pool)

        @block.scalar
        def _(act):
            act.wait_ge(consts_in, 16 * 10)
            act.activation(tanh_g[:, :], kept["gates"][:, :], ACT.Tanh).then_inc(gates_done, 1)

            def split_high(n):
                s, count = raw_ready[n]
                view, high, low, _ = pieces[n]
                act.wait_ge(raw_in[s], count)
                act.activation(high, view(stage[s]), ACT.Copy).then_inc(raw_h, 1)

            def x_highs(t):
                act.wait_ge(x_turned, t + 1)
                wait_for(act, proj_done, t * 6)
                act.activation(xc_h[:, :, :, :], turn_x, ACT.Copy).then_inc(x_high, 1)

            def squares(t, j):
                act.wait_ge(proj_taken, t * 6 + (j + 1))
                wait_for(act, ms_ready, t * 5 + (j + 1) - 5)
                for h in range(4):
                    col = (QF if j == 0 else (j - 1) * BANK) + h * HD
                    ins_ = act.activation(sq_junk[:, col:col + HD], qk[:, col:col + HD], ACT.Square,
                                          scale=1.0 / QK_GAIN,
                                          accum_out=sumsq[:, 4 * j + h:4 * j + h + 1])
                ins_.then_inc(squared, 1)

            def probs_high(t, u):
                act.wait_ge(p_turned, t * 2 + (u - 1))
                wait_for(act, pv_done, t * 4 - 4)
                act.activation(pt_h[:, u, :, :], turn[:, 1 - u, :].rearrange("p (i n) -> p i n", i=GQ),
                               ACT.Copy).then_inc(p_high, 1)

            def exponents(t, u):
                heads = slice(u * Q8, u * Q8 + Q8)
                act.wait_ge(shifted, t * 2 + (u + 1))
                act.activation(probs[:, heads, :], probs[:, heads, :], ACT.Exp).then_inc(expd, 1)

            turn_x = turn[:, 1, :].rearrange("p (s k n) -> p s k n", s=2, k=KC)
            split_high(0)
            split_high(1)
            x_highs(0)
            for n in range(2, len(pieces)):
                split_high(n)
            act.wait_ge(gate_turned, 1)
            act.activation(gate_t[:, :, :], yb[:, 0:KC * (NE + 1)].rearrange("p (k n) -> p k n", k=KC),
                           ACT.Copy).then_inc(gate_split, 1)
            def step(k, p, t):
                if has(t, -1):
                    exponents(t - 1, 0)
                if has(t, -2):
                    pk, _ = at(k, p, -2)
                    act.wait_ge(x2_turned, t - 1)
                    wait_for(act, lg_done, t - 2)
                    turned = yb[:, C:2 * C].rearrange("p (k n) -> p k n", k=KC)
                    act.activation(x2t[:, :, :], turned, ACT.Copy).then_inc(x2_copied, 1)
                    wait_for(act, x2_out[p], pk * 32)
                    act.activation(x2_h[:, p, :, :], turned, ACT.Copy).then_inc(x2_high, 1)
                if has(t, 0):
                    squares(t, 0)
                if has(t, -1):
                    exponents(t - 1, 1)
                if has(t, 0):
                    squares(t, 1)
                    squares(t, 2)
                if has(t, -1):
                    probs_high(t, 0)
                if has(t, -2):
                    act.wait_ge(lg_done, t - 1)
                    act.activation(logits[:, bass.ds(t - 2, 1), :], yb[:, 0:NE + 1].unsqueeze(1), ACT.Copy
                                   ).then_inc(lg_taken, 1)
                if has(t, 0):
                    squares(t, 3)
                if has(t, -1):
                    probs_high(t, 1)
                if has(t, 0):
                    squares(t, 4)
                for g in range(NKV):
                    if g == 2 and has(t, 1):
                        x_highs(t + 1)
                    if has(t, -1):
                        act.wait_ge(pv_done, t * 4 + (g - 3))
                        wait_for(act, y_done, t - 1)
                        act.activation(ot_h[:, GQ * g:GQ * g + GQ, :],
                                       work[:, g, :].rearrange("p (i n) -> p i n", i=GQ),
                                       ACT.Copy).then_inc(o_high, 1)
                if has(t, 0):
                    act.wait_ge(qk_turned, t * 5 + 1)
                    wait_for(act, s_done, t * 2)
                    act.activation(kt_h[:, :, :], turn[:, 0, :].rearrange("p (h n) -> p h n", h=NKV),
                                   ACT.Copy, scale=w_small[:, 7:8]).then_inc(qk_high, 1)
                    act.wait_ge(proj_taken, t * 6 + 6)
                    wait_for(act, pv_done, t * 4 - 4)
                    act.activation(v_own[:, p, 0, :], v32[:, :], ACT.Copy).then_inc(v_high, 1)
                    for j in range(4):
                        act.wait_ge(qk_turned, t * 5 + (j + 2))
                        act.activation(qt_h[:, 4 * j:4 * j + 4, :],
                                       turn[:, 1 - j % 2, :].rearrange("p (h n) -> p h n", h=4),
                                       ACT.Copy).then_inc(qk_high, 1)

            turns(step)(act)

        @block.vector
        def _(dve):
            def split_low(n):
                s, _ = raw_ready[n]
                view, high, low, _ = pieces[n]
                dve.wait_ge(raw_h, n + 1)
                dve.tensor_tensor(low, view(stage[s]), high, ALU.subtract).then_inc(raw_l, 1)

            def x_statistics(k, p, t):
                dve.wait_ge(x_in[p], k * 32 + 32)
                wait_for(dve, x_moments, t)
                dve.bn_stats(stats[:, :], xt[:, p, :]).then_inc(x_stats, 1)
                wait_for(dve, xn_ready, t)
                dve.wait_ge(x_stats, t * 2 + 1)
                dve.memset(spacer[:, 0:1], 0.0).then_inc(x_stats, 1)
                dve.bn_aggr(moments[:, :], stats[:, :]).then_inc(x_moments, 1)

            def x_normalise(k, p, t):
                dve.wait_ge(x_rstd, t + 1)
                wait_for(dve, x_turned, t)
                dve.tensor_scalar(xn[:, :], xt[:, p, :], moments[:, 0:1], rstd[:, 1:2],
                                  ALU.subtract, ALU.mult).then_inc(xn_ready, 1)

            def x_lows(t):
                dve.wait_ge(x_high, t + 1)
                dve.tensor_tensor(xc_l[:, :, :, :], turn[:, 1, :].rearrange("p (s k n) -> p s k n", s=2, k=KC),
                                  xc_h[:, :, :, :], ALU.subtract).then_inc(x_split, 1)

            def q_low(t, j):
                dve.wait_ge(qk_high, t * 5 + (j + 2))
                dve.tensor_tensor(qt_l[:, 4 * j:4 * j + 4, :],
                                  turn[:, 1 - j % 2, :].rearrange("p (h n) -> p h n", h=4),
                                  qt_h[:, 4 * j:4 * j + 4, :], ALU.subtract).then_inc(qk_split, 1)

            def add_bias(t, j):
                dve.wait_ge(proj_done, t * 6 + (j + 1))
                if j == 0:
                    wait_for(dve, qk_turned, t * 5)
                if j == 5:
                    wait_for(dve, v_split, t)
                col = QF if j == 0 else QF + KVF if j == 5 else (j - 1) * BANK
                dst = v32[:, :] if j == 5 else qk[:, col:col + BANK]
                dve.tensor_tensor(dst, work[:, bank_of[j], :], bias[:, col:col + BANK], ALU.add
                                  ).then_inc(proj_taken, 1)

            def sums(t, u):
                heads = slice(u * Q8, u * Q8 + Q8)
                dve.wait_ge(expd, t * 2 + (u + 1))
                dve.tensor_reduce(row_sum[:, heads], probs[:, heads, :], AX.X, ALU.add).then_inc(summed, 1)
                dve.wait_ge(summed, t * 2 + (u + 1))
                wait_for(dve, probs_ready, t * 2 + (u - 1))
                dve.reciprocal(row_inv[:, heads], row_sum[:, heads]).then_inc(inverted, 1)

            def take_scores(t, u):
                heads = slice(u * Q8, u * Q8 + Q8)
                pair = work[:, 2 * u:2 * u + 2, :].rearrange("p b (i n) -> p (b i) n", i=GQ)
                dve.wait_ge(s_done, t * 2 + (u + 1))
                wait_for(dve, p_turned, t * 2)
                for b in range(2):
                    rows, own = slice(b * SEQ, b * SEQ + SEQ), slice(b * SEQ, b * SEQ + SEQ)
                    dve.scalar_tensor_tensor(
                        probs[rows, heads, :], pair[rows, :, own], w_small[rows, 6:7],
                        mask[rows, :].unsqueeze(1).broadcast_to([SEQ, Q8, SEQ]), ALU.mult, ALU.add
                    ).then_inc(s_taken, 1)
                dve.wait_ge(s_taken, t * 4 + (2 * u + 2))
                dve.tensor_reduce(row_max[:, heads], probs[:, heads, :], AX.X, ALU.max).then_inc(max_done, 1)

            x_statistics(0, 0, 0)
            x_normalise(0, 0, 0)
            x_statistics(0, 1, 1)
            dve.wait_ge(consts_in, 16 * 10)
            dve.tensor_tensor(w_prod[:, :], norm_rows[:, 0, :], norm_rows[:, 1, :], ALU.mult).then_inc(w_step, 1)
            dve.tensor_tensor(w_small[:, 0:1], norm_cols[:, 0:1], norm_cols[:, 1:2], ALU.mult).then_inc(w_step, 1)
            dve.wait_ge(w_step, 2)
            dve.tensor_reduce(w_small[:, 1:2], w_prod[:, :], AX.X, ALU.max).then_inc(w_step, 1)
            dve.tensor_reduce(w_small[:, 2:3], w_prod[:, :], AX.X, ALU.min).then_inc(w_step, 1)
            dve.wait_ge(w_step, 4)
            dve.scalar_tensor_tensor(w_small[:, 3:4], w_small[:, 2:3], -1.0, w_small[:, 1:2],
                                     ALU.mult, ALU.max).then_inc(w_step, 1)
            dve.wait_ge(w_step, 5)
            dve.tensor_scalar(w_small[:, 4:5], w_small[:, 3:4], 1e-30, None, ALU.max).then_inc(w_step, 1)
            dve.wait_ge(w_step, 6)
            dve.reciprocal(w_small[:, 5:6], w_small[:, 4:5]).then_inc(w_step, 1)
            dve.tensor_scalar(w_small[:, 6:7], w_small[:, 4:5], float(np.float32(1.0) / np.sqrt(np.float32(HD))),
                              HD / QK_GAIN ** 2, ALU.mult, ALU.mult).then_inc(w_step, 1)
            dve.wait_ge(w_step, 8)
            dve.tensor_tensor(w_small[:, 7:8], w_small[:, 0:1], w_small[:, 5:6], ALU.mult).then_inc(w_step, 1)
            split_low(0)
            split_low(1)
            x_lows(0)
            dve.wait_ge(bias_in, 48)
            for n in range(2, len(pieces)):
                split_low(n)
            dve.wait_ge(w_step, 9)
            dve.wait_ge(gates_done, 1)
            dve.wait_ge(raw_l, len(pieces) - 1)

            def step(k, p, t):
                pk, pp = at(k, p, -1)
                nk, np_ = at(k, p, 1)
                if has(t, 0):
                    add_bias(t, 0)
                if has(t, -2):
                    dve.wait_ge(x2_high, t - 1)
                    dve.tensor_tensor(x2_l[:, p, :, :], yb[:, C:2 * C].rearrange("p (k n) -> p k n", k=KC),
                                      x2_h[:, p, :, :], ALU.subtract).then_inc(x2_split, 1)
                if has(t, 0):
                    add_bias(t, 1)
                if has(t, -1):
                    sums(t - 1, 0)
                if has(t, 0):
                    add_bias(t, 2)
                if has(t, -1):
                    sums(t - 1, 1)
                if has(t, 0):
                    add_bias(t, 3)
                for u in range(2):
                    if u == 0 and has(t, 0):
                        add_bias(t, 4)
                    if has(t, -1):
                        dve.wait_ge(p_high, t * 2 + (u - 1))
                        dve.tensor_tensor(pt_l[:, u, :, :], turn[:, 1 - u, :].rearrange("p (i n) -> p i n", i=GQ),
                                          pt_h[:, u, :, :], ALU.subtract).then_inc(p_split, 1)
                    if u == 0 and has(t, 1):
                        x_normalise(nk, np_, t + 1)
                    if u == 0 and has(t, 0):
                        add_bias(t, 5)
                if has(t, 2):
                    x_statistics(k + 1, p, t + 2)
                for g in range(NKV):
                    if g == 2 and has(t, 1):
                        x_lows(t + 1)
                    if has(t, -1):
                        heads = slice(GQ * g, GQ * g + GQ)
                        dve.wait_ge(o_high, t * 4 + (g - 3))
                        dve.tensor_tensor(ot_l[:, heads, :], work[:, g, :].rearrange("p (i n) -> p i n", i=GQ),
                                          ot_h[:, heads, :], ALU.subtract).then_inc(o_split, 1)
                if has(t, 0):
                    dve.wait_ge(qk_high, t * 5 + 1)
                    dve.scalar_tensor_tensor(kt_l[:, :, :], turn[:, 0, :].rearrange("p (h n) -> p h n", h=NKV),
                                             w_small[:, 7:8], kt_h[:, :, :], ALU.mult, ALU.subtract
                                             ).then_inc(qk_split, 1)
                    q_low(t, 0)
                    q_low(t, 1)
                if has(t, -1):
                    dve.wait_ge(y_done, t)
                    dve.wait_ge(xr_in[pp], pk * 16 + 16)
                    wait_for(dve, x1_out[pp], pk * 16)
                    dve.scalar_tensor_tensor(x1[:, pp, :], yb[:, 0:C], tanh_g[:, 0:1], xr[:, pp, :],
                                             ALU.mult, ALU.add).then_inc(x1_ready, 1)
                if has(t, 0):
                    q_low(t, 2)
                    q_low(t, 3)
                if has(t, -1):
                    dve.wait_ge(x1_ready, t)
                    wait_for(dve, x2_moments, t - 1)
                    dve.bn_stats(stats2[:, :], x1[:, pp, :]).then_inc(x2_stats, 1)
                    wait_for(dve, xn2_ready, t - 1)
                    dve.wait_ge(x2_stats, t * 2 - 1)
                    dve.memset(spacer[:, 1:2], 0.0).then_inc(x2_stats, 1)
                    dve.bn_aggr(moments2[:, :], stats2[:, :]).then_inc(x2_moments, 1)
                    if has(t, 0):
                        take_scores(t, 0)
                    dve.wait_ge(x2_rstd, t)
                    wait_for(dve, x2_turned, t - 1)
                    dve.tensor_scalar(xn2[:, :], x1[:, pp, :], moments2[:, 0:1], rstd2[:, 1:2],
                                      ALU.subtract, ALU.mult).then_inc(xn2_ready, 1)
                if has(t, 0):
                    if not has(t, -1):
                        take_scores(t, 0)
                    take_scores(t, 1)

            turns(step)(dve)

        @block.tensor
        def _(pe):
            def turn_tile(p, t):
                pe.wait_ge(xn_ready, t + 1)
                for s, src in enumerate((xn[:, :], ct[:, p, :])):
                    for kc in range(KC):
                        at_ = (s * KC + kc) * P
                        ins_ = pe.transpose(turn[:, 1, at_:at_ + P], src[:, kc * P:kc * P + P], ident[:, :])
                ins_.then_inc(x_turned, 1)

            def project(t, j):
                if j == 0:
                    pe.wait_ge(x_split, t + 1)
                    wait_for(pe, proj_taken, t * 6)
                if j == 1:
                    wait_for(pe, s_taken, t * 4 - 2)
                if j == 3:
                    wait_for(pe, s_taken, t * 4)
                if j == 5:
                    pe.wait_ge(proj_taken, t * 6 + 1)
                if isinstance(t, int) and t == 0:
                    pe.wait_ge(raw_l, 1 if j in (0, 5) else WO_FIRST)
                src = 1 if j in (0, 5) else 0
                w_h, w_l = (wkv_h, wkv_l) if j in (0, 5) else (wq_h, wq_l)
                col = {0: 0, 5: KVF}.get(j, (j - 1) * BANK)
                for kc in range(KC):
                    ins_ = three_products(pe, work[:, bank_of[j], :], xc_h[:, src, kc, :], xc_l[:, src, kc, :],
                                          w_h[:, kc, col:col + BANK], w_l[:, kc, col:col + BANK],
                                          kc == 0, kc == KC - 1)
                ins_.then_inc(proj_done, 1)

            def turn_heads(j):
                col = QF if j == 0 else (j - 1) * BANK
                bank = j % 2
                for i in range(4):
                    ins_ = pe.transpose(turn[:, bank, i * P:i * P + P], qk[:, col + i * HD:col + (i + 1) * HD],
                                        ident[:, :])
                ins_.then_inc(qk_turned, 1)

            def scores(t, u):
                for place in range(Q8):
                    g, i = 2 * u + place % 2, place // 2
                    h, at_ = g * GQ + i, (place % 4) * P
                    ins_ = three_products(pe, work[:, 2 * u + place // 4, at_:at_ + P], qt_h[:, h, :], qt_l[:, h, :],
                                          kt_h[:, g, :], kt_l[:, g, :], True, True)
                ins_.then_inc(s_done, 1)

            def weighted_values(p, g):
                u, slot = g // 2, g % 2
                rows = slice(slot * SEQ, slot * SEQ + SEQ)
                bank = work[:, g, :].rearrange("p (i n) -> p i n", i=GQ)
                for b in range(2):
                    v = v_own if b == slot else v_other
                    cols = slice(b * SEQ, b * SEQ + SEQ)
                    ins_ = three_products(
                        pe, bank[:, :, cols], v[rows, p, 0, g * HD:(g + 1) * HD], v[rows, p, 1, g * HD:(g + 1) * HD],
                        pt_h[rows, u, :, cols], pt_l[rows, u, :, cols], True, True)
                ins_.then_inc(pv_done, 1)

            pe.wait_ge(ident_done, 1)
            turn_tile(0, 0)
            pe.wait_ge(consts_in, 16 * 10)
            for kc in range(KC):
                ins_ = pe.transpose(yb[:, kc * (NE + 1):(kc + 1) * (NE + 1)], gate_rows[:, kc * P:kc * P + P],
                                    ident[0:NE + 1, 0:NE + 1])
            ins_.then_inc(gate_turned, 1)

            def turn_probs(t, u):
                pe.wait_ge(qk_split, t * 5 + (u + 4))
                pe.wait_ge(probs_ready, t * 2 + (u + 1))
                for i in range(GQ):
                    two = probs[:, u * Q8 + 2 * i:u * Q8 + 2 * i + 2, :].rearrange("p s e -> p (s e)")
                    ins_ = pe.transpose(turn[:, 1 - u, i * P:i * P + P], two, ident[:, :])
                ins_.then_inc(p_turned, 1)

            def output_heads(t, g):
                pe.wait_ge(o_split, t * 4 + (g + 1))
                for h in range(g * GQ, g * GQ + GQ):
                    ins_ = three_products(pe, yb[:, 0:C], ot_h[:, h, :], ot_l[:, h, :], wo_h[:, h, :],
                                          wo_l[:, h, :], h == 0, h == NH - 1)
                if g == NKV - 1:
                    ins_.then_inc(y_done, 1)

            def turn_qk(t, j):
                if j == 1:
                    if has(t, 1):
                        pe.wait_ge(x_split, t + 2)
                if j > 1:
                    pe.wait_ge(qk_split, t * 5 + (j - 1))
                pe.wait_ge(normed, t * 5 + (j + 1))
                turn_heads(j)

            def step(k, p, t):
                pk, pp = at(k, p, -1)
                nk, np_ = at(k, p, 1)
                for j in range(6):
                    if j == 5 and has(t, -1):
                        turn_probs(t - 1, 0)
                    if has(t, 0):
                        project(t, j)
                    if j == 0 and has(t, -2):
                        pe.wait_ge(xn2_ready, t - 1)
                        for kc in range(KC):
                            ins_ = pe.transpose(yb[:, C + kc * P:C + kc * P + P], xn2[:, kc * P:kc * P + P], ident[:, :])
                        ins_.then_inc(x2_turned, 1)
                    if j == 4 and has(t, -2):
                        pe.wait_ge(x2_split, t - 1)
                        for kc in range(KC):
                            ins_ = pe.matmul(yb[:, 0:NE + 1], x2t[:, kc, :], gate_t[:, kc, :],
                                             start=(kc == 0), stop=(kc == KC - 1))
                        ins_.then_inc(lg_done, 1)
                if has(t, -1):
                    turn_probs(t - 1, 1)
                    pe.wait_ge(v_swapped[pp], pk * 32 + 32)
                for g in range(NKV):
                    if g == 2 and has(t, 1):
                        if not has(t, -1):
                            pe.wait_ge(x_split, 1)
                        turn_tile(np_, t + 1)
                    if has(t, -1):
                        if g % 2 == 0:
                            pe.wait_ge(p_split, t * 2 + (g // 2 - 1))
                        if has(t, 0):
                            pe.wait_ge(proj_taken, t * 6 + (g + 2))
                        elif g == 0:
                            pe.wait_ge(s_taken, t * 4)
                        weighted_values(pp, g)
                if has(t, -1):
                    if isinstance(t, int) and t == 1:
                        pe.wait_ge(raw_l, len(pieces))
                        pe.wait_ge(gate_split, 1)
                    wait_for(pe, lg_taken, t - 1)
                for g in range(NKV):
                    if has(t, 0):
                        turn_qk(t, g)
                    if has(t, -1):
                        output_heads(t - 1, g)
                if has(t, 0):
                    turn_qk(t, 4)
                    pe.wait_ge(qk_split, t * 5 + 3)
                    scores(t, 0)
                    pe.wait_ge(qk_split, t * 5 + 5)
                    scores(t, 1)

            turns(step)(pe)


def ffn_pass(nc, ins, kept, scratch, out):
    T = kept["logits"].shape[1]
    NG = T // GT
    x1_dram, x2h_dram, x2l_dram, comb_dram = (scratch[n] for n in ("x1", "x2h", "x2l", "comb"))
    out_tok = out.rearrange("b s c -> (b s) c")
    ident, logits, tanh_g = kept["ident"], kept["logits"], kept["tanh_g"]

    with ExitStack() as es:
        def sb(name, shape, dt=F32):
            return es.enter_context(nc.sbuf_tensor(name, shape, dt))

        def sem(name):
            return es.enter_context(nc.semaphore(name))

        w12_h, w12_l = sb("w12_h", [P, CHUNKS, 2 * KC, P], F32R), sb("w12_l", [P, CHUNKS, 2 * KC, P], F32R)
        wp_h, wp_l = sb("wp_h", [P, CHUNKS, C], F32R), sb("wp_l", [P, CHUNKS, C], F32R)
        RAW = 4
        raw_fc = sb("raw_fc", [P, RAW, 2, C])
        small = [P, T, NE]
        prob, hit, pick1, pick2, comb = (sb(n, small) for n in ("prob", "hit", "pick1", "pick2", "comb"))
        col = {n: sb(f"col_{n}", [P, T]) for n in ("max", "sum", "inv", "top", "place", "sig", "sinv")}
        sgate = sb("sgate", [P, T])
        comb_t = sb("comb_t", [P, T * NE // P, P])
        xg_h, xg_l = sb("xg_h", [P, 2, KC, GROUP], F32R), sb("xg_l", [P, 2, KC, GROUP], F32R)
        weight = sb("weight", [P, 2, EX_CHUNKS, GROUP])
        xy = sb("xy", [P, 2, GT, C])
        act_s = sb("act_s", [P, 2, GROUP])
        hid = sb("hid", [P, 2, GROUP])
        hid_h, hid_l = sb("hid_h", [P, 2, GROUP], F32R), sb("hid_l", [P, 2, GROUP], F32R)
        raw_sp = weight[:, 1, 0:3, :].rearrange("p a n -> p (a n)")[:, 0:KC * F_SHARED].rearrange(
            "p (k f) -> p k f", k=KC)
        raw_ep = weight[:, 1, 3:9, :].rearrange("p a n -> p (a n)")[:, 0:KC * NE * F_MOE].rearrange(
            "p (k f) -> p k f", k=KC)

        hb = es.enter_context(nc.psum_tensor("hb", [P, 4, BANK], F32))
        acc = es.enter_context(nc.psum_tensor("acc", [P, 4, BANK], F32))

        fc_in = [sem(f"fc_in{i}") for i in range(RAW)]
        proj_in = sem("proj_in")
        zeroed, desc_ready = sem("zeroed"), sem("desc_ready")
        prep_turned, prep_high, prep_low = sem("prep_turned"), sem("prep_high"), sem("prep_low")
        route = sem("route")
        route_exp, gate_exp = sem("route_exp"), sem("gate_exp")
        comb_turned, comb_copied, comb_out = sem("comb_turned"), sem("comb_copied"), sem("comb_out")
        xg_in = [sem(f"xg_in{i}") for i in range(2)]
        wt_in = [sem(f"wt_in{i}") for i in range(2)]
        xy_in = [sem(f"xy_in{i}") for i in range(2)]
        y_out = [sem(f"y_out{i}") for i in range(2)]
        h1_done, h2_done = sem("h1_done"), sem("h2_done")
        silu_done, weighed, h_done = sem("silu_done"), sem("weighed"), sem("h_done")
        hid_high, hid_low = sem("hid_high"), sem("hid_low")
        down_done = sem("down_done")
        sh_taken, ex_taken = sem("sh_taken"), sem("ex_taken")

        prep = [("fc", c) for c in range(SH_CHUNKS)]
        prep += [("proj", (c, c + 1)) for c in range(0, SH_CHUNKS, 2)]
        prep += [("fc", c) for c in range(SH_CHUNKS, CHUNKS)]
        prep += [("proj", tuple(range(c, min(c + 2, CHUNKS)))) for c in range(SH_CHUNKS, CHUNKS, 2)]
        fill_of_fc = {what[1]: n for n, what in enumerate(prep) if what[0] == "fc"}
        fc_rows = [(ins["shared_fc1"], ins["shared_fc2"]),
                   tuple(ins[n].rearrange("e f c -> (e f) c") for n in ("expert_fc1", "expert_fc2"))]

        def rows_of(c):
            return SH_TAIL if c == SH_CHUNKS - 1 else P

        def prep_views(n, high_or_low):
            kind, c = prep[n]
            bank = hb[:, n % 4, :]
            if kind == "fc":
                dst = (w12_h, w12_l)[high_or_low]
                r = rows_of(c)
                return [(bank.rearrange("p (m f) -> p m f", m=2 * KC)[:, :, 0:r], dst[:, c, :, 0:r])]
            dst = (wp_h, wp_l)[high_or_low]
            return [(bank[0:rows_of(m), i * C:(i + 1) * C], dst[0:rows_of(m), m, :]) for i, m in enumerate(c)]

        def steps(step):
            def run(eng):
                step(0, 0, 0)
                step(0, 1, 1)
                with eng.Fori(1, NG // 2) as k:
                    step(k, 0, k * 2)
                    step(k, 1, k * 2 + 1)
                step(NG // 2, 0, NG)
            return run

        def has(n, ahead):
            return not isinstance(n, int) or 0 <= n + ahead < NG

        block = es.enter_context(nc.Block())

        @block.sync
        def _(sp):
            def load_fc(c):
                slot = c % RAW
                if c >= RAW:
                    sp.wait_ge(prep_turned, fill_of_fc[c - RAW] + 1)
                shared, r0 = c < SH_CHUNKS, (c if c < SH_CHUNKS else c - SH_CHUNKS) * P
                for f, w in enumerate(fc_rows[0 if shared else 1]):
                    sp.dma_start(raw_fc[0:rows_of(c), slot, f, :], w[r0:r0 + rows_of(c), :]
                                 ).then_inc(fc_in[slot], 16)

            def load_tokens(p, n):
                cols = bass.ds(n * GROUP, GROUP)
                for dst, src in ((xg_h, x2h_dram), (xg_l, x2l_dram)):
                    sp.dma_start(dst[:, p, :, :].bitcast(F32), src[:, :, cols].rearrange("k p n -> p k n")
                                 ).then_inc(xg_in[p], 16)

            def load_residual(p, n):
                sp.dma_start(xy[:, p, :, :], x1_dram[bass.ds(n * GROUP, GROUP), :].rearrange(
                    "(j p) c -> p j c", p=P)).then_inc(xy_in[p], 16)

            def load_weights_of_tokens(p, n):
                for cc in range(EX_CHUNKS):
                    for e, r0, r1 in expert_spans(cc):
                        src = comb_dram[bass.ds(n * GT, GT), e, :]
                        sp.dma_start(weight[r0:r1, p, cc, :].rearrange("p (j n) -> p j n", j=GT),
                                     src.partition_broadcast(r1 - r0)).then_inc(wt_in[p], 16)

            for c in range(RAW):
                load_fc(c)
            sp.dma_start(raw_sp, ins["shared_proj"].rearrange("(k p) f -> p k f", p=P)).then_inc(proj_in, 16)
            for kc in range(KC):
                sp.dma_start(raw_ep[:, kc, :].rearrange("p (e f) -> p e f", e=NE),
                             ins["expert_proj"][:, kc * P:(kc + 1) * P, :].rearrange("e p f -> p e f")
                             ).then_inc(proj_in, 16)
            load_tokens(0, 0)
            load_residual(0, 0)
            for c in range(RAW, CHUNKS):
                load_fc(c)
            sp.wait_ge(comb_copied, 1)
            sp.dma_start(comb_dram.rearrange("t e n -> (t e) n").rearrange("(h q) n -> q h n", q=P), comb_t[:, :, :]
                         ).then_inc(comb_out, 16)
            sp.wait_ge(comb_out, 16)
            load_weights_of_tokens(0, 0)

            def step(k, p, n, more):
                q = 1 - p
                if has(n, 0) and more:
                    wait_for(sp, h2_done, n * CHUNKS)
                    load_tokens(q, n + 1)
                    if isinstance(n, int) and n == 0:
                        sp.wait_ge(prep_turned, len(prep))
                    wait_for(sp, weighed, n * EX_CHUNKS)
                    load_weights_of_tokens(q, n + 1)
                if has(n, -1):
                    before = k - 1 if p == 0 else k
                    sp.wait_ge(ex_taken, n * GT)
                    sp.dma_start(out_tok[bass.ds(n * GROUP - GROUP, GROUP), :].rearrange("(j p) c -> p j c", p=P),
                                 xy[:, q, :, :]).then_inc(y_out[q], 16)
                    sp.wait_ge(y_out[q], before * 16 + 16)
                if has(n, 0) and more:
                    load_residual(q, n + 1)

            step(0, 0, 0, True)
            step(0, 1, 1, True)
            with sp.Fori(1, NG // 2 - 1) as k:
                step(k, 0, k * 2, True)
                step(k, 1, k * 2 + 1, True)
            step(NG // 2 - 1, 0, NG - 2, True)
            step(NG // 2 - 1, 1, NG - 1, False)
            step(NG // 2, 0, NG, False)

        @block.gpsimd
        def _(pool):
            def step(k, p, n):
                if not has(n, 0):
                    return
                pool.wait_ge(wt_in[p], (k * 16 + 16) * sum(len(expert_spans(cc)) for cc in range(EX_CHUNKS)))
                for cc in range(EX_CHUNKS):
                    c = SH_CHUNKS + cc
                    par = (p + c) % 2
                    pool.wait_ge(silu_done, n * CHUNKS + (c + 1))
                    pool.tensor_tensor(act_s[:, par, :], act_s[:, par, :], weight[:, p, cc, :], ALU.mult
                                       ).then_inc(weighed, 1)

            steps(step)(pool)

        @block.scalar
        def _(act):
            act.wait_ge(route, 2)
            act.activation(prob[:, :, :], prob[:, :, :], ACT.Exp).then_inc(route_exp, 1)
            act.activation(col["sig"][:, :].unsqueeze(2), logits[:, :, NE:NE + 1], ACT.Exp, scale=-1.0
                           ).then_inc(gate_exp, 1)
            for n in range(len(prep)):
                act.wait_ge(prep_turned, n + 1)
                for src, dst in prep_views(n, 0):
                    ins_ = act.activation(dst, src, ACT.Copy)
                ins_.then_inc(prep_high, 1)

            def step(k, p, n):
                for c in range(CHUNKS):
                    m = n * CHUNKS + c
                    par = (p + c) % 2
                    if has(n, 0):
                        act.wait_ge(h1_done, m + 1)
                        wait_for(act, h_done, m - 1)
                        act.activation(act_s[:, par, :], hb[:, 2 * par, :], ACT.Silu).then_inc(silu_done, 1)
                    if has(n, 0) and (c > 0 or has(n, -1)) or (c == 0 and has(n, -1)):
                        act.wait_ge(h_done, m)
                        wait_for(act, down_done, m - 2)
                        act.activation(hid_h[:, 1 - par, :], hid[:, 1 - par, :], ACT.Copy).then_inc(hid_high, 1)

            steps(step)(act)

        @block.vector
        def _(dve):
            c = SH_CHUNKS - 1
            for w in (w12_h, w12_l):
                dve.memset(w[:, c, :, SH_TAIL:P].bitcast(F32), 0.0).then_inc(zeroed, 1)
            for w in (wp_h, wp_l):
                dve.memset(w[SH_TAIL:P, c, :].bitcast(F32), 0.0).then_inc(zeroed, 1)
            for e in range(NE):
                dve.memset(kept["rank"][:, e:e + 1], float(NE - e)).then_inc(desc_ready, 1)

            chain = 0

            def link(ins_):
                nonlocal chain
                chain += 1
                ins_.then_inc(route, 1)
                dve.wait_ge(route, chain)

            wide = lambda t: t[:, :].unsqueeze(2).broadcast_to([P, T, NE])
            rank = kept["rank"][:, :].unsqueeze(1).broadcast_to([P, T, NE])
            expert_logits = logits[:, :, 0:NE]
            link(dve.tensor_reduce(col["max"][:, :], expert_logits, AX.X, ALU.max))
            link(dve.tensor_tensor(prob[:, :, :], expert_logits, wide(col["max"]), ALU.subtract))
            dve.wait_ge(route_exp, 1)
            link(dve.tensor_reduce(col["sum"][:, :], prob[:, :, :], AX.X, ALU.add))
            link(dve.reciprocal(col["inv"][:, :], col["sum"][:, :]))
            link(dve.tensor_tensor(prob[:, :, :], prob[:, :, :], wide(col["inv"]), ALU.mult))
            dve.wait_ge(desc_ready, NE)
            for pick, left in ((pick1, prob), (pick2, comb)):
                link(dve.tensor_reduce(col["top"][:, :], left[:, :, :], AX.X, ALU.max))
                link(dve.tensor_tensor(hit[:, :, :], left[:, :, :], wide(col["top"]), ALU.is_equal))
                link(dve.tensor_tensor(hit[:, :, :], hit[:, :, :], rank, ALU.mult))
                link(dve.tensor_reduce(col["place"][:, :], hit[:, :, :], AX.X, ALU.max))
                link(dve.tensor_tensor(pick[:, :, :], hit[:, :, :], wide(col["place"]), ALU.is_equal))
                if pick is pick1:
                    link(dve.scalar_tensor_tensor(comb[:, :, :], pick1[:, :, :], -2.0, prob[:, :, :],
                                                  ALU.mult, ALU.add))
            link(dve.tensor_tensor(hit[:, :, :], pick1[:, :, :], pick2[:, :, :], ALU.add))
            link(dve.tensor_tensor(comb[:, :, :], hit[:, :, :], prob[:, :, :], ALU.mult))
            dve.wait_ge(gate_exp, 1)
            link(dve.tensor_scalar(col["sinv"][:, :], col["sig"][:, :], 1.0, None, ALU.add))
            link(dve.reciprocal(col["sig"][:, :], col["sinv"][:, :]))
            link(dve.tensor_scalar(sgate[:, :], col["sig"][:, :], tanh_g[:, 1:2], None, ALU.mult))

            for n in range(len(prep)):
                dve.wait_ge(prep_high, n + 1)
                for (src, low), (_, high) in zip(prep_views(n, 1), prep_views(n, 0)):
                    ins_ = dve.tensor_tensor(low, src, high, ALU.subtract)
                ins_.then_inc(prep_low, 1)
            dve.wait_ge(comb_turned, 1)
            dve.tensor_copy(comb_t[:, :, :], hb[:, COMB_BANK, 0:T * NE].rearrange("p (h n) -> p h n", n=P)
                            ).then_inc(comb_copied, 1)

            def step(k, p, n):
                for c in range(CHUNKS):
                    m = n * CHUNKS + c
                    par = (p + c) % 2
                    if has(n, 0):
                        dve.wait_ge(h2_done, m + 1)
                        if c < SH_CHUNKS:
                            dve.wait_ge(silu_done, m + 1)
                        else:
                            dve.wait_ge(weighed, n * EX_CHUNKS + (c - SH_CHUNKS + 1))
                        wait_for(dve, hid_low, m - 1)
                        dve.tensor_tensor(hid[:, par, :], hb[:, 2 * par + 1, :], act_s[:, par, :], ALU.mult
                                          ).then_inc(h_done, 1)
                    if has(n, 0) and (c > 0 or has(n, -1)) or (c == 0 and has(n, -1)):
                        dve.wait_ge(hid_high, m)
                        dve.tensor_tensor(hid_l[:, 1 - par, :], hid[:, 1 - par, :], hid_h[:, 1 - par, :],
                                          ALU.subtract).then_inc(hid_low, 1)
                    if c == 3 and has(n, -1):
                        dve.wait_ge(down_done, n * CHUNKS)
                        for j in range(GT):
                            dve.scalar_tensor_tensor(
                                xy[:, 1 - p, j, :], acc[:, 2 + j // 2, (j % 2) * C:(j % 2 + 1) * C],
                                tanh_g[:, 1:2], xy[:, 1 - p, j, :], ALU.mult, ALU.add).then_inc(ex_taken, 1)
                    if c == SH_CHUNKS + 3 and has(n, 0):
                        dve.wait_ge(down_done, n * CHUNKS + SH_CHUNKS)
                        dve.wait_ge(xy_in[p], k * 16 + 16)
                        for j in range(GT):
                            dve.scalar_tensor_tensor(
                                xy[:, p, j, :], acc[:, j // 2, (j % 2) * C:(j % 2 + 1) * C],
                                sgate[:, bass.ds(n * GT + j, 1)], xy[:, p, j, :], ALU.mult, ALU.add
                            ).then_inc(sh_taken, 1)

            steps(step)(dve)

        @block.tensor
        def _(pe):
            for n, (kind, c) in enumerate(prep):
                if n >= 4:
                    pe.wait_ge(prep_low, n - 3)
                if kind == "fc":
                    pe.wait_ge(fc_in[c % RAW], (c // RAW + 1) * 32)
                    r = rows_of(c)
                    for m in range(2 * KC):
                        ins_ = pe.transpose(hb[:, n % 4, m * P:m * P + r],
                                            raw_fc[0:r, c % RAW, m // KC, (m % KC) * P:(m % KC + 1) * P],
                                            ident[0:r, 0:r])
                else:
                    pe.wait_ge(proj_in, 48)
                    for i, m in enumerate(c):
                        raw, f0 = (raw_sp, m * P) if m < SH_CHUNKS else (raw_ep, (m - SH_CHUNKS) * P)
                        r = rows_of(m)
                        for kc in range(KC):
                            at_ = i * C + kc * P
                            ins_ = pe.transpose(hb[0:r, n % 4, at_:at_ + P], raw[:, kc, f0:f0 + r], ident[:, :])
                ins_.then_inc(prep_turned, 1)
            pe.wait_ge(route, ROUTE_COMB)
            pe.wait_ge(prep_low, (len(prep) - 1) // 4 * 4 + 1)
            for h in range(T * NE // P):
                per = P // NE
                ins_ = pe.transpose(hb[:, COMB_BANK, h * P:(h + 1) * P],
                                    comb[:, h * per:(h + 1) * per, :].rearrange("p t e -> p (t e)"), ident[:, :])
            ins_.then_inc(comb_turned, 1)
            pe.wait_ge(prep_low, len(prep))
            pe.wait_ge(comb_copied, 1)
            pe.wait_ge(zeroed, 4)

            def up(k, p, n, c):
                m = n * CHUNKS + c
                par = (p + c) % 2
                if c == 0:
                    pe.wait_ge(xg_in[p], k * 32 + 32)
                wait_for(pe, h_done, m - 1)
                for f, done in enumerate((h1_done, h2_done)):
                    for kc in range(KC):
                        ins_ = three_products(pe, hb[:, 2 * par + f, :], w12_h[:, c, f * KC + kc, :],
                                              w12_l[:, c, f * KC + kc, :], xg_h[:, p, kc, :], xg_l[:, p, kc, :],
                                              kc == 0, kc == KC - 1)
                    ins_.then_inc(done, 1)

            def down(n, c, par):
                pe.wait_ge(hid_low, n * CHUNKS + (c + 1))
                if c == 0:
                    wait_for(pe, sh_taken, n * GT)
                if c == SH_CHUNKS:
                    wait_for(pe, ex_taken, n * GT)
                base = 0 if c < SH_CHUNKS else 2
                last = c in (SH_CHUNKS - 1, CHUNKS - 1)
                for j in range(GT):
                    dst = acc[:, base + j // 2, (j % 2) * C:(j % 2 + 1) * C]
                    cols = slice(j * P, (j + 1) * P)
                    opens = c in (0, SH_CHUNKS) and j % 2 == 0
                    pe.matmul(dst, hid_h[:, par, cols], wp_h[:, c, :], start=opens, stop=False,
                              skip_group_check=True)
                    pe.matmul(dst, hid_h[:, par, cols], wp_l[:, c, :], start=False, stop=False,
                              skip_group_check=True)
                    ins_ = pe.matmul(dst, hid_l[:, par, cols], wp_h[:, c, :], start=False, stop=last,
                                     skip_group_check=True)
                ins_.then_inc(down_done, 1)

            def step(k, p, n):
                for c in range(CHUNKS):
                    if has(n, 0):
                        up(k, p, n, c)
                    if c >= 2 and has(n, 0):
                        down(n, c - 2, (p + c) % 2)
                    if c < 2 and has(n, -1):
                        down(n - 1, c + CHUNKS - 2, (p + c) % 2)

            steps(step)(pe)


ROUTE_COMB = 18
COMB_BANK = 0


def flamingo_block(nc, x, ctx_2048, mask, g_xattn, g_ffn, Wq, bq, Wk, bk, Wv, bv, Wo, qn_w, kn_w, gate_w,
                   expert_fc1, expert_fc2, expert_proj, shared_fc1, shared_fc2, shared_proj, shared_gate_w, out):
    B, S, _ = x.shape
    N = B * S
    ins = dict(x=x, ctx=ctx_2048, mask=mask, g_xattn=g_xattn, g_ffn=g_ffn, Wq=Wq, bq=bq, Wk=Wk, bk=bk, Wv=Wv,
               bv=bv, Wo=Wo, qn=qn_w, kn=kn_w, gate_w=gate_w, expert_fc1=expert_fc1, expert_fc2=expert_fc2,
               expert_proj=expert_proj, shared_fc1=shared_fc1, shared_fc2=shared_fc2, shared_proj=shared_proj,
               shared_gate_w=shared_gate_w)
    scratch = dict(
        x1=nc.dram_tensor("x1_scratch", [N, C], F32, kind="Internal").ap(),
        x2h=nc.dram_tensor("x2h_scratch", [KC, P, N], F32, kind="Internal").ap(),
        x2l=nc.dram_tensor("x2l_scratch", [KC, P, N], F32, kind="Internal").ap(),
        comb=nc.dram_tensor("comb_scratch", [N // P, NE, P], F32, kind="Internal").ap(),
    )
    with ExitStack() as es:
        kept = {name: es.enter_context(nc.sbuf_tensor(name, shape, F32)) for name, shape in (
            ("ident", [P, P]), ("logits", [P, N // P, NE + 1]), ("gates", [P, 2]), ("tanh_g", [P, 2]),
            ("rank", [P, NE]))}
        attention_pass(nc, ins, kept, scratch)
        ffn_pass(nc, ins, kept, scratch, out)


_INS = ['x', 'ctx_2048', 'mask_1xSxS2_ff0', 'g_xattn', 'g_ffn', 'L0_xattn_Wq', 'L0_xattn_bq', 'L0_xattn_Wk',
        'L0_xattn_bk', 'L0_xattn_Wv', 'L0_xattn_bv', 'L0_xattn_Wo', 'L0_xattn_qn_w', 'L0_xattn_kn_w',
        'L0_ffn_gate_w', 'L0_ffn_expert_fc1', 'L0_ffn_expert_fc2', 'L0_ffn_expert_proj', 'L0_ffn_shared_fc1',
        'L0_ffn_shared_fc2', 'L0_ffn_shared_proj', 'L0_ffn_shared_gate_w']
_OUTS = [((64, 64, 256), 'float32')]


def kernel(**inputs):
    import numpy as _np
    import concourse.bacc as _bacc
    from concourse import mybir as _mybir
    from concourse.bass_utils import run_bass_kernel_spmd as _run

    nc = _bacc.Bacc("TRN2", target_bir_lowering=False, num_devices=1)
    arrays, args = {}, []
    for name in _INS:
        a = _np.ascontiguousarray(inputs[name])
        arrays[f"in_{name}_dram"] = a
        args.append(nc.dram_tensor(f"in_{name}_dram", a.shape, _mybir.dt.from_np(a.dtype), kind="ExternalInput").ap())
    for i, (shape, dtype) in enumerate(_OUTS):
        dt = _mybir.dt.from_np(_np.dtype(dtype))
        args.append(nc.dram_tensor(f"out_{i}_dram", shape, dt, kind="ExternalOutput").ap())
    flamingo_block(nc, *args)
    r = _run(nc, [arrays], core_ids=[0])
    return r.results[0]["out_0_dram"]
```

```python
from contextlib import ExitStack

import numpy as np
import concourse.bass as bass
from concourse import mybir

F32 = mybir.dt.float32
F32R = mybir.dt.float32r
F16 = mybir.dt.float16
BF16 = mybir.dt.bfloat16
U32 = mybir.dt.uint32
I32 = mybir.dt.int32
ACT = mybir.ActivationFunctionType
ALU = mybir.AluOpType
AX = mybir.AxisListType

P = 128
C = 256
KC = C // P
HD = 128
NH = 16
NKV = 4
GQ = NH // NKV
SEQ = 64
BANK = 512
Q8 = 8
QF = NH * HD
KVF = NKV * HD
LN_EPS = 1e-5
RMS_EPS = 1e-6
QK_GAIN = 8192.0
NE = 8
F_SHARED = 704
F_MOE = 176
SH_CHUNKS = -(-F_SHARED // P)
SH_TAIL = F_SHARED - (SH_CHUNKS - 1) * P
GROUP = 512
GT = GROUP // P


def wait_for(eng, sem, value):
    if not isinstance(value, int) or value > 0:
        eng.wait_ge(sem, value)


def three_products(eng, out, stat_hi, stat_lo, mov_hi, mov_lo, first, last):
    eng.matmul(out, stat_hi, mov_hi, start=first, stop=False)
    eng.matmul(out, stat_hi, mov_lo, start=False, stop=False)
    return eng.matmul(out, stat_lo, mov_hi, start=False, stop=last)


def attention_pass(nc, ins, kept, scratch):
    x_tok = ins["x"].rearrange("b s c -> (b s) c")
    ctx_tok = ins["ctx"].rearrange("b s c -> (b s) c")
    T = x_tok.shape[0] // P
    x1_dram, x2h_dram, x2l_dram = scratch["x1"], scratch["x2h"], scratch["x2l"]
    x2_dram, sorted_x = scratch["x2"], scratch["sorted_x"]
    ident, logits = kept["ident"], kept["logits"]
    ZP = 96
    ZC = sorted_x.shape[0] * C // (T * ZP)

    with ExitStack() as es:
        def sb(name, shape, dt=F32):
            return es.enter_context(nc.sbuf_tensor(name, shape, dt))

        def sem(name):
            return es.enter_context(nc.semaphore(name))

        wq_h, wq_l = sb("wq_h", [P, KC, QF], F32R), sb("wq_l", [P, KC, QF], F32R)
        wkv_h, wkv_l = sb("wkv_h", [P, KC, 2 * KVF], F32R), sb("wkv_l", [P, KC, 2 * KVF], F32R)
        wo_h, wo_l = sb("wo_h", [P, NH, C], F32R), sb("wo_l", [P, NH, C], F32R)
        bias = sb("bias", [P, QF + 2 * KVF])
        mask = sb("mask", [P, SEQ])
        gate_rows = sb("gate_rows", [NE + 1, C])
        gate_t = sb("gate_t", [P, KC, NE + 1])
        norm_rows = sb("norm_rows", [P, 2, HD])
        norm_cols = sb("norm_cols", [P, 2])
        w_prod = sb("w_prod", [P, HD])
        w_small = sb("w_small", [P, 8])
        neg_half = sb("neg_half", [P, NH + NKV])
        eps = sb("eps", [P, 5])
        xt = sb("xt", [P, 2, C])
        ct = sb("ct", [P, 2, C])
        xr = sb("xr", [P, 2, C])
        xn = sb("xn", [P, C])
        xc_h, xc_l = sb("xc_h", [P, 2, KC, P], F32R), sb("xc_l", [P, 2, KC, P], F32R)
        stats = sb("stats", [P, 6])
        moments = sb("moments", [P, 2])
        rstd = sb("rstd", [P, 2])
        qk = sb("qk", [P, QF + KVF])
        sq_junk = sb("sq_junk", [P, QF + KVF], BF16)
        sumsq = sb("sumsq", [P, NH + NKV])
        meansq = sb("meansq", [P, NH + NKV])
        rnorm = sb("rnorm", [P, NH + NKV])
        v32 = sb("v32", [P, KVF])
        v_own = sb("v_own", [P, 2, 2, KVF], F32R)
        v_other = sb("v_other", [P, 2, 2, KVF], F32R)
        qt_h, qt_l = sb("qt_h", [P, NH, P], F16), sb("qt_l", [P, NH, P], F16)
        kt_h, kt_l = sb("kt_h", [P, NKV, P], F16), sb("kt_l", [P, NKV, P], F16)
        probs = sb("probs", [P, NH, SEQ])
        row_max = sb("row_max", [P, NH])
        row_sum = sb("row_sum", [P, NH])
        row_inv = sb("row_inv", [P, NH])
        pt_h, pt_l = sb("pt_h", [P, 2, GQ, P], F32R), sb("pt_l", [P, 2, GQ, P], F32R)
        ot_h, ot_l = sb("ot_h", [P, NH, P], F32R), sb("ot_l", [P, NH, P], F32R)
        x1 = sb("x1", [P, 2, C])
        stats2 = sb("stats2", [P, 6])
        moments2 = sb("moments2", [P, 2])
        rstd2 = sb("rstd2", [P, 2])
        spacer = sb("spacer", [P, 2])
        xn2 = sb("xn2", [P, 2, C])
        zeros = sb("zeros", [ZP, ZC])
        x2t = sb("x2t", [P, KC, P])
        x2_h, x2_l = sb("x2_h", [P, 2, KC, P], F32R), sb("x2_l", [P, 2, KC, P], F32R)
        tanh_g = kept["tanh_g"]

        work = es.enter_context(nc.psum_tensor("work", [P, 5, BANK], F32))
        turn = es.enter_context(nc.psum_tensor("turn", [P, 2, BANK], F32))
        yb = es.enter_context(nc.psum_tensor("yb", [P, BANK], F32))

        consts_in = sem("consts_in")
        bias_in = sem("bias_in")
        raw_in = [sem(f"raw_in{i}") for i in range(2)]
        raw_h = sem("raw_h")
        raw_l = sem("raw_l")
        ident_zero, ident_done = sem("ident_zero"), sem("ident_done")
        pool_consts = sem("pool_consts")
        w_step = sem("w_step")
        gates_done = sem("gates_done")
        gate_turned, gate_split = sem("gate_turned"), sem("gate_split")
        x_in = [sem(f"x_in{i}") for i in range(2)]
        xr_in = [sem(f"xr_in{i}") for i in range(2)]
        x_stats, x_moments, x_vareps, x_rstd = sem("x_stats"), sem("x_moments"), sem("x_vareps"), sem("x_rstd")
        xn_ready, x_turned, x_high, x_split = sem("xn_ready"), sem("x_turned"), sem("x_high"), sem("x_split")
        proj_done = sem("proj_done")
        proj_taken = sem("proj_taken")
        squared = sem("squared")
        ms_ready, rn_ready = sem("ms_ready"), sem("rn_ready")
        normed = sem("normed")
        v_high, v_split = sem("v_high"), sem("v_split")
        v_swapped = [sem(f"v_swapped{i}") for i in range(2)]
        qk_turned, qk_high, qk_split = sem("qk_turned"), sem("qk_high"), sem("qk_split")
        s_done, s_taken, max_done = sem("s_done"), sem("s_taken"), sem("max_done")
        shifted, expd, summed, inverted, probs_ready = (
            sem("shifted"), sem("expd"), sem("summed"), sem("inverted"), sem("probs_ready"))
        p_turned, p_high, p_split = sem("p_turned"), sem("p_high"), sem("p_split")
        pv_done, o_high, o_split = sem("pv_done"), sem("o_high"), sem("o_split")
        y_done, x1_ready = sem("y_done"), sem("x1_ready")
        x2_stats, x2_moments, x2_vareps, x2_rstd = (
            sem("x2_stats"), sem("x2_moments"), sem("x2_vareps"), sem("x2_rstd"))
        xn2_ready, x2_turned, x2_copied, x2_high, x2_split = (
            sem("xn2_ready"), sem("x2_turned"), sem("x2_copied"), sem("x2_high"), sem("x2_split"))
        lg_done, lg_taken = sem("lg_done"), sem("lg_taken")
        zeros_ready, cleared = sem("zeros_ready"), sem("cleared")
        x1_out = [sem(f"x1_out{i}") for i in range(2)]
        x2_out = [sem(f"x2_out{i}") for i in range(2)]

        stage = [qk[:, 0:QF], es.enter_context(nc.sbuf_tensor("stage", [P, QF], F32))[:, :]]
        wq_rows = ins["Wq"].rearrange("(k p) n -> p k n", p=P)
        wo_rows = ins["Wo"].rearrange("(h p) n -> p h n", p=P)
        kv_stage = lambda s: s.rearrange("p (k n) -> p k n", k=KC)
        wo_stage = lambda s: s.rearrange("p (h n) -> p h n", n=C)
        H2 = NH // 2
        bank_of = (4, 0, 1, 2, 3, 4)
        pieces = [
            (lambda s: kv_stage(s), wkv_h[:, :, :], wkv_l[:, :, :],
             [(lambda s: kv_stage(s)[:, :, 0:KVF], ins["Wk"].rearrange("(k p) n -> p k n", p=P)),
              (lambda s: kv_stage(s)[:, :, KVF:2 * KVF], ins["Wv"].rearrange("(k p) n -> p k n", p=P))]),
            (lambda s: s, wq_h[:, 0, :], wq_l[:, 0, :], [(lambda s: s, wq_rows[:, 0, :])]),
            (lambda s: s, wq_h[:, 1, :], wq_l[:, 1, :], [(lambda s: s, wq_rows[:, 1, :])]),
            (lambda s: wo_stage(s), wo_h[:, 0:H2, :], wo_l[:, 0:H2, :],
             [(lambda s: wo_stage(s), wo_rows[:, 0:H2, :])]),
            (lambda s: wo_stage(s), wo_h[:, H2:NH, :], wo_l[:, H2:NH, :],
             [(lambda s: wo_stage(s), wo_rows[:, H2:NH, :])]),
        ]
        stage_of = [1, 0, 1, 0, 1]
        raw_count = [[], []]
        for n, piece in enumerate(pieces):
            s = stage_of[n]
            before = raw_count[s][-1][1] if raw_count[s] else 0
            raw_count[s].append((n, before + 16 * len(piece[3])))
        raw_ready = {n: (s, c) for s in range(2) for n, c in raw_count[s]}
        WO_FIRST = 3

        def at(k, p, ahead):
            q = p + ahead
            return k + q // 2, q % 2

        def turns(step):
            def run(eng):
                for t in range(4):
                    step(t // 2, t % 2, t)
                with eng.Fori(2, T // 2 - 1) as k:
                    step(k, 0, k * 2)
                    step(k, 1, k * 2 + 1)
                for t in range(T - 2, T + 2):
                    step(t // 2, t % 2, t)
            return run

        def has(t, ahead):
            return not isinstance(t, int) or 0 <= t + ahead < T

        block = es.enter_context(nc.Block())

        @block.sync
        def _(sp):
            def load_tile(k, p, t):
                rows = bass.ds(t * P, P)
                sp.dma_start(xt[:, p, :], x_tok[rows, :]).then_inc(x_in[p], 16)
                sp.dma_start(ct[:, p, :], ctx_tok[rows, :]).then_inc(x_in[p], 16)

            def load_piece(n):
                s = stage_of[n]
                earlier = [m for m in range(n) if stage_of[m] == s]
                if earlier:
                    sp.wait_ge(raw_l, earlier[-1] + 1)
                for part, src in pieces[n][3]:
                    sp.dma_start(part(stage[s]), src).then_inc(raw_in[s], 16)

            load_tile(0, 0, 0)
            load_piece(0)
            load_tile(0, 1, 1)
            load_piece(1)
            sp.dma_start(mask[0:SEQ, :], ins["mask"][0, :, :]).then_inc(consts_in, 16)
            sp.dma_start(mask[SEQ:P, :], ins["mask"][0, :, :]).then_inc(consts_in, 16)
            for n, w in enumerate((ins["qn"], ins["kn"])):
                sp.dma_start(norm_rows[:, n, :], w.partition_broadcast(P)).then_inc(consts_in, 16)
                sp.dma_start(norm_cols[:, n:n + 1], w.rearrange("(p a) -> p a", a=1)).then_inc(consts_in, 16)
            sp.dma_start(gate_rows[0:NE, :], ins["gate_w"]).then_inc(consts_in, 16)
            sp.dma_start(gate_rows[NE:NE + 1, :], ins["shared_gate_w"]).then_inc(consts_in, 16)
            for n, g in enumerate((ins["g_xattn"], ins["g_ffn"])):
                sp.dma_start(kept["gates"][:, n:n + 1], g.partition_broadcast(P)).then_inc(consts_in, 16)
            at_col = 0
            for b in (ins["bq"], ins["bk"], ins["bv"]):
                n = b.shape[0]
                sp.dma_start(bias[:, at_col:at_col + n], b.partition_broadcast(P)).then_inc(bias_in, 16)
                at_col += n
            for n in range(2, len(pieces)):
                load_piece(n)

            def step(k, p, t):
                if has(t, 2):
                    wait_for(sp, xn_ready, t + 1)
                    wait_for(sp, x_turned, t + 1)
                    load_tile(*at(k, p, 2), t + 2)
                if has(t, 0):
                    sp.dma_start(sorted_x[bass.ds(t * (ZP * ZC // C), ZP * ZC // C), :].rearrange(
                        "(p a) c -> p (a c)", p=ZP), zeros[:, :]).then_inc(cleared, 16)
                    wait_for(sp, x1_ready, t - 1)
                    sp.dma_start(xr[:, p, :], x_tok[bass.ds(t * P, P), :]).then_inc(xr_in[p], 16)
                    wait_for(sp, v_split, t + 1)
                    wait_for(sp, pv_done, t * 4 - 4)
                    half = P // 2
                    sp.dma_start(v_other[0:half, p, :, :].bitcast(F32), v_own[half:P, p, :, :].bitcast(F32)).then_inc(v_swapped[p], 16)
                    sp.dma_start(v_other[half:P, p, :, :].bitcast(F32), v_own[0:half, p, :, :].bitcast(F32)).then_inc(v_swapped[p], 16)
                if has(t, -2):
                    cols = bass.ds(t * P - 2 * P, P)
                    sp.wait_ge(x1_ready, t - 1)
                    sp.wait_ge(x2_split, t - 1)
                    sp.dma_start(x1_dram[cols, :], x1[:, p, :]).then_inc(x1_out[p], 16)
                    sp.dma_start(x2_dram[cols, :], xn2[:, p, :]).then_inc(x1_out[p], 16)
                    sp.dma_start(x2h_dram[:, :, cols].rearrange("k p n -> p k n"),
                                 x2_h[:, p, :, :].bitcast(F32)).then_inc(x2_out[p], 16)
                    sp.dma_start(x2l_dram[:, :, cols].rearrange("k p n -> p k n"),
                                 x2_l[:, p, :, :].bitcast(F32)).then_inc(x2_out[p], 16)

            sp.wait_ge(zeros_ready, 1)
            turns(step)(sp)
            sp.wait_ge(cleared, 16 * T)
            for p in range(2):
                sp.wait_ge(x1_out[p], 32 * T // 2)
                sp.wait_ge(x2_out[p], 32 * T // 2)

        @block.gpsimd
        def _(pool):
            pool.memset(ident[:, :], 0.0).then_inc(ident_zero, 1)
            pool.memset(neg_half[:, :], -0.5).then_inc(pool_consts, 1)
            pool.memset(eps[:, 0:1], LN_EPS).then_inc(pool_consts, 1)
            pool.memset(eps[:, 1:5], RMS_EPS * HD / QK_GAIN ** 2).then_inc(pool_consts, 1)
            pool.wait_ge(ident_zero, 1)
            pool.affine_select(out=ident[:, :], in_=ident[:, :], compare_op=ALU.not_equal, fill=1.0,
                               base=0, pattern=[[-1, P]], channel_multiplier=1).then_inc(ident_done, 1)
            pool.wait_ge(pool_consts, 3)

            def reciprocal_std(t):
                pool.wait_ge(x_moments, t + 1)
                wait_for(pool, xn_ready, t)
                pool.tensor_tensor(rstd[:, 0:1], moments[:, 1:2], eps[:, 0:1], ALU.add).then_inc(x_vareps, 1)
                pool.wait_ge(x_vareps, t + 1)
                pool.tensor_tensor(rstd[:, 1:2], rstd[:, 0:1], neg_half[:, 0:1], ALU.pow).then_inc(x_rstd, 1)

            def shift(t, u):
                heads = slice(u * Q8, u * Q8 + Q8)
                pool.wait_ge(max_done, t * 2 + (u + 1))
                pool.tensor_tensor(probs[:, heads, :], probs[:, heads, :],
                                   row_max[:, heads].unsqueeze(2).broadcast_to([P, Q8, SEQ]),
                                   ALU.subtract).then_inc(shifted, 1)

            def normalise_probs(t, u):
                heads = slice(u * Q8, u * Q8 + Q8)
                pool.wait_ge(inverted, t * 2 + (u + 1))
                pool.tensor_tensor(probs[:, heads, :], probs[:, heads, :],
                                   row_inv[:, heads].unsqueeze(2).broadcast_to([P, Q8, SEQ]),
                                   ALU.mult).then_inc(probs_ready, 1)

            def rms_norm(t, j):
                s = slice(4 * j, 4 * j + 4)
                col = QF if j == 0 else (j - 1) * BANK
                pool.wait_ge(squared, t * 5 + (j + 1))
                pool.tensor_tensor(meansq[:, s], sumsq[:, s], eps[:, 1:5], ALU.add).then_inc(ms_ready, 1)
                pool.wait_ge(ms_ready, t * 5 + (j + 1))
                pool.tensor_tensor(rnorm[:, s], meansq[:, s], neg_half[:, s], ALU.pow).then_inc(rn_ready, 1)
                pool.wait_ge(rn_ready, t * 5 + (j + 1))
                part = qk[:, col:col + BANK].rearrange("p (h d) -> p h d", d=HD)
                pool.tensor_tensor(part, part, rnorm[:, s].unsqueeze(2).broadcast_to([P, 4, HD]),
                                   ALU.mult).then_inc(normed, 1)

            reciprocal_std(0)
            reciprocal_std(1)

            def step(k, p, t):
                if has(t, -1):
                    shift(t - 1, 0)
                    shift(t - 1, 1)
                    normalise_probs(t - 1, 0)
                    normalise_probs(t - 1, 1)
                if has(t, 0):
                    rms_norm(t, 0)
                    for j in range(1, 5):
                        rms_norm(t, j)
                    pool.wait_ge(v_high, t + 1)
                    pool.tensor_tensor(v_own[:, p, 1, :], v32[:, :], v_own[:, p, 0, :],
                                       ALU.subtract).then_inc(v_split, 1)
                if has(t, 2):
                    reciprocal_std(t + 2)
                if has(t, -1):
                    pool.wait_ge(x2_moments, t)
                    wait_for(pool, xn2_ready, t - 1)
                    pool.tensor_tensor(rstd2[:, 0:1], moments2[:, 1:2], eps[:, 0:1], ALU.add).then_inc(x2_vareps, 1)
                    pool.wait_ge(x2_vareps, t)
                    pool.tensor_tensor(rstd2[:, 1:2], rstd2[:, 0:1], neg_half[:, 0:1], ALU.pow
                                       ).then_inc(x2_rstd, 1)

            turns(step)(pool)

        @block.scalar
        def _(act):
            act.wait_ge(consts_in, 16 * 10)
            act.activation(tanh_g[:, :], kept["gates"][:, :], ACT.Tanh).then_inc(gates_done, 1)

            def split_high(n):
                s, count = raw_ready[n]
                view, high, low, _ = pieces[n]
                act.wait_ge(raw_in[s], count)
                act.activation(high, view(stage[s]), ACT.Copy).then_inc(raw_h, 1)

            def x_highs(t):
                act.wait_ge(x_turned, t + 1)
                wait_for(act, proj_done, t * 6)
                act.activation(xc_h[:, :, :, :], turn_x, ACT.Copy).then_inc(x_high, 1)

            def squares(t, j):
                act.wait_ge(proj_taken, t * 6 + (j + 1))
                wait_for(act, ms_ready, t * 5 + (j + 1) - 5)
                for h in range(4):
                    col = (QF if j == 0 else (j - 1) * BANK) + h * HD
                    ins_ = act.activation(sq_junk[:, col:col + HD], qk[:, col:col + HD], ACT.Square,
                                          scale=1.0 / QK_GAIN,
                                          accum_out=sumsq[:, 4 * j + h:4 * j + h + 1])
                ins_.then_inc(squared, 1)

            def probs_high(t, u):
                act.wait_ge(p_turned, t * 2 + (u - 1))
                wait_for(act, pv_done, t * 4 - 4)
                act.activation(pt_h[:, u, :, :], turn[:, 1 - u, :].rearrange("p (i n) -> p i n", i=GQ),
                               ACT.Copy).then_inc(p_high, 1)

            def exponents(t, u):
                heads = slice(u * Q8, u * Q8 + Q8)
                act.wait_ge(shifted, t * 2 + (u + 1))
                act.activation(probs[:, heads, :], probs[:, heads, :], ACT.Exp).then_inc(expd, 1)

            turn_x = turn[:, 1, :].rearrange("p (s k n) -> p s k n", s=2, k=KC)
            split_high(0)
            split_high(1)
            x_highs(0)
            for n in range(2, len(pieces)):
                split_high(n)
            act.wait_ge(gate_turned, 1)
            act.activation(gate_t[:, :, :], yb[:, 0:KC * (NE + 1)].rearrange("p (k n) -> p k n", k=KC),
                           ACT.Copy).then_inc(gate_split, 1)
            def step(k, p, t):
                if has(t, -1):
                    exponents(t - 1, 0)
                if has(t, -2):
                    pk, _ = at(k, p, -2)
                    act.wait_ge(x2_turned, t - 1)
                    wait_for(act, lg_done, t - 2)
                    turned = yb[:, C:2 * C].rearrange("p (k n) -> p k n", k=KC)
                    act.activation(x2t[:, :, :], turned, ACT.Copy).then_inc(x2_copied, 1)
                    wait_for(act, x2_out[p], pk * 32)
                    act.activation(x2_h[:, p, :, :], turned, ACT.Copy).then_inc(x2_high, 1)
                if has(t, 0):
                    squares(t, 0)
                if has(t, -1):
                    exponents(t - 1, 1)
                if has(t, 0):
                    squares(t, 1)
                    squares(t, 2)
                if has(t, -1):
                    probs_high(t, 0)
                if has(t, -2):
                    act.wait_ge(lg_done, t - 1)
                    act.activation(logits[:, bass.ds(t - 2, 1), :], yb[:, 0:NE + 1].unsqueeze(1), ACT.Copy
                                   ).then_inc(lg_taken, 1)
                if has(t, 0):
                    squares(t, 3)
                if has(t, -1):
                    probs_high(t, 1)
                if has(t, 0):
                    squares(t, 4)
                for g in range(NKV):
                    if g == 2 and has(t, 1):
                        x_highs(t + 1)
                    if has(t, -1):
                        act.wait_ge(pv_done, t * 4 + (g - 3))
                        wait_for(act, y_done, t - 1)
                        act.activation(ot_h[:, GQ * g:GQ * g + GQ, :],
                                       work[:, g, :].rearrange("p (i n) -> p i n", i=GQ),
                                       ACT.Copy).then_inc(o_high, 1)
                if has(t, 0):
                    act.wait_ge(qk_turned, t * 5 + 1)
                    wait_for(act, s_done, t * 2)
                    act.activation(kt_h[:, :, :], turn[:, 0, :].rearrange("p (h n) -> p h n", h=NKV),
                                   ACT.Copy, scale=w_small[:, 7:8]).then_inc(qk_high, 1)
                    act.wait_ge(proj_taken, t * 6 + 6)
                    wait_for(act, pv_done, t * 4 - 4)
                    act.activation(v_own[:, p, 0, :], v32[:, :], ACT.Copy).then_inc(v_high, 1)
                    for j in range(4):
                        act.wait_ge(qk_turned, t * 5 + (j + 2))
                        act.activation(qt_h[:, 4 * j:4 * j + 4, :],
                                       turn[:, 1 - j % 2, :].rearrange("p (h n) -> p h n", h=4),
                                       ACT.Copy).then_inc(qk_high, 1)

            turns(step)(act)

        @block.vector
        def _(dve):
            def split_low(n):
                s, _ = raw_ready[n]
                view, high, low, _ = pieces[n]
                dve.wait_ge(raw_h, n + 1)
                dve.tensor_tensor(low, view(stage[s]), high, ALU.subtract).then_inc(raw_l, 1)

            def x_statistics(k, p, t):
                dve.wait_ge(x_in[p], k * 32 + 32)
                wait_for(dve, x_moments, t)
                dve.bn_stats(stats[:, :], xt[:, p, :]).then_inc(x_stats, 1)
                wait_for(dve, xn_ready, t)
                dve.wait_ge(x_stats, t * 2 + 1)
                dve.memset(spacer[:, 0:1], 0.0).then_inc(x_stats, 1)
                dve.bn_aggr(moments[:, :], stats[:, :]).then_inc(x_moments, 1)

            def x_normalise(k, p, t):
                dve.wait_ge(x_rstd, t + 1)
                wait_for(dve, x_turned, t)
                dve.tensor_scalar(xn[:, :], xt[:, p, :], moments[:, 0:1], rstd[:, 1:2],
                                  ALU.subtract, ALU.mult).then_inc(xn_ready, 1)

            def x_lows(t):
                dve.wait_ge(x_high, t + 1)
                dve.tensor_tensor(xc_l[:, :, :, :], turn[:, 1, :].rearrange("p (s k n) -> p s k n", s=2, k=KC),
                                  xc_h[:, :, :, :], ALU.subtract).then_inc(x_split, 1)

            def q_low(t, j):
                dve.wait_ge(qk_high, t * 5 + (j + 2))
                dve.tensor_tensor(qt_l[:, 4 * j:4 * j + 4, :],
                                  turn[:, 1 - j % 2, :].rearrange("p (h n) -> p h n", h=4),
                                  qt_h[:, 4 * j:4 * j + 4, :], ALU.subtract).then_inc(qk_split, 1)

            def add_bias(t, j):
                dve.wait_ge(proj_done, t * 6 + (j + 1))
                if j == 0:
                    wait_for(dve, qk_turned, t * 5)
                if j == 5:
                    wait_for(dve, v_split, t)
                col = QF if j == 0 else QF + KVF if j == 5 else (j - 1) * BANK
                dst = v32[:, :] if j == 5 else qk[:, col:col + BANK]
                dve.tensor_tensor(dst, work[:, bank_of[j], :], bias[:, col:col + BANK], ALU.add
                                  ).then_inc(proj_taken, 1)

            def sums(t, u):
                heads = slice(u * Q8, u * Q8 + Q8)
                dve.wait_ge(expd, t * 2 + (u + 1))
                dve.tensor_reduce(row_sum[:, heads], probs[:, heads, :], AX.X, ALU.add).then_inc(summed, 1)
                dve.wait_ge(summed, t * 2 + (u + 1))
                wait_for(dve, probs_ready, t * 2 + (u - 1))
                dve.reciprocal(row_inv[:, heads], row_sum[:, heads]).then_inc(inverted, 1)

            def take_scores(t, u):
                heads = slice(u * Q8, u * Q8 + Q8)
                pair = work[:, 2 * u:2 * u + 2, :].rearrange("p b (i n) -> p (b i) n", i=GQ)
                dve.wait_ge(s_done, t * 2 + (u + 1))
                wait_for(dve, p_turned, t * 2)
                for b in range(2):
                    rows, own = slice(b * SEQ, b * SEQ + SEQ), slice(b * SEQ, b * SEQ + SEQ)
                    dve.scalar_tensor_tensor(
                        probs[rows, heads, :], pair[rows, :, own], w_small[rows, 6:7],
                        mask[rows, :].unsqueeze(1).broadcast_to([SEQ, Q8, SEQ]), ALU.mult, ALU.add
                    ).then_inc(s_taken, 1)
                dve.wait_ge(s_taken, t * 4 + (2 * u + 2))
                dve.tensor_reduce(row_max[:, heads], probs[:, heads, :], AX.X, ALU.max).then_inc(max_done, 1)

            dve.memset(zeros[:, :], 0.0).then_inc(zeros_ready, 1)
            x_statistics(0, 0, 0)
            x_normalise(0, 0, 0)
            x_statistics(0, 1, 1)
            dve.wait_ge(consts_in, 16 * 10)
            dve.tensor_tensor(w_prod[:, :], norm_rows[:, 0, :], norm_rows[:, 1, :], ALU.mult).then_inc(w_step, 1)
            dve.tensor_tensor(w_small[:, 0:1], norm_cols[:, 0:1], norm_cols[:, 1:2], ALU.mult).then_inc(w_step, 1)
            dve.wait_ge(w_step, 2)
            dve.tensor_reduce(w_small[:, 1:2], w_prod[:, :], AX.X, ALU.max).then_inc(w_step, 1)
            dve.tensor_reduce(w_small[:, 2:3], w_prod[:, :], AX.X, ALU.min).then_inc(w_step, 1)
            dve.wait_ge(w_step, 4)
            dve.scalar_tensor_tensor(w_small[:, 3:4], w_small[:, 2:3], -1.0, w_small[:, 1:2],
                                     ALU.mult, ALU.max).then_inc(w_step, 1)
            dve.wait_ge(w_step, 5)
            dve.tensor_scalar(w_small[:, 4:5], w_small[:, 3:4], 1e-30, None, ALU.max).then_inc(w_step, 1)
            dve.wait_ge(w_step, 6)
            dve.reciprocal(w_small[:, 5:6], w_small[:, 4:5]).then_inc(w_step, 1)
            dve.tensor_scalar(w_small[:, 6:7], w_small[:, 4:5], float(np.float32(1.0) / np.sqrt(np.float32(HD))),
                              HD / QK_GAIN ** 2, ALU.mult, ALU.mult).then_inc(w_step, 1)
            dve.wait_ge(w_step, 8)
            dve.tensor_tensor(w_small[:, 7:8], w_small[:, 0:1], w_small[:, 5:6], ALU.mult).then_inc(w_step, 1)
            split_low(0)
            split_low(1)
            x_lows(0)
            dve.wait_ge(bias_in, 48)
            for n in range(2, len(pieces)):
                split_low(n)
            dve.wait_ge(w_step, 9)
            dve.wait_ge(gates_done, 1)
            dve.wait_ge(raw_l, len(pieces) - 1)

            def step(k, p, t):
                pk, pp = at(k, p, -1)
                nk, np_ = at(k, p, 1)
                if has(t, 0):
                    add_bias(t, 0)
                if has(t, -2):
                    dve.wait_ge(x2_high, t - 1)
                    dve.tensor_tensor(x2_l[:, p, :, :], yb[:, C:2 * C].rearrange("p (k n) -> p k n", k=KC),
                                      x2_h[:, p, :, :], ALU.subtract).then_inc(x2_split, 1)
                if has(t, 0):
                    add_bias(t, 1)
                if has(t, -1):
                    sums(t - 1, 0)
                if has(t, 0):
                    add_bias(t, 2)
                if has(t, -1):
                    sums(t - 1, 1)
                if has(t, 0):
                    add_bias(t, 3)
                for u in range(2):
                    if u == 0 and has(t, 0):
                        add_bias(t, 4)
                    if has(t, -1):
                        dve.wait_ge(p_high, t * 2 + (u - 1))
                        dve.tensor_tensor(pt_l[:, u, :, :], turn[:, 1 - u, :].rearrange("p (i n) -> p i n", i=GQ),
                                          pt_h[:, u, :, :], ALU.subtract).then_inc(p_split, 1)
                    if u == 0 and has(t, 1):
                        x_normalise(nk, np_, t + 1)
                    if u == 0 and has(t, 0):
                        add_bias(t, 5)
                if has(t, 2):
                    x_statistics(k + 1, p, t + 2)
                for g in range(NKV):
                    if g == 2 and has(t, 1):
                        x_lows(t + 1)
                    if has(t, -1):
                        heads = slice(GQ * g, GQ * g + GQ)
                        dve.wait_ge(o_high, t * 4 + (g - 3))
                        dve.tensor_tensor(ot_l[:, heads, :], work[:, g, :].rearrange("p (i n) -> p i n", i=GQ),
                                          ot_h[:, heads, :], ALU.subtract).then_inc(o_split, 1)
                if has(t, 0):
                    dve.wait_ge(qk_high, t * 5 + 1)
                    dve.scalar_tensor_tensor(kt_l[:, :, :], turn[:, 0, :].rearrange("p (h n) -> p h n", h=NKV),
                                             w_small[:, 7:8], kt_h[:, :, :], ALU.mult, ALU.subtract
                                             ).then_inc(qk_split, 1)
                    q_low(t, 0)
                    q_low(t, 1)
                if has(t, -1):
                    dve.wait_ge(y_done, t)
                    dve.wait_ge(xr_in[pp], pk * 16 + 16)
                    wait_for(dve, x1_out[pp], pk * 32)
                    dve.scalar_tensor_tensor(x1[:, pp, :], yb[:, 0:C], tanh_g[:, 0:1], xr[:, pp, :],
                                             ALU.mult, ALU.add).then_inc(x1_ready, 1)
                if has(t, 0):
                    q_low(t, 2)
                    q_low(t, 3)
                if has(t, -1):
                    dve.wait_ge(x1_ready, t)
                    wait_for(dve, x2_moments, t - 1)
                    dve.bn_stats(stats2[:, :], x1[:, pp, :]).then_inc(x2_stats, 1)
                    wait_for(dve, xn2_ready, t - 1)
                    dve.wait_ge(x2_stats, t * 2 - 1)
                    dve.memset(spacer[:, 1:2], 0.0).then_inc(x2_stats, 1)
                    dve.bn_aggr(moments2[:, :], stats2[:, :]).then_inc(x2_moments, 1)
                    if has(t, 0):
                        take_scores(t, 0)
                    dve.wait_ge(x2_rstd, t)
                    wait_for(dve, x2_turned, t - 1)
                    dve.tensor_scalar(xn2[:, pp, :], x1[:, pp, :], moments2[:, 0:1], rstd2[:, 1:2],
                                      ALU.subtract, ALU.mult).then_inc(xn2_ready, 1)
                if has(t, 0):
                    if not has(t, -1):
                        take_scores(t, 0)
                    take_scores(t, 1)

            turns(step)(dve)

        @block.tensor
        def _(pe):
            def turn_tile(p, t):
                pe.wait_ge(xn_ready, t + 1)
                for s, src in enumerate((xn[:, :], ct[:, p, :])):
                    for kc in range(KC):
                        at_ = (s * KC + kc) * P
                        ins_ = pe.transpose(turn[:, 1, at_:at_ + P], src[:, kc * P:kc * P + P], ident[:, :])
                ins_.then_inc(x_turned, 1)

            def project(t, j):
                if j == 0:
                    pe.wait_ge(x_split, t + 1)
                    wait_for(pe, proj_taken, t * 6)
                if j == 1:
                    wait_for(pe, s_taken, t * 4 - 2)
                if j == 3:
                    wait_for(pe, s_taken, t * 4)
                if j == 5:
                    pe.wait_ge(proj_taken, t * 6 + 1)
                if isinstance(t, int) and t == 0:
                    pe.wait_ge(raw_l, 1 if j in (0, 5) else WO_FIRST)
                src = 1 if j in (0, 5) else 0
                w_h, w_l = (wkv_h, wkv_l) if j in (0, 5) else (wq_h, wq_l)
                col = {0: 0, 5: KVF}.get(j, (j - 1) * BANK)
                for kc in range(KC):
                    ins_ = three_products(pe, work[:, bank_of[j], :], xc_h[:, src, kc, :], xc_l[:, src, kc, :],
                                          w_h[:, kc, col:col + BANK], w_l[:, kc, col:col + BANK],
                                          kc == 0, kc == KC - 1)
                ins_.then_inc(proj_done, 1)

            def turn_heads(j):
                col = QF if j == 0 else (j - 1) * BANK
                bank = j % 2
                for i in range(4):
                    ins_ = pe.transpose(turn[:, bank, i * P:i * P + P], qk[:, col + i * HD:col + (i + 1) * HD],
                                        ident[:, :])
                ins_.then_inc(qk_turned, 1)

            def scores(t, u):
                for place in range(Q8):
                    g, i = 2 * u + place % 2, place // 2
                    h, at_ = g * GQ + i, (place % 4) * P
                    ins_ = three_products(pe, work[:, 2 * u + place // 4, at_:at_ + P], qt_h[:, h, :], qt_l[:, h, :],
                                          kt_h[:, g, :], kt_l[:, g, :], True, True)
                ins_.then_inc(s_done, 1)

            def weighted_values(p, g):
                u, slot = g // 2, g % 2
                rows = slice(slot * SEQ, slot * SEQ + SEQ)
                bank = work[:, g, :].rearrange("p (i n) -> p i n", i=GQ)
                for b in range(2):
                    v = v_own if b == slot else v_other
                    cols = slice(b * SEQ, b * SEQ + SEQ)
                    ins_ = three_products(
                        pe, bank[:, :, cols], v[rows, p, 0, g * HD:(g + 1) * HD], v[rows, p, 1, g * HD:(g + 1) * HD],
                        pt_h[rows, u, :, cols], pt_l[rows, u, :, cols], True, True)
                ins_.then_inc(pv_done, 1)

            pe.wait_ge(ident_done, 1)
            turn_tile(0, 0)
            pe.wait_ge(consts_in, 16 * 10)
            for kc in range(KC):
                ins_ = pe.transpose(yb[:, kc * (NE + 1):(kc + 1) * (NE + 1)], gate_rows[:, kc * P:kc * P + P],
                                    ident[0:NE + 1, 0:NE + 1])
            ins_.then_inc(gate_turned, 1)

            def turn_probs(t, u):
                pe.wait_ge(qk_split, t * 5 + (u + 4))
                pe.wait_ge(probs_ready, t * 2 + (u + 1))
                for i in range(GQ):
                    two = probs[:, u * Q8 + 2 * i:u * Q8 + 2 * i + 2, :].rearrange("p s e -> p (s e)")
                    ins_ = pe.transpose(turn[:, 1 - u, i * P:i * P + P], two, ident[:, :])
                ins_.then_inc(p_turned, 1)

            def output_heads(t, g):
                pe.wait_ge(o_split, t * 4 + (g + 1))
                for h in range(g * GQ, g * GQ + GQ):
                    ins_ = three_products(pe, yb[:, 0:C], ot_h[:, h, :], ot_l[:, h, :], wo_h[:, h, :],
                                          wo_l[:, h, :], h == 0, h == NH - 1)
                if g == NKV - 1:
                    ins_.then_inc(y_done, 1)

            def turn_qk(t, j):
                if j == 1:
                    if has(t, 1):
                        pe.wait_ge(x_split, t + 2)
                if j > 1:
                    pe.wait_ge(qk_split, t * 5 + (j - 1))
                pe.wait_ge(normed, t * 5 + (j + 1))
                turn_heads(j)

            def step(k, p, t):
                pk, pp = at(k, p, -1)
                nk, np_ = at(k, p, 1)
                for j in range(6):
                    if j == 5 and has(t, -1):
                        turn_probs(t - 1, 0)
                    if has(t, 0):
                        project(t, j)
                    if j == 0 and has(t, -2):
                        pe.wait_ge(xn2_ready, t - 1)
                        for kc in range(KC):
                            ins_ = pe.transpose(yb[:, C + kc * P:C + kc * P + P], xn2[:, p, kc * P:kc * P + P], ident[:, :])
                        ins_.then_inc(x2_turned, 1)
                    if j == 4 and has(t, -2):
                        pe.wait_ge(x2_split, t - 1)
                        for kc in range(KC):
                            ins_ = pe.matmul(yb[:, 0:NE + 1], x2t[:, kc, :], gate_t[:, kc, :],
                                             start=(kc == 0), stop=(kc == KC - 1))
                        ins_.then_inc(lg_done, 1)
                if has(t, -1):
                    turn_probs(t - 1, 1)
                    pe.wait_ge(v_swapped[pp], pk * 32 + 32)
                for g in range(NKV):
                    if g == 2 and has(t, 1):
                        if not has(t, -1):
                            pe.wait_ge(x_split, 1)
                        turn_tile(np_, t + 1)
                    if has(t, -1):
                        if g % 2 == 0:
                            pe.wait_ge(p_split, t * 2 + (g // 2 - 1))
                        if has(t, 0):
                            pe.wait_ge(proj_taken, t * 6 + (g + 2))
                        elif g == 0:
                            pe.wait_ge(s_taken, t * 4)
                        weighted_values(pp, g)
                if has(t, -1):
                    if isinstance(t, int) and t == 1:
                        pe.wait_ge(raw_l, len(pieces))
                        pe.wait_ge(gate_split, 1)
                    wait_for(pe, lg_taken, t - 1)
                for g in range(NKV):
                    if has(t, 0):
                        turn_qk(t, g)
                    if has(t, -1):
                        output_heads(t - 1, g)
                if has(t, 0):
                    turn_qk(t, 4)
                    pe.wait_ge(qk_split, t * 5 + 3)
                    scores(t, 0)
                    pe.wait_ge(qk_split, t * 5 + 5)
                    scores(t, 1)

            turns(step)(pe)


def ffn_pass(nc, ins, kept, scratch, out):
    T = kept["logits"].shape[1]
    NG = T // GT
    x1_dram, x2h_dram, x2l_dram = scratch["x1"], scratch["x2h"], scratch["x2l"]
    x2_dram, sorted_x, sorted_y, part_dram = scratch["x2"], scratch["sorted_x"], scratch["sorted_y"], scratch["part"]
    out_tok = out.rearrange("b s c -> (b s) c")
    ident, logits, tanh_g = kept["ident"], kept["logits"], kept["tanh_g"]
    NB = sorted_x.shape[0] // P
    FA, FB = P, F_MOE - P
    F2 = 2 * F_MOE
    BEFORE = NG - 3
    UNROLL = 4
    LAG = 3

    with ExitStack() as es:
        def sb(name, shape, dt=F32):
            return es.enter_context(nc.sbuf_tensor(name, shape, dt))

        def sem(name):
            return es.enter_context(nc.semaphore(name))

        w12_h, w12_l = sb("w12_h", [P, SH_CHUNKS, 2 * KC, P], F32R), sb("w12_l", [P, SH_CHUNKS, 2 * KC, P], F32R)
        wp_h, wp_l = sb("wp_h", [P, SH_CHUNKS, C], F32R), sb("wp_l", [P, SH_CHUNKS, C], F32R)
        EX_FC, EX_P = KC * NE * F2, 2 * NE * C
        ex_all = sb("ex_all", [P, 2 * EX_FC + 2 * EX_P], F32R)
        e12_h = ex_all[:, 0:EX_FC].rearrange("p (k n) -> p k n", k=KC)
        e12_l = ex_all[:, EX_FC:2 * EX_FC].rearrange("p (k n) -> p k n", k=KC)
        ep_h = ex_all[:, 2 * EX_FC:2 * EX_FC + EX_P].rearrange("p (s n) -> p s n", s=2)
        ep_l = ex_all[:, 2 * EX_FC + EX_P:].rearrange("p (s n) -> p s n", s=2)
        picked = ex_all[:, 0:T * 2 * C].bitcast(F32).rearrange("p (t s c) -> p t s c", t=T, s=2)
        RAW = 4
        raw_fc = sb("raw_fc", [P, RAW, 2, C])
        raw_ex = raw_fc[:, :, :, :].rearrange("p (r s) f c -> p r s f c", s=2)
        raw_p = sb("raw_p", [P, KC * (F_SHARED + NE * F_MOE)])
        raw_sp = raw_p[:, 0:KC * F_SHARED].rearrange("p (k f) -> p k f", k=KC)
        raw_ep = raw_p[:, KC * F_SHARED:].rearrange("p (k f) -> p k f", k=KC)
        small = [P, T, NE]
        prob, hit, pick1, pick2, left, place = (sb(n, small) for n in ("prob", "hit", "pick1", "pick2", "left", "place"))
        before = [sb(f"before{i}", [P, T // 2 + T, NE]) for i in range(2)]
        blocks = [sb(f"blocks{i}", [P, NE // 2 + NE]) for i in range(2)]
        block_hit = sb("block_hit", [P, NE, T])
        col = {n: sb(f"col_{n}", [P, T]) for n in ("max", "sum", "inv", "top1", "top2", "place", "sig", "sinv")}
        sgate = sb("sgate", [P, T])
        gain = sb("gain", [P, 2, T])
        slot_f = sb("slot_f", [P, 2, T])
        slot = sb("slot", [P, 2, T], U32)
        n_blocks, start_row = sb("n_blocks", [P, NE]), sb("start_row", [P, NE])
        of_block = sb("of_block", [P, NB, NE - 1])
        expert_f = sb("expert_f", [P, NB])
        expert = sb("expert", [P, LAG + NB + UNROLL], I32)
        below, ones = sb("below", [P, P]), sb("ones", [P, P])
        row_steps, block_no = sb("row_steps", [P, T]), sb("block_no", [P, NB])
        xg_h, xg_l = sb("xg_h", [P, 2, KC, GROUP], F32R), sb("xg_l", [P, 2, KC, GROUP], F32R)
        xy = sb("xy", [P, 2, GT, C])
        act_s = sb("act_s", [P, 2, GROUP])
        hid = sb("hid", [P, 2, GROUP])
        hid_h, hid_l = sb("hid_h", [P, 2, GROUP], F32R), sb("hid_l", [P, 2, GROUP], F32R)
        XR = 3
        xrow = sb("xrow", [P, XR, C])
        xb = raw_p[:, 0:UNROLL * C].rearrange("p (b c) -> p b c", b=UNROLL)
        yb_sb = raw_p[:, UNROLL * C:2 * UNROLL * C].rearrange("p (b c) -> p b c", b=UNROLL)
        silu_b = raw_p[:, 2 * UNROLL * C:2 * UNROLL * C + 2 * F_MOE].rearrange("p (b c) -> p b c", b=2)
        xbt_h, xbt_l = sb("xbt_h", [P, 2, C], F32R), sb("xbt_l", [P, 2, C], F32R)
        hb_tok = sb("hb_tok", [P, 2, 2 * P])
        ht_h, ht_l = sb("ht_h", [P, 2, 2 * P], F32R), sb("ht_l", [P, 2, 2 * P], F32R)

        ps = es.enter_context(nc.psum_tensor("ps", [P, 8, BANK], F32))
        ACC, PREP = 4, 6

        fc_in = [sem(f"fc_in{i}") for i in range(RAW)]
        ex_in = [sem(f"ex_in{i}") for i in range(2)]
        proj_in = sem("proj_in")
        zeroed, consts_made = sem("zeroed"), sem("consts_made")
        prep_turned, prep_high, prep_low = sem("prep_turned"), sem("prep_high"), sem("prep_low")
        ex_turned, ex_high, ex_low = sem("ex_turned"), sem("ex_high"), sem("ex_low")
        route = sem("route")
        route_exp, gate_exp = sem("route_exp"), sem("gate_exp")
        hits_ready, counted = sem("hits_ready"), sem("counted")
        slots_ready, experts_ready = sem("slots_ready"), sem("experts_ready")
        xrow_in = [sem(f"xrow_in{i}") for i in range(XR)]
        xrow_out = [sem(f"xrow_out{i}") for i in range(XR)]
        xg_in = [sem(f"xg_in{i}") for i in range(2)]
        xy_in = [sem(f"xy_in{i}") for i in range(2)]
        xy_out = [sem(f"xy_out{i}") for i in range(2)]
        h1_done, h2_done = sem("h1_done"), sem("h2_done")
        silu_done, h_done = sem("silu_done"), sem("h_done")
        hid_high, hid_low = sem("hid_high"), sem("hid_low")
        h_through = sem("h_through")
        sh_taken = sem("sh_taken")
        finished, finish_step = sem("finished"), sem("finish_step")
        xb_in = [sem(f"xb_in{i}") for i in range(2)]
        xb_turned, xb_high, xb_low = sem("xb_turned"), sem("xb_high"), sem("xb_low")
        up_done, b_silu, b_hidden = sem("up_done"), sem("b_silu"), sem("b_hidden")
        b_turned, b_high, b_low = sem("b_turned"), sem("b_high"), sem("b_low")
        b_done, b_taken = sem("b_done"), sem("b_taken")
        b_out = [sem(f"b_out{i}") for i in range(2)]
        y_in = [sem(f"y_in{i}") for i in range(NG)]

        prep = [("fc", c) for c in range(SH_CHUNKS)]
        prep += [("proj", (c, c + 1)) for c in range(0, SH_CHUNKS, 2)]
        ex_prep = [(e, kind) for e in range(NE) for kind in range(KC + 1)]
        join_at = {(NG - 2, 1): NG - 3, (NG - 2, 2): 0, (NG - 2, 4): 1,
                   (NG - 1, 1): NG - 2, (NG - 1, 2): 2, (NG - 1, 4): 3, (NG - 1, 5): 4}
        order = [join_at[at] for at in sorted(join_at)] + [NG - 1]
        jobs = [(n, x1_dram, part_dram) for n in range(BEFORE)]
        jobs += [(n, x1_dram if n >= BEFORE else part_dram, out_tok) for n in order]
        job_of = {n: BEFORE + i for i, n in enumerate(order)}

        def rows_of(c):
            return SH_TAIL if c == SH_CHUNKS - 1 else P

        def prep_views(n, low):
            kind, c = prep[n]
            bank = ps[:, n % 4, :]
            if kind == "fc":
                dst = (w12_h, w12_l)[low]
                r = rows_of(c)
                return [(bank.rearrange("p (m f) -> p m f", m=2 * KC)[:, :, 0:r], dst[:, c, :, 0:r])]
            dst = (wp_h, wp_l)[low]
            return [(bank[0:rows_of(m), i * C:(i + 1) * C], dst[0:rows_of(m), m, :]) for i, m in enumerate(c)]

        def ex_views(m, low):
            e, kind = ex_prep[m]
            bank = ps[:, PREP + m % 2, :]
            if kind < KC:
                return [(bank[:, 0:F2], (e12_h, e12_l)[low][:, kind, e * F2:(e + 1) * F2])]
            dst = (ep_h, ep_l)[low]
            return [(bank[0:r, s * C:(s + 1) * C], dst[0:r, s, e * C:(e + 1) * C]) for s, r in ((0, FA), (1, FB))]

        def block_steps(step):
            def run(eng):
                for s in range(2 * UNROLL):
                    step(s // UNROLL, s % UNROLL, s)
                with eng.Fori(2, NB // UNROLL) as k:
                    for q in range(UNROLL):
                        step(k, q, k * UNROLL + q)
                for s in range(NB, NB + 3):
                    step(s // UNROLL, s % UNROLL, s)
            return run

        def there(s, lag):
            return not isinstance(s, int) or 0 <= s - lag < NB

        def at(k, q, lag):
            return k + (q - lag) // UNROLL, (q - lag) % UNROLL

        block = es.enter_context(nc.Block())

        @block.sync
        def _(sp):
            def load_tokens(n):
                cols = slice(n * GROUP, (n + 1) * GROUP)
                if n >= 2:
                    sp.wait_ge(h2_done, (n - 1) * SH_CHUNKS)
                for dst, src in ((xg_h, x2h_dram), (xg_l, x2l_dram)):
                    sp.dma_start(dst[:, n % 2, :, :].bitcast(F32), src[:, :, cols].rearrange("k p n -> p k n")
                                 ).then_inc(xg_in[n % 2], 16)

            def load_job(j):
                n, src, _ = jobs[j]
                if j >= 2:
                    sp.wait_ge(xy_out[j % 2], j // 2 * 16)
                if src is part_dram:
                    sp.wait_ge(xy_out[n % 2], (n // 2 + 1) * 16)
                sp.dma_start(xy[:, j % 2, :, :], src[n * GROUP:(n + 1) * GROUP, :].rearrange(
                    "(j p) c -> p j c", p=P)).then_inc(xy_in[j % 2], 16)

            def store_job(j):
                n, _, dst = jobs[j]
                if j < BEFORE:
                    sp.wait_ge(sh_taken, (j + 1) * GT)
                else:
                    sp.wait_ge(finished, j - BEFORE + 1)
                sp.dma_start(dst[n * GROUP:(n + 1) * GROUP, :].rearrange("(j p) c -> p j c", p=P),
                             xy[:, j % 2, :, :]).then_inc(xy_out[j % 2], 16)

            def load_fc(c):
                if c >= RAW:
                    sp.wait_ge(prep_turned, c - RAW + 1)
                for f, w in enumerate((ins["shared_fc1"], ins["shared_fc2"])):
                    sp.dma_start(raw_fc[0:rows_of(c), c % RAW, f, :], w[c * P:c * P + rows_of(c), :]
                                 ).then_inc(fc_in[c % RAW], 16)

            def load_expert(e):
                sp.wait_ge(prep_turned, SH_CHUNKS)
                if e >= 2:
                    sp.wait_ge(ex_turned, (e - 2) * (KC + 1) + KC)
                for f, w in enumerate((ins["expert_fc1"], ins["expert_fc2"])):
                    sp.dma_start(raw_ex[:, e % 2, 0, f, :], w[e, 0:FA, :]).then_inc(ex_in[e % 2], 16)
                    sp.dma_start(raw_ex[0:FB, e % 2, 1, f, :], w[e, FA:F_MOE, :]).then_inc(ex_in[e % 2], 16)

            def load_rows(t):
                if t >= XR:
                    sp.wait_ge(xrow_out[t % XR], t // XR * 32)
                sp.dma_start(xrow[:, t % XR, :], x2_dram[t * P:(t + 1) * P, :]).then_inc(xrow_in[t % XR], 16)

            for c in range(RAW):
                load_fc(c)
            sp.dma_start(raw_sp, ins["shared_proj"].rearrange("(k p) f -> p k f", p=P)).then_inc(proj_in, 16)
            for c in range(RAW, SH_CHUNKS):
                load_fc(c)
            load_tokens(0)
            load_job(0)
            for t in range(XR):
                load_rows(t)
            load_expert(0)
            load_expert(1)
            for kc in range(KC):
                sp.dma_start(raw_ep[:, kc, :].rearrange("p (e f) -> p e f", e=NE),
                             ins["expert_proj"][:, kc * P:(kc + 1) * P, :].rearrange("e p f -> p e f")
                             ).then_inc(proj_in, 16)
            load_tokens(1)
            load_job(1)
            for n in range(BEFORE):
                if n < BEFORE - 1:
                    per = -(-(T - XR) // (BEFORE - 1))
                    tiles = range(XR + n * per, min(T, XR + (n + 1) * per))
                    for i, t in enumerate(tiles):
                        load_rows(t)
                        if i in (2, 5) and 2 + 2 * n + i // 3 < NE:
                            load_expert(2 + 2 * n + i // 3)
                store_job(n)
                if n + 2 < BEFORE + 1:
                    load_job(n + 2)
                if n + 2 < NG:
                    load_tokens(n + 2)

            for i in range(XR):
                sp.wait_ge(xrow_out[i], len(range(i, T, XR)) * 32)

            def load_pair(row, half):
                sp.dma_start(xb[:, 2 * half:2 * half + 2, :], sorted_x[bass.ds(row, 2 * P), :].rearrange(
                    "(b p) c -> p b c", p=P)).then_inc(xb_in[half], 16)

            sp.wait_ge(ex_turned, len(ex_prep))
            for half in range(2):
                load_pair(half * 2 * P, half)

            def step(k, q, s):
                if s % 2 == 1 if isinstance(s, int) else q % 2 == 1:
                    more = s + UNROLL < NB if isinstance(s, int) else True
                    if more:
                        wait_for(sp, xb_turned, s + 1)
                        load_pair(s * P + (UNROLL - 1) * P, q // 2)
                elif there(s, 3) and there(s, 4):
                    _, qy = at(k, q, 4)
                    sp.wait_ge(b_taken, s - 2)
                    sp.dma_start(sorted_y[bass.ds(s * P - 4 * P, 2 * P), :].rearrange("(b p) c -> p b c", p=P),
                                 yb_sb[:, qy:qy + 2, :]).then_inc(b_out[qy // 2], 16)

            def block_loop(eng):
                for s in range(2 * UNROLL):
                    step(s // UNROLL, s % UNROLL, s)
                with eng.Fori(2, NB // UNROLL - 1) as k:
                    for q in range(UNROLL):
                        step(k, q, k * UNROLL + q)
                for s in range(NB - UNROLL, NB + 4):
                    step(s // UNROLL, s % UNROLL, s)

            block_loop(sp)
            load_job(BEFORE + 1)
            for j in range(BEFORE, len(jobs)):
                store_job(j)
                if j + 2 < len(jobs):
                    load_job(j + 2)
                if j == BEFORE:
                    load_tokens(NG - 1)
            for i in range(2):
                sp.wait_ge(xy_out[i], len(range(i, len(jobs), 2)) * 16)

        @block.gpsimd
        def _(pool):
            pool.iota(row_steps[:, :], pattern=[[P, T]], base=0, channel_multiplier=0,
                      allow_small_or_imprecise_dtypes=True).then_inc(consts_made, 1)
            pool.wait_ge(consts_made, 1)
            pool.iota(block_no[:, :], pattern=[[1, NB]], base=0, channel_multiplier=0,
                      allow_small_or_imprecise_dtypes=True).then_inc(consts_made, 1)
            pool.wait_ge(consts_made, 2)
            pool.memset(ones[:, :], 1.0).then_inc(consts_made, 1)
            pool.wait_ge(consts_made, 3)
            pool.affine_select(out=below[:, :], in_=ones[:, :], compare_op=ALU.is_gt, fill=0.0,
                               base=0, pattern=[[1, P]], channel_multiplier=-1).then_inc(consts_made, 1)
            pool.wait_ge(slots_ready, 1)
            for t in range(T):
                pool.wait_ge(xrow_in[t % XR], (t // XR + 1) * 16)
                for s in range(2):
                    pool.indirect_dma_start(sorted_x, bass.IndirectOffsetOnAxis(ap=slot[:, s, t:t + 1], axis=0),
                                            xrow[:, t % XR, :], None).then_inc(xrow_out[t % XR], 16)
            for i in range(2):
                pool.wait_ge(b_out[i], NB // UNROLL * 16)
            pool.wait_ge(b_done, NB)
            for n in order:
                for t in range(n * GT, (n + 1) * GT):
                    for s in range(2):
                        pool.indirect_dma_start(picked[:, t, s, :], None, sorted_y,
                                                bass.IndirectOffsetOnAxis(ap=slot[:, s, t:t + 1], axis=0)
                                                ).then_inc(y_in[n], 16)

        @block.scalar
        def _(act):
            act.wait_ge(route, 2)
            act.activation(prob[:, :, :], prob[:, :, :], ACT.Exp).then_inc(route_exp, 1)
            act.activation(col["sig"][:, :].unsqueeze(2), logits[:, :, NE:NE + 1], ACT.Exp, scale=-1.0
                           ).then_inc(gate_exp, 1)
            for n in range(len(prep)):
                act.wait_ge(prep_turned, n + 1)
                for src, dst in prep_views(n, 0):
                    ins_ = act.activation(dst, src, ACT.Copy)
                ins_.then_inc(prep_high, 1)

            def high(n, c):
                act.wait_ge(h_done, n * SH_CHUNKS + c + 1)
                wait_for(act, h_through, n * SH_CHUNKS + c - 1)
                act.activation(hid_h[:, c % 2, :], hid[:, c % 2, :], ACT.Copy).then_inc(hid_high, 1)

            def group(n):
                for c in range(SH_CHUNKS):
                    m = n * SH_CHUNKS + c
                    act.wait_ge(h1_done, m + 1)
                    wait_for(act, h_done, m - 1)
                    act.activation(act_s[:, c % 2, :], ps[:, 2 * (c % 2), :], ACT.Silu).then_inc(silu_done, 1)
                    if m < len(ex_prep):
                        act.wait_ge(ex_turned, m + 1)
                        for src, dst in ex_views(m, 0):
                            ins_ = act.activation(dst, src, ACT.Copy)
                        ins_.then_inc(ex_high, 1)
                    if c > 0:
                        high(n, c - 1)
                high(n, SH_CHUNKS - 1)

            for n in range(BEFORE):
                group(n)

            def step(k, q, s):
                if there(s, 0):
                    act.wait_ge(xb_turned, s + 1)
                    wait_for(act, up_done, s - 1)
                    act.activation(xbt_h[:, q % 2, :], ps[:, q % 2, 0:C], ACT.Copy).then_inc(xb_high, 1)
                if there(s, 1):
                    r = (q + 1) % 2
                    act.wait_ge(up_done, s)
                    wait_for(act, b_hidden, s - 2)
                    act.activation(silu_b[:, r, :], ps[:, 2 + r, 0:F_MOE], ACT.Silu).then_inc(b_silu, 1)
                if there(s, 2):
                    act.wait_ge(b_turned, s - 1)
                    wait_for(act, b_done, s - 3)
                    act.activation(ht_h[:, q % 2, :], ps[:, 4 + q % 2, 0:2 * P], ACT.Copy).then_inc(b_high, 1)
                if there(s, 3):
                    ky, qy = at(k, q, 3)
                    act.wait_ge(b_done, s - 2)
                    wait_for(act, b_out[qy // 2], ky * 16)
                    act.activation(yb_sb[:, qy, :], ps[:, 6 + qy % 2, 0:C], ACT.Copy).then_inc(b_taken, 1)

            block_steps(step)(act)
            for n in range(BEFORE, NG):
                group(n)

        @block.vector
        def _(dve):
            chain = 0

            def link(ins_):
                nonlocal chain
                chain += 1
                ins_.then_inc(route, 1)
                dve.wait_ge(route, chain)

            c = SH_CHUNKS - 1
            zeros = [w[:, c, :, SH_TAIL:P].bitcast(F32) for w in (w12_h, w12_l)]
            zeros += [w[SH_TAIL:P, c, :].bitcast(F32) for w in (wp_h, wp_l)]
            zeros += [w[32:64, 1, :].bitcast(F32) for w in (ep_h, ep_l)]
            zeros += [w[64:P, 1, :].bitcast(F32) for w in (ep_h, ep_l)]
            zeros += [hb_tok[:, :, F_MOE:2 * P]]
            zeros += [b[:, 0:T // 2, :] for b in before] + [b[:, 0:NE // 2] for b in blocks]
            zeros += [expert[:, 0:LAG].bitcast(F32), expert[:, LAG + NB:].bitcast(F32)]
            for z in zeros:
                dve.memset(z, 0.0).then_inc(zeroed, 1)
            for e in range(NE):
                dve.memset(kept["rank"][:, e:e + 1], float(NE - e)).then_inc(zeroed, 1)
            n_zeroed = len(zeros) + NE

            wide = lambda t: t.unsqueeze(2).broadcast_to([P, T, NE])
            rank = kept["rank"][:, :].unsqueeze(1).broadcast_to([P, T, NE])
            expert_logits = logits[:, :, 0:NE]
            link(dve.tensor_reduce(col["max"][:, :], expert_logits, AX.X, ALU.max))
            link(dve.tensor_tensor(prob[:, :, :], expert_logits, wide(col["max"][:, :]), ALU.subtract))
            dve.wait_ge(route_exp, 1)
            link(dve.tensor_reduce(col["sum"][:, :], prob[:, :, :], AX.X, ALU.add))
            link(dve.reciprocal(col["inv"][:, :], col["sum"][:, :]))
            link(dve.tensor_tensor(prob[:, :, :], prob[:, :, :], wide(col["inv"][:, :]), ALU.mult))
            dve.wait_ge(zeroed, n_zeroed)
            for pick, values, top in ((pick1, prob, col["top1"]), (pick2, left, col["top2"])):
                link(dve.tensor_reduce(top[:, :], values[:, :, :], AX.X, ALU.max))
                link(dve.tensor_tensor(hit[:, :, :], values[:, :, :], wide(top[:, :]), ALU.is_equal))
                link(dve.tensor_tensor(hit[:, :, :], hit[:, :, :], rank, ALU.mult))
                link(dve.tensor_reduce(col["place"][:, :], hit[:, :, :], AX.X, ALU.max))
                link(dve.tensor_tensor(pick[:, :, :], hit[:, :, :], wide(col["place"][:, :]), ALU.is_equal))
                if pick is pick1:
                    link(dve.scalar_tensor_tensor(left[:, :, :], pick1[:, :, :], -2.0, prob[:, :, :],
                                                  ALU.mult, ALU.add))
            dve.tensor_tensor(hit[:, :, :], pick1[:, :, :], pick2[:, :, :], ALU.add).then_inc(hits_ready, 1)
            for s, top in enumerate((col["top1"], col["top2"])):
                link(dve.tensor_scalar(gain[:, s, :], top[:, :], tanh_g[:, 1:2], None, ALU.mult))
            dve.wait_ge(gate_exp, 1)
            link(dve.tensor_scalar(col["sinv"][:, :], col["sig"][:, :], 1.0, None, ALU.add))
            link(dve.reciprocal(col["sig"][:, :], col["sinv"][:, :]))
            link(dve.tensor_scalar(sgate[:, :], col["sig"][:, :], tanh_g[:, 1:2], None, ALU.mult))

            for n in range(len(prep)):
                dve.wait_ge(prep_high, n + 1)
                for (src, low), (_, high) in zip(prep_views(n, 1), prep_views(n, 0)):
                    ins_ = dve.tensor_tensor(low, src, high, ALU.subtract)
                ins_.then_inc(prep_low, 1)

            dve.wait_ge(counted, 1)
            own = ps[:, PREP, 0:T * NE].rearrange("p (t e) -> p t e", e=NE)
            under = ps[:, PREP + 1, 0:T * NE].rearrange("p (t e) -> p t e", e=NE)
            link(dve.tensor_copy(before[0][:, T // 2:, :], own))
            reach, i = 1, 0
            while reach < T:
                a = before[i]
                link(dve.tensor_tensor(before[1 - i][:, T // 2:, :], a[:, T // 2:, :],
                                       a[:, T // 2 - reach:T // 2 - reach + T, :], ALU.add))
                reach, i = reach * 2, 1 - i
            upto = before[i]
            total = upto[:, T // 2 + T - 1, :]
            link(dve.tensor_tensor(block_hit[:, :, :], total.unsqueeze(2).broadcast_to([P, NE, T]),
                                   row_steps[:, :].unsqueeze(1).broadcast_to([P, NE, T]), ALU.is_gt))
            link(dve.tensor_reduce(n_blocks[:, :], block_hit[:, :, :], AX.X, ALU.add))
            link(dve.tensor_copy(blocks[0][:, NE // 2:], n_blocks[:, :]))
            reach, i = 1, 0
            while reach < NE:
                a = blocks[i]
                link(dve.tensor_tensor(blocks[1 - i][:, NE // 2:], a[:, NE // 2:],
                                       a[:, NE // 2 - reach:NE // 2 - reach + NE], ALU.add))
                reach, i = reach * 2, 1 - i
            ends = blocks[i][:, NE // 2:]
            link(dve.tensor_tensor(start_row[:, :], ends, n_blocks[:, :], ALU.subtract))
            link(dve.tensor_scalar(start_row[:, :], start_row[:, :], float(P), None, ALU.mult))
            link(dve.tensor_tensor(place[:, :, :], upto[:, T // 2:, :], own, ALU.subtract))
            link(dve.tensor_tensor(place[:, :, :], place[:, :, :], under, ALU.add))
            link(dve.tensor_tensor(place[:, :, :], place[:, :, :],
                                   start_row[:, :].unsqueeze(1).broadcast_to([P, T, NE]), ALU.add))
            for s, pick in enumerate((pick1, pick2)):
                link(dve.tensor_tensor(hit[:, :, :], pick[:, :, :], place[:, :, :], ALU.mult))
                link(dve.tensor_reduce(slot_f[:, s, :], hit[:, :, :], AX.X, ALU.add))
            dve.tensor_copy(slot[:, :, :], slot_f[:, :, :]).then_inc(slots_ready, 1)
            link(dve.tensor_tensor(of_block[:, :, :], block_no[:, :].unsqueeze(2).broadcast_to([P, NB, NE - 1]),
                                   ends[:, 0:NE - 1].unsqueeze(1).broadcast_to([P, NB, NE - 1]), ALU.is_ge))
            link(dve.tensor_reduce(expert_f[:, :], of_block[:, :, :], AX.X, ALU.add))
            dve.tensor_copy(expert[:, LAG:LAG + NB], expert_f[:, :]).then_inc(experts_ready, 1)

            def low(n, c):
                dve.wait_ge(hid_high, n * SH_CHUNKS + c + 1)
                dve.tensor_tensor(hid_l[:, c % 2, :], hid[:, c % 2, :], hid_h[:, c % 2, :],
                                  ALU.subtract).then_inc(hid_low, 1)

            def add_picked(n):
                j = job_of[n]
                dve.wait_ge(xy_in[j % 2], (j // 2 + 1) * 16)
                if n >= BEFORE:
                    dve.wait_ge(sh_taken, (n + 1) * GT)
                dve.wait_ge(y_in[n], GT * 2 * 16)
                for s in range(2):
                    for i in range(GT):
                        t = n * GT + i
                        if s == 1:
                            dve.wait_ge(finish_step, steps_done[0] + i + 1)
                        ins_ = dve.scalar_tensor_tensor(xy[:, j % 2, i, :], picked[:, t, s, :], gain[:, s, t:t + 1],
                                                        xy[:, j % 2, i, :], ALU.mult, ALU.add)
                        if s == 0:
                            ins_.then_inc(finish_step, 1)
                ins_.then_inc(finished, 1)
                steps_done[0] += GT

            steps_done = [0]

            def group(n, j):
                for c in range(SH_CHUNKS):
                    m = n * SH_CHUNKS + c
                    dve.wait_ge(h2_done, m + 1)
                    dve.wait_ge(silu_done, m + 1)
                    wait_for(dve, hid_low, m - 1)
                    dve.tensor_tensor(hid[:, c % 2, :], ps[:, 2 * (c % 2) + 1, :], act_s[:, c % 2, :], ALU.mult
                                      ).then_inc(h_done, 1)
                    if m < len(ex_prep):
                        dve.wait_ge(ex_high, m + 1)
                        for (src, lo), (_, hi) in zip(ex_views(m, 1), ex_views(m, 0)):
                            ins_ = dve.tensor_tensor(lo, src, hi, ALU.subtract)
                        ins_.then_inc(ex_low, 1)
                    if c > 0:
                        low(n, c - 1)
                    if (n, c) in join_at:
                        add_picked(join_at[n, c])
                low(n, SH_CHUNKS - 1)
                dve.wait_ge(xy_in[j % 2], (j // 2 + 1) * 16)
                dve.wait_ge(h_through, (n + 1) * SH_CHUNKS)
                for i in range(GT):
                    ins_ = dve.scalar_tensor_tensor(
                        xy[:, j % 2, i, :], ps[:, ACC + i // 2, (i % 2) * C:(i % 2 + 1) * C],
                        sgate[:, n * GT + i:n * GT + i + 1], xy[:, j % 2, i, :], ALU.mult, ALU.add)
                    ins_.then_inc(sh_taken, 1)

            for n in range(BEFORE):
                group(n, n)

            def step(k, q, s):
                if there(s, 0):
                    dve.wait_ge(xb_high, s + 1)
                    dve.tensor_tensor(xbt_l[:, q % 2, :], ps[:, q % 2, 0:C], xbt_h[:, q % 2, :],
                                      ALU.subtract).then_inc(xb_low, 1)
                if there(s, 1):
                    r = (q + 1) % 2
                    dve.wait_ge(b_silu, s)
                    wait_for(dve, b_turned, s - 2)
                    dve.tensor_tensor(hb_tok[:, r, 0:F_MOE], ps[:, 2 + r, F_MOE:F2], silu_b[:, r, :], ALU.mult
                                      ).then_inc(b_hidden, 1)
                if there(s, 2):
                    dve.wait_ge(b_high, s - 1)
                    dve.tensor_tensor(ht_l[:, q % 2, :], ps[:, 4 + q % 2, 0:2 * P], ht_h[:, q % 2, :],
                                      ALU.subtract).then_inc(b_low, 1)

            block_steps(step)(dve)
            for n in range(BEFORE, NG):
                group(n, job_of[n])
            add_picked(NG - 1)

        @block.tensor
        def _(pe):
            for n, (kind, c) in enumerate(prep):
                if n >= 4:
                    pe.wait_ge(prep_low, n - 3)
                if kind == "fc":
                    pe.wait_ge(fc_in[c % RAW], (c // RAW + 1) * 32)
                    r = rows_of(c)
                    for m in range(2 * KC):
                        ins_ = pe.transpose(ps[:, n % 4, m * P:m * P + r],
                                            raw_fc[0:r, c % RAW, m // KC, (m % KC) * P:(m % KC + 1) * P],
                                            ident[0:r, 0:r])
                else:
                    pe.wait_ge(proj_in, 48)
                    for i, m in enumerate(c):
                        r = rows_of(m)
                        for kc in range(KC):
                            at_ = i * C + kc * P
                            ins_ = pe.transpose(ps[0:r, n % 4, at_:at_ + P], raw_sp[:, kc, m * P:m * P + r], ident[:, :])
                ins_.then_inc(prep_turned, 1)
            pe.wait_ge(hits_ready, 1)
            pe.wait_ge(consts_made, 4)
            hits = hit[:, :, :].rearrange("p t e -> p (t e)")
            pe.matmul(ps[:, PREP, 0:T * NE], ones[:, :], hits, start=True, stop=True)
            pe.matmul(ps[:, PREP + 1, 0:T * NE], below[:, :], hits, start=True, stop=True).then_inc(counted, 1)
            pe.wait_ge(prep_low, len(prep))
            pe.wait_ge(zeroed, 1)

            def up(n, c):
                m = n * SH_CHUNKS + c
                if c == 0:
                    pe.wait_ge(xg_in[n % 2], (n // 2 + 1) * 32)
                wait_for(pe, h_done, m - 1)
                for f, done in enumerate((h1_done, h2_done)):
                    for kc in range(KC):
                        ins_ = three_products(pe, ps[:, 2 * (c % 2) + f, :], w12_h[:, c, f * KC + kc, :],
                                              w12_l[:, c, f * KC + kc, :], xg_h[:, n % 2, kc, :], xg_l[:, n % 2, kc, :],
                                              kc == 0, kc == KC - 1)
                    ins_.then_inc(done, 1)

            def down(n, c):
                pe.wait_ge(hid_low, n * SH_CHUNKS + (c + 1))
                if c == 0:
                    wait_for(pe, sh_taken, n * GT)
                for j in range(GT):
                    dst = ps[:, ACC + j // 2, (j % 2) * C:(j % 2 + 1) * C]
                    cols = slice(j * P, (j + 1) * P)
                    pe.matmul(dst, hid_h[:, c % 2, cols], wp_h[:, c, :], start=c == 0 and j % 2 == 0, stop=False,
                              skip_group_check=True)
                    pe.matmul(dst, hid_h[:, c % 2, cols], wp_l[:, c, :], start=False, stop=False,
                              skip_group_check=True)
                    ins_ = pe.matmul(dst, hid_l[:, c % 2, cols], wp_h[:, c, :], start=False, stop=c == SH_CHUNKS - 1,
                                     skip_group_check=True)
                ins_.then_inc(h_through, 1)

            def turn_expert(m):
                e, kind = ex_prep[m]
                if m == 0:
                    pe.wait_ge(slots_ready, 1)
                if m >= 2:
                    pe.wait_ge(ex_low, m - 1)
                bank = ps[:, PREP + m % 2, :]
                if kind < KC:
                    pe.wait_ge(ex_in[e % 2], (e // 2 + 1) * 64)
                    for f in range(2):
                        for s, r in ((0, FA), (1, FB)):
                            ins_ = pe.transpose(bank[:, f * F_MOE + s * FA:f * F_MOE + s * FA + r],
                                                raw_ex[0:r, e % 2, s, f, kind * P:(kind + 1) * P], ident[0:r, 0:r])
                else:
                    for s, r in ((0, FA), (1, FB)):
                        for kc in range(KC):
                            f0 = e * F_MOE + s * FA
                            ins_ = pe.transpose(bank[0:r, s * C + kc * P:s * C + (kc + 1) * P],
                                                raw_ep[:, kc, f0:f0 + r], ident[:, :])
                ins_.then_inc(ex_turned, 1)

            def group(n):
                for c in range(SH_CHUNKS):
                    up(n, c)
                    if n * SH_CHUNKS + c < len(ex_prep):
                        turn_expert(n * SH_CHUNKS + c)
                    if c >= 2:
                        down(n, c - 2)
                down(n, SH_CHUNKS - 2)
                down(n, SH_CHUNKS - 1)

            for n in range(BEFORE):
                group(n)

            pe.wait_ge(sh_taken, BEFORE * GT)
            pe.wait_ge(experts_ready, 1)

            turn_experts = [None]

            def step(k, q, s):
                if q == 0:
                    turn_experts[0] = nc.values_load_multi_w_load_instructions(
                        expert[0:1, bass.ds(k * UNROLL, UNROLL + 2)], engines=[mybir.EngineType.PE],
                        min_val=0, max_val=NE - 1,
                        skip_runtime_bounds_check_because="a count of NE - 1 comparisons")[1]
                e_down, e_up = turn_experts[0][q], turn_experts[0][q + 2]
                if there(s, 0):
                    kb, qb = at(k, q, 0)
                    pe.wait_ge(xb_in[qb // 2], kb * 16 + 16)
                    wait_for(pe, xb_low, s - 1)
                    for kc in range(KC):
                        ins_ = pe.transpose(ps[:, q % 2, kc * P:(kc + 1) * P], xb[:, qb, kc * P:(kc + 1) * P], ident[:, :])
                    ins_.then_inc(xb_turned, 1)
                if there(s, 1):
                    r = (q + 1) % 2
                    pe.wait_ge(xb_low, s)
                    wait_for(pe, b_hidden, s - 2)
                    cols = bass.ds(e_up * F2, F2)
                    for kc in range(KC):
                        ins_ = three_products(pe, ps[:, 2 + r, 0:F2], xbt_h[:, r, kc * P:(kc + 1) * P],
                                              xbt_l[:, r, kc * P:(kc + 1) * P], e12_h[:, kc, cols], e12_l[:, kc, cols],
                                              kc == 0, kc == KC - 1)
                    ins_.then_inc(up_done, 1)
                if there(s, 2):
                    pe.wait_ge(b_hidden, s - 1)
                    wait_for(pe, b_low, s - 3)
                    for i in range(2):
                        ins_ = pe.transpose(ps[:, 4 + q % 2, i * P:(i + 1) * P], hb_tok[:, q % 2, i * P:(i + 1) * P],
                                            ident[:, :])
                    ins_.then_inc(b_turned, 1)
                if there(s, 3):
                    r = (q + 1) % 2
                    pe.wait_ge(b_low, s - 2)
                    wait_for(pe, b_taken, s - 4)
                    cols = bass.ds(e_down * C, C)
                    for i in range(2):
                        ins_ = three_products(pe, ps[:, 6 + r, 0:C], ht_h[:, r, i * P:(i + 1) * P],
                                              ht_l[:, r, i * P:(i + 1) * P], ep_h[:, i, cols], ep_l[:, i, cols],
                                              i == 0, i == 1)
                    ins_.then_inc(b_done, 1)

            block_steps(step)(pe)
            pe.wait_ge(b_low, NB)
            pe.wait_ge(b_taken, NB)
            for n in range(BEFORE, NG):
                group(n)


def flamingo_block(nc, x, ctx_2048, mask, g_xattn, g_ffn, Wq, bq, Wk, bk, Wv, bv, Wo, qn_w, kn_w, gate_w,
                   expert_fc1, expert_fc2, expert_proj, shared_fc1, shared_fc2, shared_proj, shared_gate_w, out):
    B, S, _ = x.shape
    N = B * S
    ins = dict(x=x, ctx=ctx_2048, mask=mask, g_xattn=g_xattn, g_ffn=g_ffn, Wq=Wq, bq=bq, Wk=Wk, bk=bk, Wv=Wv,
               bv=bv, Wo=Wo, qn=qn_w, kn=kn_w, gate_w=gate_w, expert_fc1=expert_fc1, expert_fc2=expert_fc2,
               expert_proj=expert_proj, shared_fc1=shared_fc1, shared_fc2=shared_fc2, shared_proj=shared_proj,
               shared_gate_w=shared_gate_w)
    scratch = dict(
        x1=nc.dram_tensor("x1_scratch", [N, C], F32, kind="Internal").ap(),
        x2h=nc.dram_tensor("x2h_scratch", [KC, P, N], F32, kind="Internal").ap(),
        x2l=nc.dram_tensor("x2l_scratch", [KC, P, N], F32, kind="Internal").ap(),
        x2=nc.dram_tensor("x2_scratch", [N, C], F32, kind="Internal").ap(),
        sorted_x=nc.dram_tensor("sorted_x", [2 * N + NE * P, C], F32, kind="Internal").ap(),
        sorted_y=nc.dram_tensor("sorted_y", [2 * N + NE * P, C], F32, kind="Internal").ap(),
        part=nc.dram_tensor("part_scratch", [N, C], F32, kind="Internal").ap(),
    )
    with ExitStack() as es:
        kept = {name: es.enter_context(nc.sbuf_tensor(name, shape, F32)) for name, shape in (
            ("ident", [P, P]), ("logits", [P, N // P, NE + 1]), ("gates", [P, 2]), ("tanh_g", [P, 2]),
            ("rank", [P, NE]))}
        attention_pass(nc, ins, kept, scratch)
        ffn_pass(nc, ins, kept, scratch, out)


_INS = ['x', 'ctx_2048', 'mask_1xSxS2_ff0', 'g_xattn', 'g_ffn', 'L0_xattn_Wq', 'L0_xattn_bq', 'L0_xattn_Wk',
        'L0_xattn_bk', 'L0_xattn_Wv', 'L0_xattn_bv', 'L0_xattn_Wo', 'L0_xattn_qn_w', 'L0_xattn_kn_w',
        'L0_ffn_gate_w', 'L0_ffn_expert_fc1', 'L0_ffn_expert_fc2', 'L0_ffn_expert_proj', 'L0_ffn_shared_fc1',
        'L0_ffn_shared_fc2', 'L0_ffn_shared_proj', 'L0_ffn_shared_gate_w']
_OUTS = [((64, 64, 256), 'float32')]


def kernel(**inputs):
    import numpy as _np
    import concourse.bacc as _bacc
    from concourse import mybir as _mybir
    from concourse.bass_utils import run_bass_kernel_spmd as _run

    nc = _bacc.Bacc("TRN2", target_bir_lowering=False, num_devices=1)
    arrays, args = {}, []
    for name in _INS:
        a = _np.ascontiguousarray(inputs[name])
        arrays[f"in_{name}_dram"] = a
        args.append(nc.dram_tensor(f"in_{name}_dram", a.shape, _mybir.dt.from_np(a.dtype), kind="ExternalInput").ap())
    for i, (shape, dtype) in enumerate(_OUTS):
        dt = _mybir.dt.from_np(_np.dtype(dtype))
        args.append(nc.dram_tensor(f"out_{i}_dram", shape, dt, kind="ExternalOutput").ap())
    flamingo_block(nc, *args)
    r = _run(nc, [arrays], core_ids=[0])
    return r.results[0]["out_0_dram"]
```

```python
from contextlib import ExitStack

import numpy as np
import concourse.bass as bass
from concourse import mybir

F32 = mybir.dt.float32
F32R = mybir.dt.float32r
F16 = mybir.dt.float16
BF16 = mybir.dt.bfloat16
U32 = mybir.dt.uint32
I32 = mybir.dt.int32
ACT = mybir.ActivationFunctionType
ALU = mybir.AluOpType
AX = mybir.AxisListType

P = 128
C = 256
KC = C // P
HD = 128
NH = 16
NKV = 4
GQ = NH // NKV
SEQ = 64
BANK = 512
Q8 = 8
QF = NH * HD
KVF = NKV * HD
LN_EPS = 1e-5
RMS_EPS = 1e-6
QK_GAIN = 8192.0
NE = 8
F_SHARED = 704
F_MOE = 176
SH_CHUNKS = -(-F_SHARED // P)
SH_TAIL = F_SHARED - (SH_CHUNKS - 1) * P
RAW_CHUNKS = 4
GROUP = 512
GT = GROUP // P


def wait_for(eng, sem, value):
    if not isinstance(value, int) or value > 0:
        eng.wait_ge(sem, value)


def three_products(eng, out, stat_hi, stat_lo, mov_hi, mov_lo, first, last):
    eng.matmul(out, stat_hi, mov_hi, start=first, stop=False)
    eng.matmul(out, stat_hi, mov_lo, start=False, stop=False)
    return eng.matmul(out, stat_lo, mov_hi, start=False, stop=last)


def attention_pass(nc, ins, kept, scratch):
    x_tok = ins["x"].rearrange("b s c -> (b s) c")
    ctx_tok = ins["ctx"].rearrange("b s c -> (b s) c")
    T = x_tok.shape[0] // P
    x1_dram, x2h_dram, x2l_dram = scratch["x1"], scratch["x2h"], scratch["x2l"]
    x2_dram, sorted_x = scratch["x2"], scratch["sorted_x"]
    ident, logits = kept["ident"], kept["logits"]
    ZP = 96
    ZC = sorted_x.shape[0] * C // (T * ZP)

    with ExitStack() as es:
        def sb(name, shape, dt=F32):
            return es.enter_context(nc.sbuf_tensor(name, shape, dt))

        def sem(name):
            return es.enter_context(nc.semaphore(name))

        wq_h, wq_l = sb("wq_h", [P, KC, QF], F32R), sb("wq_l", [P, KC, QF], F32R)
        wkv_h, wkv_l = sb("wkv_h", [P, KC, 2 * KVF], F32R), sb("wkv_l", [P, KC, 2 * KVF], F32R)
        wo_h, wo_l = sb("wo_h", [P, NH, C], F32R), sb("wo_l", [P, NH, C], F32R)
        bias = sb("bias", [P, QF + 2 * KVF])
        mask = sb("mask", [P, SEQ])
        gate_rows = sb("gate_rows", [NE + 1, C])
        gate_t = sb("gate_t", [P, KC, NE + 1])
        norm_rows = sb("norm_rows", [P, 2, HD])
        norm_cols = sb("norm_cols", [P, 2])
        w_prod = sb("w_prod", [P, HD])
        w_small = sb("w_small", [P, 8])
        neg_half = sb("neg_half", [P, NH + NKV])
        eps = sb("eps", [P, 5])
        xt = sb("xt", [P, 2, C])
        ct = sb("ct", [P, 2, C])
        xr = sb("xr", [P, 2, C])
        xn = sb("xn", [P, C])
        xc_h, xc_l = sb("xc_h", [P, 2, KC, P], F32R), sb("xc_l", [P, 2, KC, P], F32R)
        stats = sb("stats", [P, 6])
        moments = sb("moments", [P, 2])
        rstd = sb("rstd", [P, 2])
        qk = sb("qk", [P, QF + KVF])
        sq_junk = sb("sq_junk", [P, QF + KVF], BF16)
        sumsq = sb("sumsq", [P, NH + NKV])
        meansq = sb("meansq", [P, NH + NKV])
        rnorm = sb("rnorm", [P, NH + NKV])
        v32 = sb("v32", [P, KVF])
        v_own = sb("v_own", [P, 2, 2, KVF], F32R)
        v_other = sb("v_other", [P, 2, 2, KVF], F32R)
        qt_h, qt_l = sb("qt_h", [P, NH, P], F16), sb("qt_l", [P, NH, P], F16)
        kt_h, kt_l = sb("kt_h", [P, NKV, P], F16), sb("kt_l", [P, NKV, P], F16)
        probs = sb("probs", [P, NH, SEQ])
        row_max = sb("row_max", [P, NH])
        row_sum = sb("row_sum", [P, NH])
        row_inv = sb("row_inv", [P, NH])
        pt_h, pt_l = sb("pt_h", [P, 2, GQ, P], F32R), sb("pt_l", [P, 2, GQ, P], F32R)
        ot_h, ot_l = sb("ot_h", [P, NH, P], F32R), sb("ot_l", [P, NH, P], F32R)
        x1 = sb("x1", [P, 2, C])
        stats2 = sb("stats2", [P, 6])
        moments2 = sb("moments2", [P, 2])
        rstd2 = sb("rstd2", [P, 2])
        spacer = sb("spacer", [P, 2])
        xn2 = sb("xn2", [P, 2, C])
        zeros = sb("zeros", [ZP, ZC])
        x2t = sb("x2t", [P, KC, P])
        x2_h, x2_l = sb("x2_h", [P, 2, KC, P], F32R), sb("x2_l", [P, 2, KC, P], F32R)
        tanh_g = kept["tanh_g"]

        work = es.enter_context(nc.psum_tensor("work", [P, 5, BANK], F32))
        turn = es.enter_context(nc.psum_tensor("turn", [P, 2, BANK], F32))
        yb = es.enter_context(nc.psum_tensor("yb", [P, BANK], F32))

        consts_in = sem("consts_in")
        bias_in = sem("bias_in")
        raw_in = [sem(f"raw_in{i}") for i in range(3)]
        raw_h = sem("raw_h")
        raw_l = sem("raw_l")
        ident_zero, ident_done = sem("ident_zero"), sem("ident_done")
        pool_consts = sem("pool_consts")
        w_step = sem("w_step")
        gates_done = sem("gates_done")
        gate_turned, gate_split = sem("gate_turned"), sem("gate_split")
        x_in = [sem(f"x_in{i}") for i in range(2)]
        xr_in = [sem(f"xr_in{i}") for i in range(2)]
        x_stats, x_moments, x_vareps, x_rstd = sem("x_stats"), sem("x_moments"), sem("x_vareps"), sem("x_rstd")
        xn_ready, x_turned, x_high, x_split = sem("xn_ready"), sem("x_turned"), sem("x_high"), sem("x_split")
        proj_done = sem("proj_done")
        proj_taken = sem("proj_taken")
        squared = sem("squared")
        ms_ready, rn_ready = sem("ms_ready"), sem("rn_ready")
        normed, normed_act = sem("normed"), sem("normed_act")
        v_high, v_split = sem("v_high"), sem("v_split")
        v_swapped = [sem(f"v_swapped{i}") for i in range(2)]
        qk_turned, qk_high, qk_split = sem("qk_turned"), sem("qk_high"), sem("qk_split")
        s_done, s_taken, max_done = sem("s_done"), sem("s_taken"), sem("max_done")
        shifted, expd, summed, inverted, probs_ready = (
            sem("shifted"), sem("expd"), sem("summed"), sem("inverted"), sem("probs_ready"))
        p_turned, p_high, p_split = sem("p_turned"), sem("p_high"), sem("p_split")
        pv_done, o_high, o_split = sem("pv_done"), sem("o_high"), sem("o_split")
        y_done, x1_ready = sem("y_done"), sem("x1_ready")
        x2_stats, x2_moments, x2_vareps, x2_rstd = (
            sem("x2_stats"), sem("x2_moments"), sem("x2_vareps"), sem("x2_rstd"))
        xn2_ready, x2_turned, x2_copied, x2_high, x2_split = (
            sem("xn2_ready"), sem("x2_turned"), sem("x2_copied"), sem("x2_high"), sem("x2_split"))
        lg_done, lg_taken = sem("lg_done"), sem("lg_taken")
        raw_fc_in = sem("raw_fc_in")
        zeros_ready, cleared = sem("zeros_ready"), sem("cleared")
        x1_out = [sem(f"x1_out{i}") for i in range(2)]
        x2_out = [sem(f"x2_out{i}") for i in range(2)]

        stage = [qk[:, 0:QF], kept["raw_fc"][:, :, :, :].rearrange("p r f c -> p (r f c)"), es.enter_context(nc.sbuf_tensor("stage", [P, QF], F32))[:, :]]
        wq_rows = ins["Wq"].rearrange("(k p) n -> p k n", p=P)
        wo_rows = ins["Wo"].rearrange("(h p) n -> p h n", p=P)
        kv_stage = lambda s: s.rearrange("p (k n) -> p k n", k=KC)
        wo_stage = lambda s: s.rearrange("p (h n) -> p h n", n=C)
        H2 = NH // 2
        ACT_NORM = 3
        bank_of = (4, 0, 1, 2, 3, 4)
        pieces = [
            (lambda s: kv_stage(s), wkv_h[:, :, :], wkv_l[:, :, :],
             [(lambda s: kv_stage(s)[:, :, 0:KVF], ins["Wk"].rearrange("(k p) n -> p k n", p=P)),
              (lambda s: kv_stage(s)[:, :, KVF:2 * KVF], ins["Wv"].rearrange("(k p) n -> p k n", p=P))]),
            (lambda s: s, wq_h[:, 0, :], wq_l[:, 0, :], [(lambda s: s, wq_rows[:, 0, :])]),
            (lambda s: s, wq_h[:, 1, :], wq_l[:, 1, :], [(lambda s: s, wq_rows[:, 1, :])]),
            (lambda s: wo_stage(s), wo_h[:, 0:H2, :], wo_l[:, 0:H2, :],
             [(lambda s: wo_stage(s), wo_rows[:, 0:H2, :])]),
            (lambda s: wo_stage(s), wo_h[:, H2:NH, :], wo_l[:, H2:NH, :],
             [(lambda s: wo_stage(s), wo_rows[:, H2:NH, :])]),
        ]
        stage_of = [2, 0, 1, 2, 1]
        raw_count = [[], [], []]
        for n, piece in enumerate(pieces):
            s = stage_of[n]
            before = raw_count[s][-1][1] if raw_count[s] else 0
            raw_count[s].append((n, before + 16 * len(piece[3])))
        raw_ready = {n: (s, c) for s in range(3) for n, c in raw_count[s]}
        WO_FIRST = 3

        def at(k, p, ahead):
            q = p + ahead
            return k + q // 2, q % 2

        def turns(step):
            def run(eng):
                for t in range(4):
                    step(t // 2, t % 2, t)
                with eng.Fori(2, T // 2 - 1) as k:
                    step(k, 0, k * 2)
                    step(k, 1, k * 2 + 1)
                for t in range(T - 2, T + 2):
                    step(t // 2, t % 2, t)
            return run

        def has(t, ahead):
            return not isinstance(t, int) or 0 <= t + ahead < T

        block = es.enter_context(nc.Block())

        @block.sync
        def _(sp):
            def load_tile(k, p, t):
                rows = bass.ds(t * P, P)
                sp.dma_start(xt[:, p, :], x_tok[rows, :]).then_inc(x_in[p], 16)
                sp.dma_start(ct[:, p, :], ctx_tok[rows, :]).then_inc(x_in[p], 16)

            def load_piece(n):
                s = stage_of[n]
                earlier = [m for m in range(n) if stage_of[m] == s]
                if earlier:
                    sp.wait_ge(raw_l, earlier[-1] + 1)
                for part, src in pieces[n][3]:
                    sp.dma_start(part(stage[s]), src).then_inc(raw_in[s], 16)

            load_tile(0, 0, 0)
            for n in range(WO_FIRST):
                load_piece(n)
            load_tile(0, 1, 1)
            at_col = 0
            for b in (ins["bq"], ins["bk"], ins["bv"]):
                n = b.shape[0]
                sp.dma_start(bias[:, at_col:at_col + n], b.partition_broadcast(P)).then_inc(bias_in, 16)
                at_col += n
            sp.dma_start(mask[0:SEQ, :], ins["mask"][0, :, :]).then_inc(consts_in, 16)
            sp.dma_start(mask[SEQ:P, :], ins["mask"][0, :, :]).then_inc(consts_in, 16)
            for n, w in enumerate((ins["qn"], ins["kn"])):
                sp.dma_start(norm_rows[:, n, :], w.partition_broadcast(P)).then_inc(consts_in, 16)
                sp.dma_start(norm_cols[:, n:n + 1], w.rearrange("(p a) -> p a", a=1)).then_inc(consts_in, 16)
            sp.dma_start(gate_rows[0:NE, :], ins["gate_w"]).then_inc(consts_in, 16)
            sp.dma_start(gate_rows[NE:NE + 1, :], ins["shared_gate_w"]).then_inc(consts_in, 16)
            for n, g in enumerate((ins["g_xattn"], ins["g_ffn"])):
                sp.dma_start(kept["gates"][:, n:n + 1], g.partition_broadcast(P)).then_inc(consts_in, 16)
            for n in range(WO_FIRST, len(pieces)):
                load_piece(n)

            def step(k, p, t):
                if has(t, 2):
                    wait_for(sp, xn_ready, t + 1)
                    wait_for(sp, x_turned, t + 1)
                    load_tile(*at(k, p, 2), t + 2)
                if has(t, 0):
                    sp.dma_start(sorted_x[bass.ds(t * (ZP * ZC // C), ZP * ZC // C), :].rearrange(
                        "(p a) c -> p (a c)", p=ZP), zeros[:, :]).then_inc(cleared, 16)
                    wait_for(sp, x1_ready, t - 1)
                    sp.dma_start(xr[:, p, :], x_tok[bass.ds(t * P, P), :]).then_inc(xr_in[p], 16)
                    wait_for(sp, v_split, t + 1)
                    wait_for(sp, pv_done, t * 4 - 4)
                    half = P // 2
                    sp.dma_start(v_other[0:half, p, :, :].bitcast(F32), v_own[half:P, p, :, :].bitcast(F32)).then_inc(v_swapped[p], 16)
                    sp.dma_start(v_other[half:P, p, :, :].bitcast(F32), v_own[0:half, p, :, :].bitcast(F32)).then_inc(v_swapped[p], 16)
                if has(t, -2):
                    cols = bass.ds(t * P - 2 * P, P)
                    sp.wait_ge(x1_ready, t - 1)
                    sp.wait_ge(x2_split, t - 1)
                    sp.dma_start(x1_dram[cols, :], x1[:, p, :]).then_inc(x1_out[p], 16)
                    sp.dma_start(x2_dram[cols, :], xn2[:, p, :]).then_inc(x1_out[p], 16)
                    sp.dma_start(x2h_dram[:, :, cols].rearrange("k p n -> p k n"),
                                 x2_h[:, p, :, :].bitcast(F32)).then_inc(x2_out[p], 16)
                    sp.dma_start(x2l_dram[:, :, cols].rearrange("k p n -> p k n"),
                                 x2_l[:, p, :, :].bitcast(F32)).then_inc(x2_out[p], 16)

            sp.wait_ge(zeros_ready, 1)
            turns(step)(sp)
            for c in range(RAW_CHUNKS):
                for f, w in enumerate((ins["shared_fc1"], ins["shared_fc2"])):
                    sp.dma_start(kept["raw_fc"][:, c, f, :], w[c * P:(c + 1) * P, :]).then_inc(raw_fc_in, 16)
            sp.wait_ge(raw_fc_in, RAW_CHUNKS * 32)
            sp.wait_ge(cleared, 16 * T)
            for p in range(2):
                sp.wait_ge(x1_out[p], 32 * T // 2)
                sp.wait_ge(x2_out[p], 32 * T // 2)

        @block.gpsimd
        def _(pool):
            pool.memset(ident[:, :], 0.0).then_inc(ident_zero, 1)
            pool.memset(neg_half[:, :], -0.5).then_inc(pool_consts, 1)
            pool.memset(eps[:, 0:1], LN_EPS).then_inc(pool_consts, 1)
            pool.memset(eps[:, 1:5], RMS_EPS * HD / QK_GAIN ** 2).then_inc(pool_consts, 1)
            pool.wait_ge(ident_zero, 1)
            pool.affine_select(out=ident[:, :], in_=ident[:, :], compare_op=ALU.not_equal, fill=1.0,
                               base=0, pattern=[[-1, P]], channel_multiplier=1).then_inc(ident_done, 1)
            pool.wait_ge(pool_consts, 3)

            def reciprocal_std(t):
                pool.wait_ge(x_moments, t + 1)
                wait_for(pool, xn_ready, t)
                pool.tensor_tensor(rstd[:, 0:1], moments[:, 1:2], eps[:, 0:1], ALU.add).then_inc(x_vareps, 1)
                pool.wait_ge(x_vareps, t + 1)
                pool.tensor_tensor(rstd[:, 1:2], rstd[:, 0:1], neg_half[:, 0:1], ALU.pow).then_inc(x_rstd, 1)

            def shift(t, u):
                heads = slice(u * Q8, u * Q8 + Q8)
                pool.wait_ge(max_done, t * 2 + (u + 1))
                pool.tensor_tensor(probs[:, heads, :], probs[:, heads, :],
                                   row_max[:, heads].unsqueeze(2).broadcast_to([P, Q8, SEQ]),
                                   ALU.subtract).then_inc(shifted, 1)

            def normalise_probs(t, u):
                heads = slice(u * Q8, u * Q8 + Q8)
                pool.wait_ge(inverted, t * 2 + (u + 1))
                pool.tensor_tensor(probs[:, heads, :], probs[:, heads, :],
                                   row_inv[:, heads].unsqueeze(2).broadcast_to([P, Q8, SEQ]),
                                   ALU.mult).then_inc(probs_ready, 1)

            def rms_norm(t, j):
                s = slice(4 * j, 4 * j + 4)
                col = QF if j == 0 else (j - 1) * BANK
                pool.wait_ge(squared, t * 5 + (j + 1))
                pool.tensor_tensor(meansq[:, s], sumsq[:, s], eps[:, 1:5], ALU.add).then_inc(ms_ready, 1)
                pool.wait_ge(ms_ready, t * 5 + (j + 1))
                pool.tensor_tensor(rnorm[:, s], meansq[:, s], neg_half[:, s], ALU.pow).then_inc(rn_ready, 1)
                if j == ACT_NORM:
                    return
                pool.wait_ge(rn_ready, t * 5 + (j + 1))
                part = qk[:, col:col + BANK].rearrange("p (h d) -> p h d", d=HD)
                pool.tensor_tensor(part, part, rnorm[:, s].unsqueeze(2).broadcast_to([P, 4, HD]),
                                   ALU.mult).then_inc(normed, 1)

            reciprocal_std(0)
            reciprocal_std(1)

            def step(k, p, t):
                if has(t, -1):
                    shift(t - 1, 0)
                if has(t, -2):
                    pool.wait_ge(x2_moments, t - 1)
                    wait_for(pool, xn2_ready, t - 2)
                    pool.tensor_tensor(rstd2[:, 0:1], moments2[:, 1:2], eps[:, 0:1], ALU.add).then_inc(x2_vareps, 1)
                    pool.wait_ge(x2_vareps, t - 1)
                    pool.tensor_tensor(rstd2[:, 1:2], rstd2[:, 0:1], neg_half[:, 0:1], ALU.pow
                                       ).then_inc(x2_rstd, 1)
                if has(t, -1):
                    shift(t - 1, 1)
                if has(t, -1):
                    normalise_probs(t - 1, 0)
                    normalise_probs(t - 1, 1)
                if has(t, 0):
                    rms_norm(t, 0)
                    for j in range(1, 5):
                        rms_norm(t, j)
                    pool.wait_ge(v_high, t + 1)
                    pool.tensor_tensor(v_own[:, p, 1, :], v32[:, :], v_own[:, p, 0, :],
                                       ALU.subtract).then_inc(v_split, 1)
                if has(t, 2):
                    reciprocal_std(t + 2)

            turns(step)(pool)

        @block.scalar
        def _(act):
            def split_high(n):
                s, count = raw_ready[n]
                view, high, low, _ = pieces[n]
                act.wait_ge(raw_in[s], count)
                act.activation(high, view(stage[s]), ACT.Copy).then_inc(raw_h, 1)

            def x_highs(t):
                act.wait_ge(x_turned, t + 1)
                wait_for(act, proj_done, t * 6)
                act.activation(xc_h[:, :, :, :], turn_x, ACT.Copy).then_inc(x_high, 1)

            def squares(t, j):
                act.wait_ge(proj_taken, t * 6 + (j + 1))
                wait_for(act, ms_ready, t * 5 + (j + 1) - 5)
                for h in range(4):
                    col = (QF if j == 0 else (j - 1) * BANK) + h * HD
                    ins_ = act.activation(sq_junk[:, col:col + HD], qk[:, col:col + HD], ACT.Square,
                                          scale=1.0 / QK_GAIN,
                                          accum_out=sumsq[:, 4 * j + h:4 * j + h + 1])
                ins_.then_inc(squared, 1)

            def probs_high(t, u):
                act.wait_ge(p_turned, t * 2 + (u - 1))
                wait_for(act, pv_done, t * 4 - 4)
                act.activation(pt_h[:, u, :, :], turn[:, 1 - u, :].rearrange("p (i n) -> p i n", i=GQ),
                               ACT.Copy).then_inc(p_high, 1)

            def exponents(t, u):
                heads = slice(u * Q8, u * Q8 + Q8)
                act.wait_ge(shifted, t * 2 + (u + 1))
                act.activation(probs[:, heads, :], probs[:, heads, :], ACT.Exp).then_inc(expd, 1)

            turn_x = turn[:, 1, :].rearrange("p (s k n) -> p s k n", s=2, k=KC)
            split_high(0)
            x_highs(0)
            for n in range(1, WO_FIRST):
                split_high(n)

            def step(k, p, t):
                if has(t, -1):
                    exponents(t - 1, 0)
                if has(t, 0):
                    squares(t, 0)
                if has(t, -1):
                    exponents(t - 1, 1)
                if has(t, 0):
                    squares(t, 1)
                if has(t, -2):
                    pk, _ = at(k, p, -2)
                    act.wait_ge(x2_turned, t - 1)
                    wait_for(act, lg_done, t - 2)
                    turned = yb[:, C:2 * C].rearrange("p (k n) -> p k n", k=KC)
                    act.activation(x2t[:, :, :], turned, ACT.Copy).then_inc(x2_copied, 1)
                    wait_for(act, x2_out[p], pk * 32)
                    act.activation(x2_h[:, p, :, :], turned, ACT.Copy).then_inc(x2_high, 1)
                if has(t, 0):
                    squares(t, 2)
                if has(t, -1):
                    probs_high(t, 0)
                if has(t, 0):
                    squares(t, 3)
                if has(t, -1):
                    probs_high(t, 1)
                if has(t, 0):
                    squares(t, 4)
                if isinstance(t, int) and t == 0:
                    act.wait_ge(gate_turned, 1)
                    act.activation(gate_t[:, :, :], yb[:, 0:KC * (NE + 1)].rearrange("p (k n) -> p k n", k=KC),
                                   ACT.Copy).then_inc(gate_split, 1)
                    act.activation(tanh_g[:, :], kept["gates"][:, :], ACT.Tanh).then_inc(gates_done, 1)
                for g in range(NKV):
                    if g == 2 and has(t, 1):
                        x_highs(t + 1)
                    if g == 2 and has(t, -2):
                        act.wait_ge(lg_done, t - 1)
                        act.activation(logits[:, bass.ds(t - 2, 1), :], yb[:, 0:NE + 1].unsqueeze(1), ACT.Copy
                                       ).then_inc(lg_taken, 1)
                    if has(t, -1):
                        act.wait_ge(pv_done, t * 4 + (g - 3))
                        wait_for(act, y_done, t - 1)
                        act.activation(ot_h[:, GQ * g:GQ * g + GQ, :],
                                       work[:, g, :].rearrange("p (i n) -> p i n", i=GQ),
                                       ACT.Copy).then_inc(o_high, 1)
                if isinstance(t, int) and t == 0:
                    act.wait_ge(w_step, 9)
                if has(t, 0):
                    act.wait_ge(qk_turned, t * 5 + 1)
                    wait_for(act, s_done, t * 2)
                    act.activation(kt_h[:, :, :], turn[:, 0, :].rearrange("p (h n) -> p h n", h=NKV),
                                   ACT.Copy, scale=w_small[:, 7:8]).then_inc(qk_high, 1)
                    act.wait_ge(proj_taken, t * 6 + 6)
                    wait_for(act, pv_done, t * 4 - 4)
                    act.activation(v_own[:, p, 0, :], v32[:, :], ACT.Copy).then_inc(v_high, 1)
                    for j in range(4):
                        if j == 1:
                            act.wait_ge(rn_ready, t * 5 + (ACT_NORM + 1))
                            for h in range(GQ):
                                col = (ACT_NORM - 1) * BANK + h * HD
                                n = ACT_NORM * GQ + h
                                ins_ = act.activation(qk[:, col:col + HD], qk[:, col:col + HD], ACT.Copy,
                                                      scale=rnorm[:, n:n + 1])
                            ins_.then_inc(normed_act, 1)
                        act.wait_ge(qk_turned, t * 5 + (j + 2))
                        act.activation(qt_h[:, 4 * j:4 * j + 4, :],
                                       turn[:, 1 - j % 2, :].rearrange("p (h n) -> p h n", h=4),
                                       ACT.Copy).then_inc(qk_high, 1)
                if isinstance(t, int) and t == 0:
                    for n in range(WO_FIRST, len(pieces)):
                        split_high(n)

            turns(step)(act)

        @block.vector
        def _(dve):
            def split_low(n):
                s, _ = raw_ready[n]
                view, high, low, _ = pieces[n]
                dve.wait_ge(raw_h, n + 1)
                dve.tensor_tensor(low, view(stage[s]), high, ALU.subtract).then_inc(raw_l, 1)

            def x_statistics(k, p, t):
                dve.wait_ge(x_in[p], k * 32 + 32)
                wait_for(dve, x_moments, t)
                dve.bn_stats(stats[:, :], xt[:, p, :]).then_inc(x_stats, 1)
                wait_for(dve, xn_ready, t)
                dve.wait_ge(x_stats, t * 2 + 1)
                dve.memset(spacer[:, 0:1], 0.0).then_inc(x_stats, 1)
                dve.bn_aggr(moments[:, :], stats[:, :]).then_inc(x_moments, 1)

            def x_normalise(k, p, t):
                dve.wait_ge(x_rstd, t + 1)
                wait_for(dve, x_turned, t)
                dve.tensor_scalar(xn[:, :], xt[:, p, :], moments[:, 0:1], rstd[:, 1:2],
                                  ALU.subtract, ALU.mult).then_inc(xn_ready, 1)

            def x_lows(t):
                dve.wait_ge(x_high, t + 1)
                dve.tensor_tensor(xc_l[:, :, :, :], turn[:, 1, :].rearrange("p (s k n) -> p s k n", s=2, k=KC),
                                  xc_h[:, :, :, :], ALU.subtract).then_inc(x_split, 1)

            def q_low(t, j):
                dve.wait_ge(qk_high, t * 5 + (j + 2))
                dve.tensor_tensor(qt_l[:, 4 * j:4 * j + 4, :],
                                  turn[:, 1 - j % 2, :].rearrange("p (h n) -> p h n", h=4),
                                  qt_h[:, 4 * j:4 * j + 4, :], ALU.subtract).then_inc(qk_split, 1)

            def add_bias(t, j):
                dve.wait_ge(proj_done, t * 6 + (j + 1))
                if j == 0:
                    wait_for(dve, qk_turned, t * 5)
                if j == 5:
                    wait_for(dve, v_split, t)
                col = QF if j == 0 else QF + KVF if j == 5 else (j - 1) * BANK
                dst = v32[:, :] if j == 5 else qk[:, col:col + BANK]
                dve.tensor_tensor(dst, work[:, bank_of[j], :], bias[:, col:col + BANK], ALU.add
                                  ).then_inc(proj_taken, 1)

            def sums(t, u):
                heads = slice(u * Q8, u * Q8 + Q8)
                dve.wait_ge(expd, t * 2 + (u + 1))
                dve.tensor_reduce(row_sum[:, heads], probs[:, heads, :], AX.X, ALU.add).then_inc(summed, 1)
                dve.wait_ge(summed, t * 2 + (u + 1))
                wait_for(dve, probs_ready, t * 2 + (u - 1))
                dve.reciprocal(row_inv[:, heads], row_sum[:, heads]).then_inc(inverted, 1)

            def take_scores(t, u):
                heads = slice(u * Q8, u * Q8 + Q8)
                pair = work[:, 2 * u:2 * u + 2, :].rearrange("p b (i n) -> p (b i) n", i=GQ)
                dve.wait_ge(s_done, t * 2 + (u + 1))
                wait_for(dve, p_turned, t * 2)
                for b in range(2):
                    rows, own = slice(b * SEQ, b * SEQ + SEQ), slice(b * SEQ, b * SEQ + SEQ)
                    dve.scalar_tensor_tensor(
                        probs[rows, heads, :], pair[rows, :, own], w_small[rows, 6:7],
                        mask[rows, :].unsqueeze(1).broadcast_to([SEQ, Q8, SEQ]), ALU.mult, ALU.add
                    ).then_inc(s_taken, 1)

            def largest_scores(t, u):
                heads = slice(u * Q8, u * Q8 + Q8)
                dve.wait_ge(s_taken, t * 4 + (2 * u + 2))
                dve.tensor_reduce(row_max[:, heads], probs[:, heads, :], AX.X, ALU.max).then_inc(max_done, 1)

            dve.memset(zeros[:, :], 0.0).then_inc(zeros_ready, 1)
            x_statistics(0, 0, 0)
            x_normalise(0, 0, 0)
            split_low(0)
            x_lows(0)
            for n in range(1, WO_FIRST):
                split_low(n)
            x_statistics(0, 1, 1)
            dve.wait_ge(bias_in, 48)
            dve.wait_ge(raw_l, WO_FIRST)

            def norm_weights():
                dve.wait_ge(consts_in, 16 * 10)
                dve.tensor_tensor(w_prod[:, :], norm_rows[:, 0, :], norm_rows[:, 1, :], ALU.mult).then_inc(w_step, 1)
                dve.tensor_tensor(w_small[:, 0:1], norm_cols[:, 0:1], norm_cols[:, 1:2], ALU.mult).then_inc(w_step, 1)
                dve.wait_ge(w_step, 2)
                dve.tensor_reduce(w_small[:, 1:2], w_prod[:, :], AX.X, ALU.max).then_inc(w_step, 1)
                dve.tensor_reduce(w_small[:, 2:3], w_prod[:, :], AX.X, ALU.min).then_inc(w_step, 1)
                dve.wait_ge(w_step, 4)
                dve.scalar_tensor_tensor(w_small[:, 3:4], w_small[:, 2:3], -1.0, w_small[:, 1:2],
                                         ALU.mult, ALU.max).then_inc(w_step, 1)
                dve.wait_ge(w_step, 5)
                dve.tensor_scalar(w_small[:, 4:5], w_small[:, 3:4], 1e-30, None, ALU.max).then_inc(w_step, 1)
                dve.wait_ge(w_step, 6)
                dve.reciprocal(w_small[:, 5:6], w_small[:, 4:5]).then_inc(w_step, 1)
                dve.tensor_scalar(w_small[:, 6:7], w_small[:, 4:5], float(np.float32(1.0) / np.sqrt(np.float32(HD))),
                                  HD / QK_GAIN ** 2, ALU.mult, ALU.mult).then_inc(w_step, 1)
                dve.wait_ge(w_step, 8)
                dve.tensor_tensor(w_small[:, 7:8], w_small[:, 0:1], w_small[:, 5:6], ALU.mult).then_inc(w_step, 1)
                dve.wait_ge(w_step, 9)
                dve.wait_ge(gates_done, 1)

            def step(k, p, t):
                pk, pp = at(k, p, -1)
                nk, np_ = at(k, p, 1)
                if has(t, 0):
                    add_bias(t, 0)
                if has(t, 0):
                    add_bias(t, 1)
                if has(t, -2):
                    dve.wait_ge(x2_rstd, t - 1)
                    wait_for(dve, x2_turned, t - 2)
                    dve.tensor_scalar(xn2[:, p, :], x1[:, p, :], moments2[:, 0:1], rstd2[:, 1:2],
                                      ALU.subtract, ALU.mult).then_inc(xn2_ready, 1)
                if has(t, -1):
                    sums(t - 1, 0)
                if has(t, 0):
                    add_bias(t, 2)
                if has(t, -1):
                    sums(t - 1, 1)
                if has(t, 0):
                    add_bias(t, 3)
                for u in range(2):
                    if u == 0 and has(t, 0):
                        add_bias(t, 4)
                    if has(t, -1):
                        dve.wait_ge(p_high, t * 2 + (u - 1))
                        dve.tensor_tensor(pt_l[:, u, :, :], turn[:, 1 - u, :].rearrange("p (i n) -> p i n", i=GQ),
                                          pt_h[:, u, :, :], ALU.subtract).then_inc(p_split, 1)
                    if u == 0 and has(t, -2):
                        dve.wait_ge(x2_high, t - 1)
                        dve.tensor_tensor(x2_l[:, p, :, :], yb[:, C:2 * C].rearrange("p (k n) -> p k n", k=KC),
                                          x2_h[:, p, :, :], ALU.subtract).then_inc(x2_split, 1)
                    if u == 0 and has(t, 1):
                        x_normalise(nk, np_, t + 1)
                    if u == 0 and has(t, 0):
                        add_bias(t, 5)
                    if u == 0 and isinstance(t, int) and t == 0:
                        norm_weights()
                if has(t, 2):
                    x_statistics(k + 1, p, t + 2)
                for g in range(NKV):
                    if g == 2 and has(t, 1):
                        x_lows(t + 1)
                    if has(t, -1):
                        heads = slice(GQ * g, GQ * g + GQ)
                        dve.wait_ge(o_high, t * 4 + (g - 3))
                        dve.tensor_tensor(ot_l[:, heads, :], work[:, g, :].rearrange("p (i n) -> p i n", i=GQ),
                                          ot_h[:, heads, :], ALU.subtract).then_inc(o_split, 1)
                if has(t, 0):
                    dve.wait_ge(qk_high, t * 5 + 1)
                    dve.scalar_tensor_tensor(kt_l[:, :, :], turn[:, 0, :].rearrange("p (h n) -> p h n", h=NKV),
                                             w_small[:, 7:8], kt_h[:, :, :], ALU.mult, ALU.subtract
                                             ).then_inc(qk_split, 1)
                    q_low(t, 0)
                    q_low(t, 1)
                    q_low(t, 2)
                    q_low(t, 3)
                    take_scores(t, 0)
                    largest_scores(t, 0)
                if has(t, -1):
                    dve.wait_ge(y_done, t)
                    dve.wait_ge(xr_in[pp], pk * 16 + 16)
                    wait_for(dve, x1_out[pp], pk * 32)
                    dve.scalar_tensor_tensor(x1[:, pp, :], yb[:, 0:C], tanh_g[:, 0:1], xr[:, pp, :],
                                             ALU.mult, ALU.add).then_inc(x1_ready, 1)
                if has(t, -1):
                    dve.wait_ge(x1_ready, t)
                    wait_for(dve, x2_moments, t - 1)
                    dve.bn_stats(stats2[:, :], x1[:, pp, :]).then_inc(x2_stats, 1)
                    wait_for(dve, xn2_ready, t - 1)
                    dve.wait_ge(x2_stats, t * 2 - 1)
                    dve.memset(spacer[:, 1:2], 0.0).then_inc(x2_stats, 1)
                    dve.bn_aggr(moments2[:, :], stats2[:, :]).then_inc(x2_moments, 1)
                if has(t, 0):
                    take_scores(t, 1)
                    largest_scores(t, 1)
                if isinstance(t, int) and t == 0:
                    for n in range(WO_FIRST, len(pieces)):
                        split_low(n)

            turns(step)(dve)

        @block.tensor
        def _(pe):
            def turn_tile(p, t):
                pe.wait_ge(xn_ready, t + 1)
                for s, src in enumerate((xn[:, :], ct[:, p, :])):
                    for kc in range(KC):
                        at_ = (s * KC + kc) * P
                        ins_ = pe.transpose(turn[:, 1, at_:at_ + P], src[:, kc * P:kc * P + P], ident[:, :])
                ins_.then_inc(x_turned, 1)

            def project(t, j):
                if j == 0:
                    pe.wait_ge(x_split, t + 1)
                    wait_for(pe, proj_taken, t * 6)
                if j == 1:
                    wait_for(pe, s_taken, t * 4 - 2)
                if j == 3:
                    wait_for(pe, s_taken, t * 4)
                if j == 5:
                    pe.wait_ge(proj_taken, t * 6 + 1)
                if isinstance(t, int) and t == 0:
                    pe.wait_ge(raw_l, 1 if j in (0, 5) else WO_FIRST)
                src = 1 if j in (0, 5) else 0
                w_h, w_l = (wkv_h, wkv_l) if j in (0, 5) else (wq_h, wq_l)
                col = {0: 0, 5: KVF}.get(j, (j - 1) * BANK)
                for kc in range(KC):
                    ins_ = three_products(pe, work[:, bank_of[j], :], xc_h[:, src, kc, :], xc_l[:, src, kc, :],
                                          w_h[:, kc, col:col + BANK], w_l[:, kc, col:col + BANK],
                                          kc == 0, kc == KC - 1)
                ins_.then_inc(proj_done, 1)

            def turn_heads(j):
                col = QF if j == 0 else (j - 1) * BANK
                bank = j % 2
                for i in range(4):
                    ins_ = pe.transpose(turn[:, bank, i * P:i * P + P], qk[:, col + i * HD:col + (i + 1) * HD],
                                        ident[:, :])
                ins_.then_inc(qk_turned, 1)

            def scores(t, u):
                for place in range(Q8):
                    g, i = 2 * u + place % 2, place // 2
                    h, at_ = g * GQ + i, (place % 4) * P
                    ins_ = three_products(pe, work[:, 2 * u + place // 4, at_:at_ + P], qt_h[:, h, :], qt_l[:, h, :],
                                          kt_h[:, g, :], kt_l[:, g, :], True, True)
                ins_.then_inc(s_done, 1)

            def weighted_values(p, g):
                u, slot = g // 2, g % 2
                rows = slice(slot * SEQ, slot * SEQ + SEQ)
                bank = work[:, g, :].rearrange("p (i n) -> p i n", i=GQ)
                for b in range(2):
                    v = v_own if b == slot else v_other
                    cols = slice(b * SEQ, b * SEQ + SEQ)
                    ins_ = three_products(
                        pe, bank[:, :, cols], v[rows, p, 0, g * HD:(g + 1) * HD], v[rows, p, 1, g * HD:(g + 1) * HD],
                        pt_h[rows, u, :, cols], pt_l[rows, u, :, cols], True, True)
                ins_.then_inc(pv_done, 1)

            pe.wait_ge(ident_done, 1)
            turn_tile(0, 0)
            def turn_probs(t, u):
                pe.wait_ge(qk_split, t * 5 + (u + 4))
                pe.wait_ge(probs_ready, t * 2 + (u + 1))
                for i in range(GQ):
                    two = probs[:, u * Q8 + 2 * i:u * Q8 + 2 * i + 2, :].rearrange("p s e -> p (s e)")
                    ins_ = pe.transpose(turn[:, 1 - u, i * P:i * P + P], two, ident[:, :])
                ins_.then_inc(p_turned, 1)

            def output_heads(t, g):
                if g == 0:
                    wait_for(pe, lg_taken, t)
                pe.wait_ge(o_split, t * 4 + (g + 1))
                for h in range(g * GQ, g * GQ + GQ):
                    ins_ = three_products(pe, yb[:, 0:C], ot_h[:, h, :], ot_l[:, h, :], wo_h[:, h, :],
                                          wo_l[:, h, :], h == 0, h == NH - 1)
                if g == NKV - 1:
                    ins_.then_inc(y_done, 1)

            def turn_qk(t, j):
                if j == 1:
                    if has(t, 1):
                        pe.wait_ge(x_split, t + 2)
                if j > 1:
                    pe.wait_ge(qk_split, t * 5 + (j - 1))
                if j == ACT_NORM:
                    pe.wait_ge(normed_act, t + 1)
                else:
                    pe.wait_ge(normed, t * 4 + (j + 1 if j < ACT_NORM else j))
                turn_heads(j)

            def step(k, p, t):
                pk, pp = at(k, p, -1)
                nk, np_ = at(k, p, 1)
                for j in range(6):
                    if j == 5 and has(t, -1):
                        turn_probs(t - 1, 0)
                    if has(t, 0):
                        project(t, j)
                    if j == 2 and has(t, -2):
                        pe.wait_ge(xn2_ready, t - 1)
                        for kc in range(KC):
                            ins_ = pe.transpose(yb[:, C + kc * P:C + kc * P + P], xn2[:, p, kc * P:kc * P + P], ident[:, :])
                        ins_.then_inc(x2_turned, 1)
                if isinstance(t, int) and t == 0:
                    pe.wait_ge(consts_in, 16 * 10)
                    for kc in range(KC):
                        ins_ = pe.transpose(yb[:, kc * (NE + 1):(kc + 1) * (NE + 1)], gate_rows[:, kc * P:kc * P + P],
                                            ident[0:NE + 1, 0:NE + 1])
                    ins_.then_inc(gate_turned, 1)
                if has(t, -1):
                    turn_probs(t - 1, 1)
                if has(t, -1):
                    pe.wait_ge(v_swapped[pp], pk * 32 + 32)
                for g in range(NKV):
                    if g == 2 and has(t, 1):
                        if not has(t, -1):
                            pe.wait_ge(x_split, 1)
                        turn_tile(np_, t + 1)
                    if g == 2 and has(t, -2):
                        pe.wait_ge(x2_split, t - 1)
                        for kc in range(KC):
                            ins_ = pe.matmul(yb[:, 0:NE + 1], x2t[:, kc, :], gate_t[:, kc, :],
                                             start=(kc == 0), stop=(kc == KC - 1))
                        ins_.then_inc(lg_done, 1)
                    if has(t, -1):
                        if g % 2 == 0:
                            pe.wait_ge(p_split, t * 2 + (g // 2 - 1))
                        if has(t, 0):
                            pe.wait_ge(proj_taken, t * 6 + (g + 2))
                        elif g == 0:
                            pe.wait_ge(s_taken, t * 4)
                        weighted_values(pp, g)
                if has(t, -1):
                    if isinstance(t, int) and t == 1:
                        pe.wait_ge(raw_l, len(pieces))
                        pe.wait_ge(gate_split, 1)
                for g in range(NKV):
                    if has(t, 0):
                        turn_qk(t, g)
                    if g == 3 and has(t, 0):
                        turn_qk(t, 4)
                        scores(t, 0)
                    if has(t, -1):
                        output_heads(t - 1, g)
                if has(t, 0):
                    pe.wait_ge(qk_split, t * 5 + 5)
                    scores(t, 1)

            turns(step)(pe)


def ffn_pass(nc, ins, kept, scratch, out):
    T = kept["logits"].shape[1]
    NG = T // GT
    x1_dram, x2h_dram, x2l_dram = scratch["x1"], scratch["x2h"], scratch["x2l"]
    x2_dram, sorted_x, sorted_y, part_dram = scratch["x2"], scratch["sorted_x"], scratch["sorted_y"], scratch["part"]
    out_tok = out.rearrange("b s c -> (b s) c")
    ident, logits, tanh_g = kept["ident"], kept["logits"], kept["tanh_g"]
    NB = sorted_x.shape[0] // P
    FA, FB = P, F_MOE - P
    F2 = 2 * F_MOE
    BEFORE = NG - 3
    UNROLL = 4
    LAG = 3

    with ExitStack() as es:
        def sb(name, shape, dt=F32):
            return es.enter_context(nc.sbuf_tensor(name, shape, dt))

        def sem(name):
            return es.enter_context(nc.semaphore(name))

        w12_h, w12_l = sb("w12_h", [P, SH_CHUNKS, 2 * KC, P], F32R), sb("w12_l", [P, SH_CHUNKS, 2 * KC, P], F32R)
        wp_h, wp_l = sb("wp_h", [P, SH_CHUNKS, C], F32R), sb("wp_l", [P, SH_CHUNKS, C], F32R)
        EX_FC, EX_P = KC * NE * F2, 2 * NE * C
        ex_all = sb("ex_all", [P, 2 * EX_FC + 2 * EX_P], F32R)
        e12_h = ex_all[:, 0:EX_FC].rearrange("p (k n) -> p k n", k=KC)
        e12_l = ex_all[:, EX_FC:2 * EX_FC].rearrange("p (k n) -> p k n", k=KC)
        ep_h = ex_all[:, 2 * EX_FC:2 * EX_FC + EX_P].rearrange("p (s n) -> p s n", s=2)
        ep_l = ex_all[:, 2 * EX_FC + EX_P:].rearrange("p (s n) -> p s n", s=2)
        picked = ex_all[:, 0:T * 2 * C].bitcast(F32).rearrange("p (t s c) -> p t s c", t=T, s=2)
        raw_fc, RAW = kept["raw_fc"], RAW_CHUNKS
        raw_ex = raw_fc[:, :, :, :].rearrange("p (r s) f c -> p r s f c", s=2)
        raw_p = sb("raw_p", [P, KC * (F_SHARED + NE * F_MOE)])
        raw_sp = raw_p[:, 0:KC * F_SHARED].rearrange("p (k f) -> p k f", k=KC)
        raw_ep = raw_p[:, KC * F_SHARED:].rearrange("p (k f) -> p k f", k=KC)
        small = [P, T, NE]
        prob, pick1, pick2, place = (sb(n, small) for n in ("prob", "pick1", "pick2", "place"))
        work2 = sb("work2", [P, 2 * T * NE])
        hit, left = (work2[:, i * T * NE:(i + 1) * T * NE].rearrange("p (t e) -> p t e", e=NE) for i in range(2))
        before = [sb(f"before{i}", [P, T // 2 + T, NE]) for i in range(2)]
        blocks = [sb(f"blocks{i}", [P, NE // 2 + NE]) for i in range(2)]
        block_hit = sb("block_hit", [P, NE, T])
        col = {n: sb(f"col_{n}", [P, T]) for n in ("max", "sum", "inv", "top1", "top2", "place", "sig", "sinv")}
        sgate = sb("sgate", [P, T])
        gain = sb("gain", [P, 2, T])
        slot_f = sb("slot_f", [P, 2, T])
        slot = sb("slot", [P, 2, T], U32)
        n_blocks, start_row = sb("n_blocks", [P, NE]), sb("start_row", [P, NE])
        of_block = work2[:, 0:NB * (NE - 1)].rearrange("p (b e) -> p b e", e=NE - 1)
        expert_f = sb("expert_f", [P, NB])
        expert = sb("expert", [P, LAG + NB + UNROLL], I32)
        below, ones = sb("below", [P, P]), sb("ones", [P, P])
        row_steps, block_no = sb("row_steps", [P, T]), sb("block_no", [P, NB])
        xg_h, xg_l = sb("xg_h", [P, 2, KC, GROUP], F32R), sb("xg_l", [P, 2, KC, GROUP], F32R)
        xy = sb("xy", [P, 2, GT, C])
        act_s = sb("act_s", [P, 2, GROUP])
        hid = sb("hid", [P, 2, GROUP])
        hid_h, hid_l = sb("hid_h", [P, 2, GROUP], F32R), sb("hid_l", [P, 2, GROUP], F32R)
        XR = 4
        xrow = sb("xrow", [P, XR, C])
        xb = raw_p[:, 0:UNROLL * C].rearrange("p (b c) -> p b c", b=UNROLL)
        yb_sb = raw_p[:, UNROLL * C:2 * UNROLL * C].rearrange("p (b c) -> p b c", b=UNROLL)
        silu_b = raw_p[:, 2 * UNROLL * C:2 * UNROLL * C + 2 * F_MOE].rearrange("p (b c) -> p b c", b=2)
        xbt_h, xbt_l = sb("xbt_h", [P, 2, C], F32R), sb("xbt_l", [P, 2, C], F32R)
        hb_tok = sb("hb_tok", [P, 2, 2 * P])
        ht_h, ht_l = sb("ht_h", [P, 2, 2 * P], F32R), sb("ht_l", [P, 2, 2 * P], F32R)

        ps = es.enter_context(nc.psum_tensor("ps", [P, 8, BANK], F32))
        ACC, PREP = 4, 6

        fc_in = [sem(f"fc_in{i}") for i in range(RAW)]
        ex_in = [sem(f"ex_in{i}") for i in range(2)]
        sp_in, ep_in = sem("sp_in"), sem("ep_in")
        zeroed, consts_made = sem("zeroed"), sem("consts_made")
        prep_turned, prep_high, prep_low = sem("prep_turned"), sem("prep_high"), sem("prep_low")
        ex_turned, ex_high, ex_low = sem("ex_turned"), sem("ex_high"), sem("ex_low")
        route = sem("route")
        route_exp, gate_exp = sem("route_exp"), sem("gate_exp")
        hits_ready, counted = sem("hits_ready"), sem("counted")
        slots_ready, experts_ready = sem("slots_ready"), sem("experts_ready")
        xrow_in = [sem(f"xrow_in{i}") for i in range(XR)]
        xrow_out = [sem(f"xrow_out{i}") for i in range(XR)]
        xg_in = [sem(f"xg_in{i}") for i in range(2)]
        xy_in = [sem(f"xy_in{i}") for i in range(2)]
        xy_out = [sem(f"xy_out{i}") for i in range(2)]
        h1_done, h2_done = sem("h1_done"), sem("h2_done")
        silu_done, h_done = sem("silu_done"), sem("h_done")
        hid_high, hid_low = sem("hid_high"), sem("hid_low")
        h_through = sem("h_through")
        sh_taken = sem("sh_taken")
        finished, finish_step = sem("finished"), sem("finish_step")
        xb_in = [sem(f"xb_in{i}") for i in range(2)]
        xb_turned, xb_high, xb_low = sem("xb_turned"), sem("xb_high"), sem("xb_low")
        up_done, b_silu, b_hidden = sem("up_done"), sem("b_silu"), sem("b_hidden")
        b_turned, b_high, b_low = sem("b_turned"), sem("b_high"), sem("b_low")
        b_done, b_taken = sem("b_done"), sem("b_taken")
        b_out = [sem(f"b_out{i}") for i in range(2)]
        y_in = [sem(f"y_in{i}") for i in range(NG)]

        prep = [("fc", c) for c in range(SH_CHUNKS)]
        prep += [("proj", (c, c + 1)) for c in range(0, SH_CHUNKS, 2)]
        ex_prep = [(e, kind) for e in range(NE) for kind in range(KC + 1)]
        beside = {(2 + m // 2 // SH_CHUNKS, m // 2 % SH_CHUNKS): (m, m + 1) for m in range(0, len(ex_prep), 2)}
        join_at = {(NG - 2, 1): NG - 3, (NG - 2, 2): 0, (NG - 2, 4): 1,
                   (NG - 1, 1): NG - 2, (NG - 1, 2): 2, (NG - 1, 4): 3, (NG - 1, 5): 4}
        order = [join_at[at] for at in sorted(join_at)] + [NG - 1]
        jobs = [(n, x1_dram, part_dram) for n in range(BEFORE)]
        jobs += [(n, x1_dram if n >= BEFORE else part_dram, out_tok) for n in order]
        job_of = {n: BEFORE + i for i, n in enumerate(order)}

        def rows_of(c):
            return SH_TAIL if c == SH_CHUNKS - 1 else P

        def prep_views(n, low):
            kind, c = prep[n]
            bank = ps[:, n % 4, :]
            if kind == "fc":
                dst = (w12_h, w12_l)[low]
                r = rows_of(c)
                return [(bank.rearrange("p (m f) -> p m f", m=2 * KC)[:, :, 0:r], dst[:, c, :, 0:r])]
            dst = (wp_h, wp_l)[low]
            return [(bank[0:rows_of(m), i * C:(i + 1) * C], dst[0:rows_of(m), m, :]) for i, m in enumerate(c)]

        def ex_views(m, low):
            e, kind = ex_prep[m]
            bank = ps[:, PREP + m % 2, :]
            if kind < KC:
                return [(bank[:, 0:F2], (e12_h, e12_l)[low][:, kind, e * F2:(e + 1) * F2])]
            dst = (ep_h, ep_l)[low]
            return [(bank[0:r, s * C:(s + 1) * C], dst[0:r, s, e * C:(e + 1) * C]) for s, r in ((0, FA), (1, FB))]

        def block_steps(step):
            def run(eng):
                for s in range(2 * UNROLL):
                    step(s // UNROLL, s % UNROLL, s)
                with eng.Fori(2, NB // UNROLL) as k:
                    for q in range(UNROLL):
                        step(k, q, k * UNROLL + q)
                for s in range(NB, NB + 3):
                    step(s // UNROLL, s % UNROLL, s)
            return run

        def there(s, lag):
            return not isinstance(s, int) or 0 <= s - lag < NB

        def at(k, q, lag):
            return k + (q - lag) // UNROLL, (q - lag) % UNROLL

        def load_tokens(queue, n):
            cols = slice(n * GROUP, (n + 1) * GROUP)
            if n >= 2:
                queue.wait_ge(h2_done, (n - 1) * SH_CHUNKS)
            for dst, src in ((xg_h, x2h_dram), (xg_l, x2l_dram)):
                queue.dma_start(dst[:, n % 2, :, :].bitcast(F32), src[:, :, cols].rearrange("k p n -> p k n")
                                ).then_inc(xg_in[n % 2], 16)

        def load_job(queue, j):
            n, src, _ = jobs[j]
            if j >= 2:
                queue.wait_ge(xy_out[j % 2], j // 2 * 16)
            if src is part_dram:
                queue.wait_ge(xy_out[n % 2], (n // 2 + 1) * 16)
            queue.dma_start(xy[:, j % 2, :, :], src[n * GROUP:(n + 1) * GROUP, :].rearrange(
                "(j p) c -> p j c", p=P)).then_inc(xy_in[j % 2], 16)

        def store_job(queue, j):
            n, _, dst = jobs[j]
            if j < BEFORE:
                queue.wait_ge(sh_taken, (j + 1) * GT)
            else:
                queue.wait_ge(finished, j - BEFORE + 1)
            queue.dma_start(dst[n * GROUP:(n + 1) * GROUP, :].rearrange("(j p) c -> p j c", p=P),
                            xy[:, j % 2, :, :]).then_inc(xy_out[j % 2], 16)

        def load_fc(queue, c):
            if c >= RAW:
                queue.wait_ge(prep_turned, c - RAW + 1)
            for f, w in enumerate((ins["shared_fc1"], ins["shared_fc2"])):
                queue.dma_start(raw_fc[0:rows_of(c), c % RAW, f, :], w[c * P:c * P + rows_of(c), :]
                                ).then_inc(fc_in[c % RAW], 16)

        def fetch_expert(queue, e):
            for f, w in enumerate((ins["expert_fc1"], ins["expert_fc2"])):
                queue.dma_start(raw_ex[:, e % 2, 0, f, :], w[e, 0:FA, :]).then_inc(ex_in[e % 2], 16)
                queue.dma_start(raw_ex[0:FB, e % 2, 1, f, :], w[e, FA:F_MOE, :]).then_inc(ex_in[e % 2], 16)

        block = es.enter_context(nc.Block())

        @block.sync
        def _(sp):
            def load_rows(t):
                if t >= XR:
                    sp.wait_ge(xrow_out[t % XR], t // XR * 32)
                sp.dma_start(xrow[:, t % XR, :], x2_dram[t * P:(t + 1) * P, :]).then_inc(xrow_in[t % XR], 16)

            sp.dma_start(raw_sp, ins["shared_proj"].rearrange("(k p) f -> p k f", p=P)).then_inc(sp_in, 16)
            for c in range(RAW, SH_CHUNKS):
                load_fc(sp, c)
            load_tokens(sp, 0)
            load_job(sp, 0)
            sp.wait_ge(prep_turned, SH_CHUNKS)
            fetch_expert(sp, 0)
            fetch_expert(sp, 1)
            for t in range(XR):
                load_rows(t)
            for kc in range(KC):
                sp.dma_start(raw_ep[:, kc, :].rearrange("p (e f) -> p e f", e=NE),
                             ins["expert_proj"][:, kc * P:(kc + 1) * P, :].rearrange("e p f -> p e f")
                             ).then_inc(ep_in, 16)
            load_tokens(sp, 1)
            load_job(sp, 1)
            for t in range(XR, T):
                load_rows(t)
            for i in range(XR):
                sp.wait_ge(xrow_out[i], len(range(i, T, XR)) * 32)

            def load_pair(row, half):
                sp.dma_start(xb[:, 2 * half:2 * half + 2, :], sorted_x[bass.ds(row, 2 * P), :].rearrange(
                    "(b p) c -> p b c", p=P)).then_inc(xb_in[half], 16)

            sp.wait_ge(ex_turned, len(ex_prep))
            for half in range(2):
                load_pair(half * 2 * P, half)
            store_job(sp, BEFORE - 1)
            load_tokens(sp, BEFORE + 1)

            def step(k, q, s):
                if s % 2 == 1 if isinstance(s, int) else q % 2 == 1:
                    more = s + UNROLL < NB if isinstance(s, int) else True
                    if more:
                        wait_for(sp, xb_turned, s + 1)
                        load_pair(s * P + (UNROLL - 1) * P, q // 2)
                elif there(s, 3) and there(s, 4):
                    _, qy = at(k, q, 4)
                    sp.wait_ge(b_taken, s - 2)
                    sp.dma_start(sorted_y[bass.ds(s * P - 4 * P, 2 * P), :].rearrange("(b p) c -> p b c", p=P),
                                 yb_sb[:, qy:qy + 2, :]).then_inc(b_out[qy // 2], 16)

            def block_loop(eng):
                for s in range(2 * UNROLL):
                    step(s // UNROLL, s % UNROLL, s)
                with eng.Fori(2, NB // UNROLL - 1) as k:
                    for q in range(UNROLL):
                        step(k, q, k * UNROLL + q)
                for s in range(NB - UNROLL, NB + 4):
                    step(s // UNROLL, s % UNROLL, s)

            block_loop(sp)
            load_job(sp, BEFORE + 1)
            for j in range(BEFORE, len(jobs)):
                store_job(sp, j)
                if j + 2 < len(jobs):
                    load_job(sp, j + 2)
                if j == BEFORE:
                    load_tokens(sp, NG - 1)
            for i in range(2):
                sp.wait_ge(xy_out[i], len(range(i, len(jobs), 2)) * 16)

        @block.gpsimd
        def _(pool):
            pool.iota(row_steps[:, :], pattern=[[P, T]], base=0, channel_multiplier=0,
                      allow_small_or_imprecise_dtypes=True).then_inc(consts_made, 1)
            pool.wait_ge(consts_made, 1)
            pool.iota(block_no[:, :], pattern=[[1, NB]], base=0, channel_multiplier=0,
                      allow_small_or_imprecise_dtypes=True).then_inc(consts_made, 1)
            pool.wait_ge(consts_made, 2)
            pool.memset(ones[:, :], 1.0).then_inc(consts_made, 1)
            pool.wait_ge(consts_made, 3)
            pool.affine_select(out=below[:, :], in_=ones[:, :], compare_op=ALU.is_gt, fill=0.0,
                               base=0, pattern=[[1, P]], channel_multiplier=-1).then_inc(consts_made, 1)
            made = 4
            for part in (ep_h, ep_l):
                for r0, r1 in ((32, 64), (64, P)):
                    pool.wait_ge(consts_made, made)
                    pool.memset(part[r0:r1, 1, :].bitcast(F32), 0.0).then_inc(consts_made, 1)
                    made += 1
            pool.wait_ge(slots_ready, 1)
            for t in range(T):
                pool.wait_ge(xrow_in[t % XR], (t // XR + 1) * 16)
                for s in range(2):
                    pool.indirect_dma_start(sorted_x, bass.IndirectOffsetOnAxis(ap=slot[:, s, t:t + 1], axis=0),
                                            xrow[:, t % XR, :], None).then_inc(xrow_out[t % XR], 16)
            for i in range(2):
                pool.wait_ge(b_out[i], NB // UNROLL * 16)
            pool.wait_ge(b_done, NB)
            for n in order:
                for t in range(n * GT, (n + 1) * GT):
                    for s in range(2):
                        pool.indirect_dma_start(picked[:, t, s, :], None, sorted_y,
                                                bass.IndirectOffsetOnAxis(ap=slot[:, s, t:t + 1], axis=0)
                                                ).then_inc(y_in[n], 16)

        @block.scalar
        def _(act):
            act.activation(col["sig"][:, :].unsqueeze(2), logits[:, :, NE:NE + 1], ACT.Exp, scale=-1.0
                           ).then_inc(gate_exp, 1)
            act.wait_ge(route, 2)
            act.activation(prob[:, :, :], prob[:, :, :], ACT.Exp).then_inc(route_exp, 1)
            for n in range(len(prep)):
                act.wait_ge(prep_turned, n + 1)
                for src, dst in prep_views(n, 0):
                    ins_ = act.activation(dst, src, ACT.Copy)
                ins_.then_inc(prep_high, 1)

            def high(n, c):
                act.wait_ge(h_done, n * SH_CHUNKS + c + 1)
                wait_for(act, h_through, n * SH_CHUNKS + c - 1)
                act.activation(hid_h[:, c % 2, :], hid[:, c % 2, :], ACT.Copy).then_inc(hid_high, 1)

            def group(n):
                for c in range(SH_CHUNKS):
                    m = n * SH_CHUNKS + c
                    act.wait_ge(h1_done, m + 1)
                    wait_for(act, h_done, m - 1)
                    act.activation(act_s[:, c % 2, :], ps[:, 2 * (c % 2), :], ACT.Silu).then_inc(silu_done, 1)
                    if c > 0:
                        high(n, c - 1)
                    if 0 < n < BEFORE and c == 1:
                        store_job(act, n - 1)
                        load_tokens(act, n + 1)
                    if 0 < n < BEFORE and c == 3:
                        load_job(act, n + 1)
                    for m in beside.get((n, c), ()):
                        act.wait_ge(ex_turned, m + 1)
                        if m == 0:
                            act.wait_ge(consts_made, 8)
                        for src, dst in ex_views(m, 0):
                            ins_ = act.activation(dst, src, ACT.Copy)
                        ins_.then_inc(ex_high, 1)
                        e, kind = ex_prep[m]
                        if kind == KC - 1 and e + 2 < NE:
                            fetch_expert(act, e + 2)
                high(n, SH_CHUNKS - 1)

            for n in range(BEFORE):
                group(n)

            def step(k, q, s):
                if there(s, 0):
                    act.wait_ge(xb_turned, s + 1)
                    wait_for(act, up_done, s - 1)
                    act.activation(xbt_h[:, q % 2, :], ps[:, q % 2, 0:C], ACT.Copy).then_inc(xb_high, 1)
                if there(s, 1):
                    r = (q + 1) % 2
                    act.wait_ge(up_done, s)
                    wait_for(act, b_hidden, s - 2)
                    act.activation(silu_b[:, r, :], ps[:, 2 + r, 0:F_MOE], ACT.Silu).then_inc(b_silu, 1)
                if there(s, 2):
                    act.wait_ge(b_turned, s - 1)
                    wait_for(act, b_done, s - 3)
                    act.activation(ht_h[:, q % 2, :], ps[:, 4 + q % 2, 0:2 * P], ACT.Copy).then_inc(b_high, 1)
                if there(s, 3):
                    ky, qy = at(k, q, 3)
                    act.wait_ge(b_done, s - 2)
                    wait_for(act, b_out[qy // 2], ky * 16)
                    act.activation(yb_sb[:, qy, :], ps[:, 6 + qy % 2, 0:C], ACT.Copy).then_inc(b_taken, 1)

            block_steps(step)(act)
            for n in range(BEFORE, NG):
                group(n)

        @block.vector
        def _(dve):
            chain = 0

            def link(ins_):
                nonlocal chain
                chain += 1
                ins_.then_inc(route, 1)
                dve.wait_ge(route, chain)

            c = SH_CHUNKS - 1
            zeros = [w[:, c, :, SH_TAIL:P].bitcast(F32) for w in (w12_h, w12_l)]
            zeros += [w[SH_TAIL:P, c, :].bitcast(F32) for w in (wp_h, wp_l)]
            zeros += [hb_tok[:, :, F_MOE:2 * P]]
            zeros += [b[:, 0:T // 2, :] for b in before] + [b[:, 0:NE // 2] for b in blocks]
            zeros += [expert[:, 0:LAG].bitcast(F32), expert[:, LAG + NB:].bitcast(F32)]
            for z in zeros:
                dve.memset(z, 0.0).then_inc(zeroed, 1)
            for e in range(NE):
                dve.memset(kept["rank"][:, e:e + 1], float(NE - e)).then_inc(zeroed, 1)
            n_zeroed = len(zeros) + NE

            wide = lambda t: t.unsqueeze(2).broadcast_to([P, T, NE])
            rank = kept["rank"][:, :].unsqueeze(1).broadcast_to([P, T, NE])
            expert_logits = logits[:, :, 0:NE]
            link(dve.tensor_reduce(col["max"][:, :], expert_logits, AX.X, ALU.max))
            link(dve.tensor_tensor(prob[:, :, :], expert_logits, wide(col["max"][:, :]), ALU.subtract))

            for n in range(len(prep)):
                dve.wait_ge(prep_high, n + 1)
                for (src, low), (_, high) in zip(prep_views(n, 1), prep_views(n, 0)):
                    ins_ = dve.tensor_tensor(low, src, high, ALU.subtract)
                ins_.then_inc(prep_low, 1)

            def shared_gates():
                dve.wait_ge(gate_exp, 1)
                link(dve.tensor_scalar(col["sinv"][:, :], col["sig"][:, :], 1.0, None, ALU.add))
                link(dve.reciprocal(col["sig"][:, :], col["sinv"][:, :]))
                link(dve.tensor_scalar(sgate[:, :], col["sig"][:, :], tanh_g[:, 1:2], None, ALU.mult))
                dve.wait_ge(route_exp, 1)
                link(dve.tensor_reduce(col["sum"][:, :], prob[:, :, :], AX.X, ALU.add))

            def probabilities():
                link(dve.reciprocal(col["inv"][:, :], col["sum"][:, :]))
                link(dve.tensor_tensor(prob[:, :, :], prob[:, :, :], wide(col["inv"][:, :]), ALU.mult))
                dve.wait_ge(zeroed, n_zeroed)

            def find(values, top):
                link(dve.tensor_reduce(top[:, :], values[:, :, :], AX.X, ALU.max))
                link(dve.tensor_tensor(hit[:, :, :], values[:, :, :], wide(top[:, :]), ALU.is_equal))
                link(dve.tensor_tensor(hit[:, :, :], hit[:, :, :], rank, ALU.mult))

            def choose(pick):
                link(dve.tensor_reduce(col["place"][:, :], hit[:, :, :], AX.X, ALU.max))
                link(dve.tensor_tensor(pick[:, :, :], hit[:, :, :], wide(col["place"][:, :]), ALU.is_equal))

            def without_first():
                link(dve.scalar_tensor_tensor(left[:, :, :], pick1[:, :, :], -2.0, prob[:, :, :],
                                              ALU.mult, ALU.add))

            def both_hits():
                dve.tensor_tensor(hit[:, :, :], pick1[:, :, :], pick2[:, :, :], ALU.add).then_inc(hits_ready, 1)

            def gains():
                for s, top in enumerate((col["top1"], col["top2"])):
                    link(dve.tensor_scalar(gain[:, s, :], top[:, :], tanh_g[:, 1:2], None, ALU.mult))

            own = ps[:, PREP, 0:T * NE].rearrange("p (t e) -> p t e", e=NE)
            under = ps[:, PREP + 1, 0:T * NE].rearrange("p (t e) -> p t e", e=NE)

            def take_counts():
                dve.wait_ge(counted, 1)
                link(dve.tensor_copy(before[0][:, T // 2:, :], own))

            def add_tiles(reach, i):
                a = before[i]
                link(dve.tensor_tensor(before[1 - i][:, T // 2:, :], a[:, T // 2:, :],
                                       a[:, T // 2 - reach:T // 2 - reach + T, :], ALU.add))

            assert T == 32 and NE == 8
            upto = before[1]

            def count_blocks():
                total = upto[:, T // 2 + T - 1, :]
                link(dve.tensor_tensor(block_hit[:, :, :], total.unsqueeze(2).broadcast_to([P, NE, T]),
                                       row_steps[:, :].unsqueeze(1).broadcast_to([P, NE, T]), ALU.is_gt))
                link(dve.tensor_reduce(n_blocks[:, :], block_hit[:, :, :], AX.X, ALU.add))

            ends = blocks[1][:, NE // 2:]

            def start_rows():
                link(dve.tensor_copy(blocks[0][:, NE // 2:], n_blocks[:, :]))
                reach, i = 1, 0
                while reach < NE:
                    a = blocks[i]
                    link(dve.tensor_tensor(blocks[1 - i][:, NE // 2:], a[:, NE // 2:],
                                           a[:, NE // 2 - reach:NE // 2 - reach + NE], ALU.add))
                    reach, i = reach * 2, 1 - i
                link(dve.tensor_tensor(start_row[:, :], ends, n_blocks[:, :], ALU.subtract))
                link(dve.tensor_scalar(start_row[:, :], start_row[:, :], float(P), None, ALU.mult))

            def places():
                link(dve.tensor_tensor(place[:, :, :], upto[:, T // 2:, :], own, ALU.subtract))
                link(dve.tensor_tensor(place[:, :, :], place[:, :, :], under, ALU.add))
                link(dve.tensor_tensor(place[:, :, :], place[:, :, :],
                                       start_row[:, :].unsqueeze(1).broadcast_to([P, T, NE]), ALU.add))

            def place_of(s, pick):
                link(dve.tensor_tensor(hit[:, :, :], pick[:, :, :], place[:, :, :], ALU.mult))
                link(dve.tensor_reduce(slot_f[:, s, :], hit[:, :, :], AX.X, ALU.add))

            def slots():
                place_of(1, pick2)
                dve.tensor_copy(slot[:, :, :], slot_f[:, :, :]).then_inc(slots_ready, 1)

            def experts_of_blocks():
                link(dve.tensor_tensor(of_block[:, :, :], block_no[:, :].unsqueeze(2).broadcast_to([P, NB, NE - 1]),
                                       ends[:, 0:NE - 1].unsqueeze(1).broadcast_to([P, NB, NE - 1]), ALU.is_ge))
                link(dve.tensor_reduce(expert_f[:, :], of_block[:, :, :], AX.X, ALU.add))
                dve.tensor_copy(expert[:, LAG:LAG + NB], expert_f[:, :]).then_inc(experts_ready, 1)

            def routing(n, c):
                if (n, c) == (0, 0):
                    shared_gates()
                elif (n, c) == (0, 1):
                    probabilities()
                    find(prob, col["top1"])
                elif (n, c) == (0, 2):
                    choose(pick1)
                    without_first()
                elif (n, c) == (0, 3):
                    find(left, col["top2"])
                elif (n, c) == (0, 4):
                    choose(pick2)
                    both_hits()
                elif (n, c) == (0, 5):
                    gains()
                elif (n, c) == (1, 0):
                    take_counts()
                    add_tiles(1, 0)
                    add_tiles(2, 1)
                elif (n, c) == (1, 1):
                    add_tiles(4, 0)
                    add_tiles(8, 1)
                    add_tiles(16, 0)
                    count_blocks()
                elif (n, c) == (1, 2):
                    start_rows()
                    places()
                elif (n, c) == (1, 3):
                    place_of(0, pick1)
                    slots()
                elif (n, c) == (1, 4):
                    experts_of_blocks()

            def low(n, c):
                dve.wait_ge(hid_high, n * SH_CHUNKS + c + 1)
                dve.tensor_tensor(hid_l[:, c % 2, :], hid[:, c % 2, :], hid_h[:, c % 2, :],
                                  ALU.subtract).then_inc(hid_low, 1)

            def add_picked(n):
                j = job_of[n]
                dve.wait_ge(xy_in[j % 2], (j // 2 + 1) * 16)
                if n >= BEFORE:
                    dve.wait_ge(sh_taken, (n + 1) * GT)
                dve.wait_ge(y_in[n], GT * 2 * 16)
                for s in range(2):
                    for i in range(GT):
                        t = n * GT + i
                        if s == 1:
                            dve.wait_ge(finish_step, steps_done[0] + i + 1)
                        ins_ = dve.scalar_tensor_tensor(xy[:, j % 2, i, :], picked[:, t, s, :], gain[:, s, t:t + 1],
                                                        xy[:, j % 2, i, :], ALU.mult, ALU.add)
                        if s == 0:
                            ins_.then_inc(finish_step, 1)
                ins_.then_inc(finished, 1)
                steps_done[0] += GT

            steps_done = [0]

            def group(n, j):
                for c in range(SH_CHUNKS):
                    m = n * SH_CHUNKS + c
                    dve.wait_ge(h2_done, m + 1)
                    dve.wait_ge(silu_done, m + 1)
                    wait_for(dve, hid_low, m - 1)
                    dve.tensor_tensor(hid[:, c % 2, :], ps[:, 2 * (c % 2) + 1, :], act_s[:, c % 2, :], ALU.mult
                                      ).then_inc(h_done, 1)
                    if c > 0:
                        low(n, c - 1)
                    routing(n, c)
                    for m in beside.get((n, c), ()):
                        dve.wait_ge(ex_high, m + 1)
                        for (src, lo), (_, hi) in zip(ex_views(m, 1), ex_views(m, 0)):
                            ins_ = dve.tensor_tensor(lo, src, hi, ALU.subtract)
                        ins_.then_inc(ex_low, 1)
                    if (n, c) in join_at:
                        add_picked(join_at[n, c])
                low(n, SH_CHUNKS - 1)
                dve.wait_ge(xy_in[j % 2], (j // 2 + 1) * 16)
                dve.wait_ge(h_through, (n + 1) * SH_CHUNKS)
                for i in range(GT):
                    ins_ = dve.scalar_tensor_tensor(
                        xy[:, j % 2, i, :], ps[:, ACC + i // 2, (i % 2) * C:(i % 2 + 1) * C],
                        sgate[:, n * GT + i:n * GT + i + 1], xy[:, j % 2, i, :], ALU.mult, ALU.add)
                    ins_.then_inc(sh_taken, 1)

            for n in range(BEFORE):
                group(n, n)

            def step(k, q, s):
                if there(s, 0):
                    dve.wait_ge(xb_high, s + 1)
                    dve.tensor_tensor(xbt_l[:, q % 2, :], ps[:, q % 2, 0:C], xbt_h[:, q % 2, :],
                                      ALU.subtract).then_inc(xb_low, 1)
                if there(s, 1):
                    r = (q + 1) % 2
                    dve.wait_ge(b_silu, s)
                    wait_for(dve, b_turned, s - 2)
                    dve.tensor_tensor(hb_tok[:, r, 0:F_MOE], ps[:, 2 + r, F_MOE:F2], silu_b[:, r, :], ALU.mult
                                      ).then_inc(b_hidden, 1)
                if there(s, 2):
                    dve.wait_ge(b_high, s - 1)
                    dve.tensor_tensor(ht_l[:, q % 2, :], ps[:, 4 + q % 2, 0:2 * P], ht_h[:, q % 2, :],
                                      ALU.subtract).then_inc(b_low, 1)

            block_steps(step)(dve)
            for n in range(BEFORE, NG):
                group(n, job_of[n])
            add_picked(NG - 1)

        @block.tensor
        def _(pe):
            for n, (kind, c) in enumerate(prep):
                if n >= 4:
                    pe.wait_ge(prep_low, n - 3)
                if kind == "fc":
                    if c >= RAW:
                        pe.wait_ge(fc_in[c % RAW], c // RAW * 32)
                    r = rows_of(c)
                    for m in range(2 * KC):
                        ins_ = pe.transpose(ps[:, n % 4, m * P:m * P + r],
                                            raw_fc[0:r, c % RAW, m // KC, (m % KC) * P:(m % KC + 1) * P],
                                            ident[0:r, 0:r])
                else:
                    pe.wait_ge(sp_in, 16)
                    for i, m in enumerate(c):
                        r = rows_of(m)
                        for kc in range(KC):
                            at_ = i * C + kc * P
                            ins_ = pe.transpose(ps[0:r, n % 4, at_:at_ + P], raw_sp[:, kc, m * P:m * P + r], ident[:, :])
                ins_.then_inc(prep_turned, 1)
            pe.wait_ge(prep_low, len(prep))
            pe.wait_ge(zeroed, 4)

            def count_hits():
                pe.wait_ge(hits_ready, 1)
                pe.wait_ge(consts_made, 4)
                hits = hit[:, :, :].rearrange("p t e -> p (t e)")
                pe.matmul(ps[:, PREP, 0:T * NE], ones[:, :], hits, start=True, stop=True)
                pe.matmul(ps[:, PREP + 1, 0:T * NE], below[:, :], hits, start=True, stop=True).then_inc(counted, 1)

            def up(n, c):
                m = n * SH_CHUNKS + c
                if c == 0:
                    pe.wait_ge(xg_in[n % 2], (n // 2 + 1) * 32)
                wait_for(pe, h_done, m - 1)
                for f, done in enumerate((h1_done, h2_done)):
                    for kc in range(KC):
                        ins_ = three_products(pe, ps[:, 2 * (c % 2) + f, :], w12_h[:, c, f * KC + kc, :],
                                              w12_l[:, c, f * KC + kc, :], xg_h[:, n % 2, kc, :], xg_l[:, n % 2, kc, :],
                                              kc == 0, kc == KC - 1)
                    ins_.then_inc(done, 1)

            def down(n, c):
                pe.wait_ge(hid_low, n * SH_CHUNKS + (c + 1))
                if c == 0:
                    wait_for(pe, sh_taken, n * GT)
                for j in range(GT):
                    dst = ps[:, ACC + j // 2, (j % 2) * C:(j % 2 + 1) * C]
                    cols = slice(j * P, (j + 1) * P)
                    pe.matmul(dst, hid_h[:, c % 2, cols], wp_h[:, c, :], start=c == 0 and j % 2 == 0, stop=False,
                              skip_group_check=True)
                    pe.matmul(dst, hid_h[:, c % 2, cols], wp_l[:, c, :], start=False, stop=False,
                              skip_group_check=True)
                    ins_ = pe.matmul(dst, hid_l[:, c % 2, cols], wp_h[:, c, :], start=False, stop=c == SH_CHUNKS - 1,
                                     skip_group_check=True)
                ins_.then_inc(h_through, 1)

            def turn_expert(m):
                e, kind = ex_prep[m]
                if m == 0:
                    pe.wait_ge(slots_ready, 1)
                if m >= 2:
                    pe.wait_ge(ex_low, m - 1)
                bank = ps[:, PREP + m % 2, :]
                if kind < KC:
                    pe.wait_ge(ex_in[e % 2], (e // 2 + 1) * 64)
                    for f in range(2):
                        for s, r in ((0, FA), (1, FB)):
                            ins_ = pe.transpose(bank[:, f * F_MOE + s * FA:f * F_MOE + s * FA + r],
                                                raw_ex[0:r, e % 2, s, f, kind * P:(kind + 1) * P], ident[0:r, 0:r])
                else:
                    pe.wait_ge(ep_in, 32)
                    for s, r in ((0, FA), (1, FB)):
                        for kc in range(KC):
                            f0 = e * F_MOE + s * FA
                            ins_ = pe.transpose(bank[0:r, s * C + kc * P:s * C + (kc + 1) * P],
                                                raw_ep[:, kc, f0:f0 + r], ident[:, :])
                ins_.then_inc(ex_turned, 1)

            def group(n):
                for c in range(SH_CHUNKS):
                    up(n, c)
                    for m in beside.get((n, c), ()):
                        turn_expert(m)
                    if c >= 2:
                        down(n, c - 2)
                down(n, SH_CHUNKS - 2)
                down(n, SH_CHUNKS - 1)
                if n == 0:
                    count_hits()

            for n in range(BEFORE):
                group(n)

            pe.wait_ge(experts_ready, 1)

            turn_experts = [None]

            def step(k, q, s):
                if q == 0:
                    turn_experts[0] = nc.values_load_multi_w_load_instructions(
                        expert[0:1, bass.ds(k * UNROLL, UNROLL + 2)], engines=[mybir.EngineType.PE],
                        min_val=0, max_val=NE - 1,
                        skip_runtime_bounds_check_because="a count of NE - 1 comparisons")[1]
                e_down, e_up = turn_experts[0][q], turn_experts[0][q + 2]
                if there(s, 0):
                    kb, qb = at(k, q, 0)
                    pe.wait_ge(xb_in[qb // 2], kb * 16 + 16)
                    wait_for(pe, xb_low, s - 1)
                    for kc in range(KC):
                        ins_ = pe.transpose(ps[:, q % 2, kc * P:(kc + 1) * P], xb[:, qb, kc * P:(kc + 1) * P], ident[:, :])
                    ins_.then_inc(xb_turned, 1)
                if there(s, 1):
                    r = (q + 1) % 2
                    pe.wait_ge(xb_low, s)
                    wait_for(pe, b_hidden, s - 2)
                    cols = bass.ds(e_up * F2, F2)
                    for kc in range(KC):
                        ins_ = three_products(pe, ps[:, 2 + r, 0:F2], xbt_h[:, r, kc * P:(kc + 1) * P],
                                              xbt_l[:, r, kc * P:(kc + 1) * P], e12_h[:, kc, cols], e12_l[:, kc, cols],
                                              kc == 0, kc == KC - 1)
                    ins_.then_inc(up_done, 1)
                if there(s, 2):
                    if isinstance(s, int) and s == 2:
                        pe.wait_ge(sh_taken, BEFORE * GT)
                    pe.wait_ge(b_hidden, s - 1)
                    wait_for(pe, b_low, s - 3)
                    for i in range(2):
                        ins_ = pe.transpose(ps[:, 4 + q % 2, i * P:(i + 1) * P], hb_tok[:, q % 2, i * P:(i + 1) * P],
                                            ident[:, :])
                    ins_.then_inc(b_turned, 1)
                if there(s, 3):
                    r = (q + 1) % 2
                    pe.wait_ge(b_low, s - 2)
                    wait_for(pe, b_taken, s - 4)
                    cols = bass.ds(e_down * C, C)
                    for i in range(2):
                        ins_ = three_products(pe, ps[:, 6 + r, 0:C], ht_h[:, r, i * P:(i + 1) * P],
                                              ht_l[:, r, i * P:(i + 1) * P], ep_h[:, i, cols], ep_l[:, i, cols],
                                              i == 0, i == 1)
                    ins_.then_inc(b_done, 1)

            block_steps(step)(pe)
            pe.wait_ge(b_low, NB)
            pe.wait_ge(b_taken, NB)
            for n in range(BEFORE, NG):
                group(n)


def flamingo_block(nc, x, ctx_2048, mask, g_xattn, g_ffn, Wq, bq, Wk, bk, Wv, bv, Wo, qn_w, kn_w, gate_w,
                   expert_fc1, expert_fc2, expert_proj, shared_fc1, shared_fc2, shared_proj, shared_gate_w, out):
    B, S, _ = x.shape
    N = B * S
    ins = dict(x=x, ctx=ctx_2048, mask=mask, g_xattn=g_xattn, g_ffn=g_ffn, Wq=Wq, bq=bq, Wk=Wk, bk=bk, Wv=Wv,
               bv=bv, Wo=Wo, qn=qn_w, kn=kn_w, gate_w=gate_w, expert_fc1=expert_fc1, expert_fc2=expert_fc2,
               expert_proj=expert_proj, shared_fc1=shared_fc1, shared_fc2=shared_fc2, shared_proj=shared_proj,
               shared_gate_w=shared_gate_w)
    scratch = dict(
        x1=nc.dram_tensor("x1_scratch", [N, C], F32, kind="Internal").ap(),
        x2h=nc.dram_tensor("x2h_scratch", [KC, P, N], F32, kind="Internal").ap(),
        x2l=nc.dram_tensor("x2l_scratch", [KC, P, N], F32, kind="Internal").ap(),
        x2=nc.dram_tensor("x2_scratch", [N, C], F32, kind="Internal").ap(),
        sorted_x=nc.dram_tensor("sorted_x", [2 * N + NE * P, C], F32, kind="Internal").ap(),
        sorted_y=nc.dram_tensor("sorted_y", [2 * N + NE * P, C], F32, kind="Internal").ap(),
        part=nc.dram_tensor("part_scratch", [N, C], F32, kind="Internal").ap(),
    )
    with ExitStack() as es:
        kept = {name: es.enter_context(nc.sbuf_tensor(name, shape, F32)) for name, shape in (
            ("ident", [P, P]), ("logits", [P, N // P, NE + 1]), ("gates", [P, 2]), ("tanh_g", [P, 2]),
            ("rank", [P, NE]), ("raw_fc", [P, RAW_CHUNKS, 2, C]))}
        attention_pass(nc, ins, kept, scratch)
        ffn_pass(nc, ins, kept, scratch, out)


_INS = ['x', 'ctx_2048', 'mask_1xSxS2_ff0', 'g_xattn', 'g_ffn', 'L0_xattn_Wq', 'L0_xattn_bq', 'L0_xattn_Wk',
        'L0_xattn_bk', 'L0_xattn_Wv', 'L0_xattn_bv', 'L0_xattn_Wo', 'L0_xattn_qn_w', 'L0_xattn_kn_w',
        'L0_ffn_gate_w', 'L0_ffn_expert_fc1', 'L0_ffn_expert_fc2', 'L0_ffn_expert_proj', 'L0_ffn_shared_fc1',
        'L0_ffn_shared_fc2', 'L0_ffn_shared_proj', 'L0_ffn_shared_gate_w']
_OUTS = [((64, 64, 256), 'float32')]


def kernel(**inputs):
    import numpy as _np
    import concourse.bacc as _bacc
    from concourse import mybir as _mybir
    from concourse.bass_utils import run_bass_kernel_spmd as _run

    nc = _bacc.Bacc("TRN2", target_bir_lowering=False, num_devices=1)
    arrays, args = {}, []
    for name in _INS:
        a = _np.ascontiguousarray(inputs[name])
        arrays[f"in_{name}_dram"] = a
        args.append(nc.dram_tensor(f"in_{name}_dram", a.shape, _mybir.dt.from_np(a.dtype), kind="ExternalInput").ap())
    for i, (shape, dtype) in enumerate(_OUTS):
        dt = _mybir.dt.from_np(_np.dtype(dtype))
        args.append(nc.dram_tensor(f"out_{i}_dram", shape, dt, kind="ExternalOutput").ap())
    flamingo_block(nc, *args)
    r = _run(nc, [arrays], core_ids=[0])
    return r.results[0]["out_0_dram"]
```
